# Optimizing a Trainium2 kernel written in Bass

```python
import numpy as np
import jax
import jax.numpy as jnp

def _softmax(x, axis=-1):
    return jax.nn.softmax(x, axis=axis)
def _gelu(x):
    return jax.nn.gelu(x, approximate=True)
def _silu(x):
    return jax.nn.silu(x)
def _sigmoid(x):
    return jax.nn.sigmoid(x)
def _layernorm(x, axis=-1, eps=1e-5):
    m = jnp.mean(x, axis=axis, keepdims=True)
    v = jnp.var(x, axis=axis, keepdims=True)
    return (x - m) / jnp.sqrt(v + eps)
def _scatter_add(tgt, idx, src, axis=0):
    return tgt.at[idx].add(src)
def _segment_sum(src, seg, n):
    return jax.ops.segment_sum(src, seg, n)

kernel_name = 'mk_dlrm_tower_d1_rec_3be06f'

def setup_inputs(seed: int = 0):
    np.random.seed(seed)
    _w = jnp.asarray
    def _rec_inputs():
        import jax
        import jax.numpy as jnp
        _tk = jax.random.key(seed)
        ids = jnp.stack([jax.random.randint(jax.random.fold_in(_tk, 200 + f), (1024,), 0, v, jnp.int32) for f, v in enumerate([100000, 10000, 10000, 1000])], axis=1)
        tbl_0 = 0.05 * jax.random.normal(jax.random.fold_in(_tk, 500 + 0), (100000, 4), jnp.float32)
        tbl_1 = 0.05 * jax.random.normal(jax.random.fold_in(_tk, 500 + 1), (10000, 4), jnp.float32)
        tbl_2 = 0.05 * jax.random.normal(jax.random.fold_in(_tk, 500 + 2), (10000, 4), jnp.float32)
        tbl_3 = 0.05 * jax.random.normal(jax.random.fold_in(_tk, 500 + 3), (1000, 4), jnp.float32)
        _rk = jax.random.fold_in(_tk, 7)
        r_x = 7.22013e-05 + 1.00017 * jax.random.normal(jax.random.fold_in(_rk, 101), (1024, 2048), jnp.float32)
        W_top1 = 0.0197642 * jax.random.normal(jax.random.fold_in(_tk, 801), (2560, 512), jnp.float32)
        W_top2 = 0.0441942 * jax.random.normal(jax.random.fold_in(_tk, 802), (512, 256), jnp.float32)
        W_top3 = 0.0625 * jax.random.normal(jax.random.fold_in(_tk, 803), (256, 1), jnp.float32)
        b_top1 = jnp.zeros((512,), jnp.float32)
        b_top2 = jnp.zeros((256,), jnp.float32)
        return r_x, ids, tbl_0, tbl_1, tbl_2, tbl_3, W_top1, b_top1, W_top2, b_top2, W_top3
    r_x, ids, tbl_0, tbl_1, tbl_2, tbl_3, W_top1, b_top1, W_top2, b_top2, W_top3 = _rec_inputs()
    def _L0_rec_setup():
        import jax, jax.numpy as jnp
        import numpy as np
        B, IN, HID, D, N, OUT = (4096, 2048, 2048, 512, 4, 512)
        H = 8
        HD = D // H

        def _ln(x, g, b):
            m = x.mean(-1, keepdims=True)
            v = ((x - m) ** 2).mean(-1, keepdims=True)
            return (x - m) / jnp.sqrt(v + 1e-05) * g + b
        key = jax.random.key(seed)
        ks = jax.random.split(key, 32)

        def nrm(k, shape, scale=0.02):
            return jax.random.normal(k, shape, jnp.float32) * scale
        inp = {}
        inp['x'] = jax.random.normal(ks[0], (B, IN), jnp.float32)
        inp['strength'] = jax.random.uniform(ks[1], (B, N, N), jnp.float32)
        for t, i in (('er', 2), ('ei', 4)):
            inp[t + '_W1'] = nrm(ks[i], (HID, IN))
            inp[t + '_b1'] = jnp.zeros((HID,), jnp.float32)
            inp[t + '_g1'] = jnp.ones((HID,), jnp.float32)
            inp[t + '_be1'] = jnp.zeros((HID,), jnp.float32)
            inp[t + '_W2'] = nrm(ks[i + 1], (N * D, HID))
            inp[t + '_b2'] = jnp.zeros((N * D,), jnp.float32)
        names = ['Wq_r', 'Wq_i', 'Wk_r', 'Wk_i', 'Wv_r', 'Wv_i', 'Wo_r', 'Wo_i']
        for j, nm in enumerate(names):
            inp[nm] = nrm(ks[6 + j], (D, D))
            inp['b' + nm[1:]] = jnp.zeros((D,), jnp.float32)
        inp['int_Wr'] = jnp.tile(jnp.eye(D, dtype=jnp.float32)[None], (N, 1, 1))
        inp['int_Wi'] = jnp.zeros((N, D, D), jnp.float32)
        inp['meas_Mr'] = nrm(ks[20], (OUT, D), 1.0 / np.sqrt(D))
        inp['meas_Mi'] = nrm(ks[21], (OUT, D), 1.0 / np.sqrt(D))
        inp['post_W'] = nrm(ks[22], (OUT, OUT))
        inp['post_b'] = jnp.zeros((OUT,), jnp.float32)
        inp['post_g'] = jnp.ones((OUT,), jnp.float32)
        inp['post_be'] = jnp.zeros((OUT,), jnp.float32)
        return inp
    _L0_rec_all = _L0_rec_setup()
    _L0_rec_in = {k: v for k, v in _L0_rec_all.items() if k in ('er_W1', 'er_b1', 'er_g1', 'er_be1', 'er_W2', 'er_b2', 'ei_W1', 'ei_b1', 'ei_g1', 'ei_be1', 'ei_W2', 'ei_b2', 'Wq_r', 'bq_r', 'Wq_i', 'bq_i', 'Wk_r', 'bk_r', 'Wk_i', 'bk_i', 'Wv_r', 'bv_r', 'Wv_i', 'bv_i', 'Wo_r', 'bo_r', 'Wo_i', 'bo_i', 'int_Wr', 'int_Wi', 'meas_Mr', 'meas_Mi', 'post_W', 'post_b', 'post_g', 'post_be', )}
    del _L0_rec_all

    return {
        "r_x": r_x,
        "ids": ids,
        "tbl_0": tbl_0,
        "tbl_1": tbl_1,
        "tbl_2": tbl_2,
        "tbl_3": tbl_3,
        "W_top1": W_top1,
        "b_top1": b_top1,
        "W_top2": W_top2,
        "b_top2": b_top2,
        "W_top3": W_top3,
        "L0_rec_er_W1": _L0_rec_in["er_W1"],
        "L0_rec_er_b1": _L0_rec_in["er_b1"],
        "L0_rec_er_g1": _L0_rec_in["er_g1"],
        "L0_rec_er_be1": _L0_rec_in["er_be1"],
        "L0_rec_er_W2": _L0_rec_in["er_W2"],
        "L0_rec_er_b2": _L0_rec_in["er_b2"],
        "L0_rec_ei_W1": _L0_rec_in["ei_W1"],
        "L0_rec_ei_b1": _L0_rec_in["ei_b1"],
        "L0_rec_ei_g1": _L0_rec_in["ei_g1"],
        "L0_rec_ei_be1": _L0_rec_in["ei_be1"],
        "L0_rec_ei_W2": _L0_rec_in["ei_W2"],
        "L0_rec_ei_b2": _L0_rec_in["ei_b2"],
        "L0_rec_Wq_r": _L0_rec_in["Wq_r"],
        "L0_rec_bq_r": _L0_rec_in["bq_r"],
        "L0_rec_Wq_i": _L0_rec_in["Wq_i"],
        "L0_rec_bq_i": _L0_rec_in["bq_i"],
        "L0_rec_Wk_r": _L0_rec_in["Wk_r"],
        "L0_rec_bk_r": _L0_rec_in["bk_r"],
        "L0_rec_Wk_i": _L0_rec_in["Wk_i"],
        "L0_rec_bk_i": _L0_rec_in["bk_i"],
        "L0_rec_Wv_r": _L0_rec_in["Wv_r"],
        "L0_rec_bv_r": _L0_rec_in["bv_r"],
        "L0_rec_Wv_i": _L0_rec_in["Wv_i"],
        "L0_rec_bv_i": _L0_rec_in["bv_i"],
        "L0_rec_Wo_r": _L0_rec_in["Wo_r"],
        "L0_rec_bo_r": _L0_rec_in["bo_r"],
        "L0_rec_Wo_i": _L0_rec_in["Wo_i"],
        "L0_rec_bo_i": _L0_rec_in["bo_i"],
        "L0_rec_int_Wr": _L0_rec_in["int_Wr"],
        "L0_rec_int_Wi": _L0_rec_in["int_Wi"],
        "L0_rec_meas_Mr": _L0_rec_in["meas_Mr"],
        "L0_rec_meas_Mi": _L0_rec_in["meas_Mi"],
        "L0_rec_post_W": _L0_rec_in["post_W"],
        "L0_rec_post_b": _L0_rec_in["post_b"],
        "L0_rec_post_g": _L0_rec_in["post_g"],
        "L0_rec_post_be": _L0_rec_in["post_be"],
    }

def reference(r_x, ids, tbl_0, tbl_1, tbl_2, tbl_3, W_top1, b_top1, W_top2, b_top2, W_top3, L0_rec_er_W1, L0_rec_er_b1, L0_rec_er_g1, L0_rec_er_be1, L0_rec_er_W2, L0_rec_er_b2, L0_rec_ei_W1, L0_rec_ei_b1, L0_rec_ei_g1, L0_rec_ei_be1, L0_rec_ei_W2, L0_rec_ei_b2, L0_rec_Wq_r, L0_rec_bq_r, L0_rec_Wq_i, L0_rec_bq_i, L0_rec_Wk_r, L0_rec_bk_r, L0_rec_Wk_i, L0_rec_bk_i, L0_rec_Wv_r, L0_rec_bv_r, L0_rec_Wv_i, L0_rec_bv_i, L0_rec_Wo_r, L0_rec_bo_r, L0_rec_Wo_i, L0_rec_bo_i, L0_rec_int_Wr, L0_rec_int_Wi, L0_rec_meas_Mr, L0_rec_meas_Mi, L0_rec_post_W, L0_rec_post_b, L0_rec_post_g, L0_rec_post_be):
    import jax
    import jax.numpy as jnp
    def _L0_rec_ref(x, strength, er_W1, er_b1, er_g1, er_be1, er_W2, er_b2, ei_W1, ei_b1, ei_g1, ei_be1, ei_W2, ei_b2, Wq_r, bq_r, Wq_i, bq_i, Wk_r, bk_r, Wk_i, bk_i, Wv_r, bv_r, Wv_i, bv_i, Wo_r, bo_r, Wo_i, bo_i, int_Wr, int_Wi, meas_Mr, meas_Mi, post_W, post_b, post_g, post_be):
        import jax, jax.numpy as jnp
        import numpy as np
        B, IN, HID, D, N, OUT = (4096, 2048, 2048, 512, 4, 512)
        H = 8
        HD = D // H

        def _ln(x, g, b):
            m = x.mean(-1, keepdims=True)
            v = ((x - m) ** 2).mean(-1, keepdims=True)
            return (x - m) / jnp.sqrt(v + 1e-05) * g + b
        Bsz = x.shape[0]

        def enc(W1, b1, g, be, W2, b2):
            h = jax.nn.gelu(_ln(x @ W1.T + b1, g, be), approximate=False)
            return (h @ W2.T + b2).reshape(Bsz, N, D)
        sr = enc(er_W1, er_b1, er_g1, er_be1, er_W2, er_b2)
        si = enc(ei_W1, ei_b1, ei_g1, ei_be1, ei_W2, ei_b2)

        def heads(t):
            return t.reshape(Bsz, N, H, HD).transpose(0, 2, 1, 3)
        qr = heads(sr @ Wq_r.T + bq_r)
        qi = heads(si @ Wq_i.T + bq_i)
        kr = heads(sr @ Wk_r.T + bk_r)
        ki = heads(si @ Wk_i.T + bk_i)
        vr = heads(sr @ Wv_r.T + bv_r)
        vi = heads(si @ Wv_i.T + bv_i)
        ar = jnp.einsum('bhnd,bhmd->bhnm', qr, kr) + jnp.einsum('bhnd,bhmd->bhnm', qi, ki)
        ai = jnp.einsum('bhnd,bhmd->bhnm', qi, kr) - jnp.einsum('bhnd,bhmd->bhnm', qr, ki)
        mag = jnp.sqrt(ar ** 2 + ai ** 2 + 1e-08) * HD ** (-0.5)
        w = jax.nn.softmax(mag, axis=-1)
        out_r = jnp.einsum('bhnm,bhmd->bhnd', w, vr).transpose(0, 2, 1, 3).reshape(Bsz, N, D)
        out_i = jnp.einsum('bhnm,bhmd->bhnd', w, vi).transpose(0, 2, 1, 3).reshape(Bsz, N, D)
        attn_r = out_r @ Wo_r.T + bo_r
        attn_i = out_i @ Wo_i.T + bo_i
        R = jnp.einsum('bnd,ned->bne', attn_r, int_Wr) - jnp.einsum('bnd,ned->bne', attn_i, int_Wi)
        I = jnp.einsum('bnd,ned->bne', attn_r, int_Wi) + jnp.einsum('bnd,ned->bne', attn_i, int_Wr)
        Ri, Ii = (R[:, :, None, :], I[:, :, None, :])
        Rj, Ij = (R[:, None, :, :], I[:, None, :, :])
        phase = jnp.arctan2(Ii * Rj - Ri * Ij, Ri * Rj + Ii * Ij)
        f = jnp.cos(phase) * strength[..., None]
        sup_r = jnp.einsum('bijd,bjd->bd', f, R)
        sup_i = jnp.einsum('bijd,bjd->bd', f, I)
        norm = jnp.sqrt(jnp.sum(sup_r ** 2 + sup_i ** 2, axis=-1, keepdims=True) + 1e-08)
        sup_r = sup_r / norm
        sup_i = sup_i / norm
        mr = sup_r @ meas_Mr.T - sup_i @ meas_Mi.T
        mi = sup_r @ meas_Mi.T + sup_i @ meas_Mr.T
        amp = jnp.sqrt(mr ** 2 + mi ** 2)
        out = jax.nn.gelu(_ln(amp @ post_W.T + post_b, post_g, post_be), approximate=False)
        return out

    e = jnp.stack([tbl_0[ids[:, 0]], tbl_1[ids[:, 1]], tbl_2[ids[:, 2]], tbl_3[ids[:, 3]]], axis=1)
    z = _L0_rec_ref(r_x, e, L0_rec_er_W1, L0_rec_er_b1, L0_rec_er_g1, L0_rec_er_be1, L0_rec_er_W2, L0_rec_er_b2, L0_rec_ei_W1, L0_rec_ei_b1, L0_rec_ei_g1, L0_rec_ei_be1, L0_rec_ei_W2, L0_rec_ei_b2, L0_rec_Wq_r, L0_rec_bq_r, L0_rec_Wq_i, L0_rec_bq_i, L0_rec_Wk_r, L0_rec_bk_r, L0_rec_Wk_i, L0_rec_bk_i, L0_rec_Wv_r, L0_rec_bv_r, L0_rec_Wv_i, L0_rec_bv_i, L0_rec_Wo_r, L0_rec_bo_r, L0_rec_Wo_i, L0_rec_bo_i, L0_rec_int_Wr, L0_rec_int_Wi, L0_rec_meas_Mr, L0_rec_meas_Mi, L0_rec_post_W, L0_rec_post_b, L0_rec_post_g, L0_rec_post_be)
    z = z.reshape(z.shape[0], -1)
    h = jnp.concatenate([z, r_x], axis=1)
    h = jnp.maximum(h @ W_top1 + b_top1, 0.0)
    h = jnp.maximum(h @ W_top2 + b_top2, 0.0)
    y = h @ W_top3
    return y


_drawn_inputs = setup_inputs


def setup_inputs(seed=0):
    import zlib

    import numpy as np

    out = dict(_drawn_inputs(seed))
    spreads = {'b_top1': (0.0, 0.1),
     'b_top2': (0.0, 0.1),
     'L0_rec_er_b1': (0.0, 0.8),
     'L0_rec_er_g1': (1.0, 0.6),
     'L0_rec_er_be1': (0.0, 0.8),
     'L0_rec_er_b2': (0.0, 0.8),
     'L0_rec_ei_b1': (0.0, 0.8),
     'L0_rec_ei_g1': (1.0, 0.6),
     'L0_rec_ei_be1': (0.0, 0.8),
     'L0_rec_ei_b2': (0.0, 0.8),
     'L0_rec_bq_r': (0.0, 0.8),
     'L0_rec_bq_i': (0.0, 0.8),
     'L0_rec_bk_r': (0.0, 0.8),
     'L0_rec_bk_i': (0.0, 0.8),
     'L0_rec_bv_r': (0.0, 0.1),
     'L0_rec_bv_i': (0.0, 0.1),
     'L0_rec_bo_r': (0.0, 0.1),
     'L0_rec_bo_i': (0.0, 0.1),
     'L0_rec_int_Wi': (0.0, 0.1),
     'L0_rec_post_b': (0.0, 0.1),
     'L0_rec_post_g': (1.0, 0.2),
     'L0_rec_post_be': (0.0, 0.1)}
    factors = {'L0_rec_Wq_r': 8.0, 'L0_rec_Wq_i': 8.0, 'L0_rec_Wk_r': 8.0, 'L0_rec_Wk_i': 8.0}
    for name, (base, spread) in spreads.items():
        noise = np.random.default_rng([zlib.crc32(name.encode()), seed]).standard_normal(out[name].shape)
        drawn = base * np.exp(spread * noise) if base else spread * noise
        out[name] = jnp.asarray(drawn.astype(out[name].dtype))
    for name, factor in factors.items():
        out[name] = (out[name] * factor).astype(out[name].dtype)
    return out
```

```python
from contextlib import ExitStack

import numpy as np

import concourse.bass as bass
from concourse import mybir

F32 = mybir.dt.float32
F32R = mybir.dt.float32r
I32 = mybir.dt.int32
ALU = mybir.AluOpType
ACT = mybir.ActivationFunctionType
AX = mybir.AxisListType

P = 128
B = 1024
IN = 2048
HID = 2048
D = 512
N = 4
HEADS = 8
HD = D // HEADS
HALF = 512
NHALF = B // HALF
TPH = HALF // P
TILES = B // P
KT = IN // P
DK = D // P
UNIT_K = 2
UNITS = KT // UNIT_K
CHUNKS = 17
HP = HEADS // 2
EPS = 1e-5
TINY = 1e-37


def wait_apart(eng, sem, value, passed):
    eng.wait_ge(sem, value)
    eng.sem_inc(passed, 1)


def encoder_stage(nc, ctx, dram, consts):
    def sb(name, shape, dt=F32):
        return ctx.enter_context(nc.sbuf_tensor(name, shape, dt))

    def sem(name):
        return ctx.enter_context(nc.semaphore(name))

    ident = consts["ident"]
    a_hi, a_lo = sb("a_hi", [P, KT, HALF], F32R), sb("a_lo", [P, KT, HALF], F32R)
    b_hi, b_lo = sb("b_hi", [P, KT, HALF], F32R), sb("b_lo", [P, KT, HALF], F32R)
    hid = [sb("hid_r", [P, TPH, HID]), sb("hid_i", [P, TPH, HID])]
    raw = sb("raw", [P, 2, UNIT_K, 512])
    w_hi, w_lo = sb("w_hi", [P, 2, UNIT_K, 512], F32R), sb("w_lo", [P, 2, UNIT_K, 512], F32R)
    bias1 = sb("bias1", [P, 512])
    normed = sb("normed", [P, TPH, P])
    stats = sb("stats", [P, TPH, 4, 6])
    mv = sb("mv", [P, TPH, 2])
    var_eps = sb("var_eps", [P, TPH])
    rstd = sb("rstd", [P, TPH])
    neg_half = sb("neg_half", [P, TPH])
    ln_cols = sb("ln_cols_sb", [P, 2, 2, KT])
    b2_cols = sb("b2_cols_sb", [P, 2 * N * DK])
    acc = [ctx.enter_context(nc.psum_tensor(f"acc{t}", [P, 512], F32)) for t in range(4)]
    turn = [ctx.enter_context(nc.psum_tensor(f"turn{t}", [P, 512], F32)) for t in range(2)]

    raw_full = [sem("raw_full0"), sem("raw_full1")]
    raw_free = sem("raw_free")
    x_hi_done, x_lo_done = sem("x_hi_done"), sem("x_lo_done")
    x_in = [sem(f"x_in{q}") for q in range(4)]
    w_hi_done = sem("w_hi_done")
    w_free = sem("w_free")
    acc_done = sem("acc_done")
    acc_free = sem("acc_free")
    bias_in = sem("bias_in")
    params_in = sem("params_in")
    stat_done = sem("stat_done")
    aggr_done = sem("aggr_done")
    eps_done = sem("eps_done")
    rstd_done = sem("rstd_done")
    half_set = sem("half_set")
    norm_done = sem("norm_done")
    turned = sem("turned")
    gelu_done = sem("gelu_done")
    h_hi_done = sem("h_hi_done")
    turn_free = sem("turn_free")
    top_out = sem("top_out")
    passed = sem("passed")
    s_out = [sem("s_out_r"), sem("s_out_i")]

    TOP, L1, L2 = range(3)
    phases = [(0, None, TOP, None), (1, 0, L1, None), (5, 1, L1, 0), (9, 0, L2, 1), (13, 1, L2, None)]
    S_OUT = 16 * N * TPH
    XU = UNITS
    SU = UNITS * CHUNKS

    def load_x(sp, half):
        for q in range(4):
            sp.dma_start(hid[0][:, q, :], dram["x_t"][half, :, q * 4:(q + 1) * 4, :]).then_inc(x_in[q], 16)

    def store_s(sp, enc, half, n):
        for t in range(TPH):
            sp.dma_start(dram["s_t"][enc, bass.ds(half * TPH + t, 1), :, bass.ds(n * DK, DK), :]
                         .rearrange("o p k b -> (o p) k b"),
                         hid[enc][:, bass.ds(n, 1), :].rearrange("p o (k t b) -> p (o k) t b", k=DK, t=TPH)[:, :, t, :]
                         ).then_inc(s_out[enc], 16)

    def x_unit(u):
        return hid[0][:, u // 2, (u % 2) * UNIT_K * 512:(u % 2 + 1) * UNIT_K * 512]

    def loop(eng, count, body):
        body(0, True)
        if count > 1:
            with eng.Fori(1, count) as c:
                body(c, False)

    with nc.Block() as block:

        @block.sync
        def _(sp):
            sp.dma_start(ln_cols[:, :, :, :], dram["ln_cols"]).then_inc(params_in, 16)
            sp.dma_start(b2_cols[:, :], dram["b2_cols"]).then_inc(params_in, 16)
            load_x(sp, 0)
            with sp.Fori(0, NHALF) as half:
                for first, enc, kind, _ in phases:
                    def chunk(c, peeled):
                        ci = c + first
                        for u in range(UNITS):
                            sp.wait_ge(raw_free, half * SU + ci * UNITS + u + 1)
                            sp.dma_start(raw[:, u % 2], dram["enc_w"][ci, u]).then_inc(raw_full[u % 2], 16)
                            if u == 4 and kind != L2:
                                sp.wait_ge(acc_free, half * (4 * CHUNKS) + ci * 4 + 4)
                                sp.dma_start(bias1[:, :], dram["enc_b1"][bass.ds(ci, 1), :].to_broadcast([P, 512])
                                             ).then_inc(bias_in, 16)
                            if u == 5 and kind == L1 and enc == 0 and peeled:
                                sp.dma_start(dram["top_x"][half], hid[1][:, :, 0:512]).then_inc(top_out, 16)
                            if u == 5 and kind == L2 and not (peeled and enc == 0):
                                pe_, pc = (enc, c - 1) if not peeled else (0, 3)
                                sp.wait_ge(acc_free, half * (4 * CHUNKS) + ci * 4 + 4)
                                store_s(sp, pe_, half, pc)
                            if u == 6 and kind == L2 and enc == 1 and peeled:
                                with sp.If(half < NHALF - 1):
                                    sp.wait_ge(s_out[0], half * S_OUT + S_OUT)
                                    load_x(sp, NHALF - 1)
                    loop(sp, 1 if kind == TOP else 4, chunk)
                sp.wait_ge(acc_free, half * (4 * CHUNKS) + 4 * CHUNKS + 4)
                store_s(sp, 1, half, 3)
            sp.wait_ge(s_out[0], S_OUT * NHALF)
            sp.wait_ge(s_out[1], S_OUT * NHALF)
            sp.wait_ge(top_out, 16 * NHALF)

        @block.scalar
        def _(act):
            act.wait_ge(params_in, 32)
            with act.Fori(0, NHALF) as half:
                for u in range(XU):
                    act.wait_ge(x_in[u // 2], half * 16 + 16)
                    if u == 0:
                        act.wait_ge(acc_done, half * (4 * CHUNKS))
                    act.activation(a_hi[:, u * UNIT_K:(u + 1) * UNIT_K, :], x_unit(u), ACT.Copy
                                   ).then_inc(x_hi_done, 1)
                for first, enc, kind, turn_enc in phases:
                    def chunk(c, peeled):
                        ci = c + first
                        for u in range(UNITS):
                            act.wait_ge(raw_full[u % 2],
                                        half * (8 * SU) + ci * (8 * UNITS) + 16 * (u // 2) + 16)
                            if u == 1:
                                act.wait_ge(acc_done, half * (4 * CHUNKS) + ci * 4)
                            else:
                                act.wait_ge(w_free, half * (CHUNKS * (UNITS - 1)) + ci * (UNITS - 1) + max(u - 1, 0))
                            act.activation(w_hi[:, u % 2], raw[:, u % 2], ACT.Copy).then_inc(w_hi_done, 1)
                            if turn_enc is not None and u >= 4:
                                jj = u - 4
                                h_hi = b_hi if turn_enc == 0 else a_hi
                                g = half * (2 * KT) + c * 4 + (turn_enc * KT + jj)
                                kt = c * 4 + jj
                                act.wait_ge(turned, g + 1)
                                act.activation(turn[jj % 2][:, :], turn[jj % 2][:, :], ACT.Gelu,
                                               scale=ln_cols[:, turn_enc, 0, bass.ds(kt, 1)],
                                               bias=ln_cols[:, turn_enc, 1, bass.ds(kt, 1)]).then_inc(gelu_done, 1)
                                act.wait_ge(gelu_done, g + 1)
                                act.activation(h_hi[:, bass.ds(kt, 1), :], turn[jj % 2][:, :], ACT.Copy
                                               ).then_inc(h_hi_done, 1)
                    loop(act, 1 if kind == TOP else 4, chunk)

        @block.gpsimd
        def _(pool):
            pool.sem_inc(raw_free, 2)
            pool.memset(neg_half[:, :], -0.5).then_inc(half_set, 1)
            pool.wait_ge(half_set, 1)
            with pool.Fori(0, NHALF) as half:
                for first, enc, kind, turn_enc in phases:
                    def chunk(c, peeled):
                        ci = c + first
                        for u in range(UNITS):
                            if u == 2 and peeled and turn_enc is not None:
                                pool.wait_ge(eps_done, half * 2 + turn_enc + 1)
                                pool.tensor_tensor(rstd[:, :], var_eps[:, :], neg_half[:, :], ALU.pow
                                                   ).then_inc(rstd_done, 1)
                            pool.wait_ge(w_hi_done, half * (CHUNKS * UNITS) + ci * UNITS + u + 1)
                            pool.tensor_tensor(w_lo[:, u % 2], raw[:, u % 2], w_hi[:, u % 2], ALU.subtract
                                               ).then_inc(raw_free, 1)
                    loop(pool, 1 if kind == TOP else 4, chunk)

        @block.tensor
        def _(pe):
            with pe.Fori(0, NHALF) as half:
                for first, enc, kind, turn_enc in phases:
                    def chunk(c):
                        ci = c + first
                        for u in range(UNITS):
                            pe.wait_ge(raw_free, half * SU + ci * UNITS + (2 + u + 1))
                            if kind == TOP:
                                pe.wait_ge(x_lo_done, half * XU + u + 1)
                            if kind == L2:
                                pe.wait_ge(turn_free, half * (2 * KT) + (2 + enc * KT + UNIT_K * (u + 1)))
                            for kk in range(UNIT_K):
                                k = u * UNIT_K + kk
                                for t in range(4):
                                    if k == 0:
                                        pe.wait_ge(acc_free, half * (4 * CHUNKS) + ci * 4 + t + 1)
                                    if kind == L2:
                                        m_hi, m_lo = (b_hi, b_lo) if enc == 0 else (a_hi, a_lo)
                                        s_hi = w_hi[:, u % 2, kk, t * P:(t + 1) * P]
                                        s_lo = w_lo[:, u % 2, kk, t * P:(t + 1) * P]
                                        m_hi, m_lo = m_hi[:, k, :], m_lo[:, k, :]
                                    else:
                                        s_hi = a_hi[:, k, t * P:(t + 1) * P]
                                        s_lo = a_lo[:, k, t * P:(t + 1) * P]
                                        m_hi, m_lo = w_hi[:, u % 2, kk, :], w_lo[:, u % 2, kk, :]
                                    pe.matmul(acc[t][:, :], s_hi, m_hi, start=(k == 0), stop=False)
                                    pe.matmul(acc[t][:, :], s_hi, m_lo, start=False, stop=False)
                                    mm = pe.matmul(acc[t][:, :], s_lo, m_hi, start=False, stop=(k == KT - 1))
                                    if k == KT - 1:
                                        mm.then_inc(acc_done, 1)
                            if u < UNITS - 1:
                                mm.then_inc(w_free, 1)
                            if turn_enc is not None and 2 <= u < 6:
                                jj = u - 2
                                g = half * (2 * KT) + c * 4 + (turn_enc * KT + jj)
                                pe.wait_ge(norm_done, g * 4 + 4)
                                pe.wait_ge(turn_free, g + 1)
                                for t in range(TPH):
                                    mm = pe.transpose(turn[jj % 2][:, t * P:(t + 1) * P], normed[:, t, :], ident)
                                mm.then_inc(turned, 1)
                    if kind == TOP:
                        chunk(0)
                    else:
                        with pe.Fori(0, 4) as c:
                            chunk(c)

        @block.vector
        def _(dve):
            dve.sem_inc(acc_free, 4)
            dve.sem_inc(turn_free, 2)
            dve.wait_ge(params_in, 32)
            with dve.Fori(0, NHALF) as half:
                for u in range(XU):
                    dve.wait_ge(x_hi_done, half * XU + u + 1)
                    dve.tensor_tensor(a_lo[:, u * UNIT_K:(u + 1) * UNIT_K, :], x_unit(u),
                                      a_hi[:, u * UNIT_K:(u + 1) * UNIT_K, :], ALU.subtract).then_inc(x_lo_done, 1)
                for first, enc, kind, turn_enc in phases:
                    def norm(c, jj):
                        g = half * (2 * KT) + c * 4 + (turn_enc * KT + jj)
                        dve.wait_ge(turned, g)
                        for t in range(TPH):
                            dve.tensor_scalar(normed[:, t, :], hid[turn_enc][:, t, bass.ds(c * 512 + jj * P, P)],
                                              mv[:, t, 0:1], rstd[:, t:t + 1], ALU.subtract, ALU.mult
                                              ).then_inc(norm_done, 1)

                    def low(c, jj):
                        h_hi, h_lo = (b_hi, b_lo) if turn_enc == 0 else (a_hi, a_lo)
                        g = half * (2 * KT) + c * 4 + (turn_enc * KT + jj)
                        kt = c * 4 + jj
                        dve.wait_ge(h_hi_done, g + 1)
                        dve.tensor_tensor(h_lo[:, bass.ds(kt, 1), :], turn[jj % 2][:, :],
                                          h_hi[:, bass.ds(kt, 1), :], ALU.subtract).then_inc(turn_free, 1)

                    def chunk(c, peeled):
                        ci = c + first
                        done = half * (4 * CHUNKS) + ci * 4
                        if turn_enc is not None:
                            norm(c, 0)
                            for jj in range(1, 4):
                                norm(c, jj)
                                low(c, jj - 1)
                            low(c, 3)
                        if kind != L2:
                            dve.wait_ge(bias_in, (half * 9 + ci) * 16 + 16)
                        if kind == TOP:
                            dve.wait_ge(s_out[1], half * S_OUT)
                        if kind == L1 and peeled:
                            if enc == 1:
                                dve.wait_ge(top_out, half * 16 + 16)
                            else:
                                dve.wait_ge(s_out[0], half * S_OUT)
                        for t in range(4):
                            dve.wait_ge(acc_done, done + t + 1)
                            if kind == TOP:
                                dve.tensor_tensor(hid[1][:, t, 0:512], acc[t][:, :], bias1[:, :], ALU.add
                                                  ).then_inc(acc_free, 1)
                            elif kind == L1:
                                h = hid[enc][:, t, bass.ds(c * 512, 512)]
                                dve.tensor_tensor(h, acc[t][:, :], bias1[:, :], ALU.add).then_inc(acc_free, 1)
                                dve.wait_ge(acc_free, done + (4 + t + 1))
                                dve.bn_stats(stats[:, t, bass.ds(c, 1), :], h).then_inc(stat_done, 1)
                            else:
                                dve.tensor_scalar(hid[enc][:, bass.ds(c, 1), t * 512:(t + 1) * 512], acc[t][:, :],
                                                  b2_cols[:, bass.ds(c * DK + (enc * N * DK + t), 1)], None, ALU.add
                                                  ).then_inc(acc_free, 1)
                    if kind == TOP:
                        chunk(0, True)
                    elif kind == L1:
                        loop(dve, 4, chunk)
                        wait_apart(dve, stat_done, half * 32 + (enc * 16 + 16), passed)
                        for t in range(TPH):
                            dve.bn_aggr(mv[:, t, :], stats[:, t, :, :].rearrange("p c s -> p (c s)")
                                        ).then_inc(aggr_done, 1)
                        dve.wait_ge(aggr_done, half * 8 + (enc * 4 + 4))
                        dve.tensor_scalar(var_eps[:, :], mv[:, :, 1], EPS, None, ALU.add).then_inc(eps_done, 1)
                        dve.wait_ge(rstd_done, half * 2 + enc + 1)
                    else:
                        loop(dve, 4, chunk)


def attention_stage(nc, ctx, dram, consts):
    def sb(name, shape, dt=F32):
        return ctx.enter_context(nc.sbuf_tensor(name, shape, dt))

    def sem(name):
        return ctx.enter_context(nc.semaphore(name))

    ident = consts["ident"]
    QKV = 3 * P
    STEPS = TILES * HP
    PAIRS = N * N * 2
    w_hi, w_lo = sb("qkv_hi", [P, 2, DK, HP * QKV], F32R), sb("qkv_lo", [P, 2, DK, HP * QKV], F32R)
    qk_bias = sb("qk_bias_sb", [P, 2, HP, 2 * P])
    v_cols = sb("v_cols_sb", [P, 2, HP])
    s_raw = sb("s_raw", [P, 2, N * DK, P])
    s_hi, s_lo = sb("s_hi", [P, 2, N * DK, P], F32R), sb("s_lo", [P, 2, N * DK, P], F32R)
    qk = sb("qk", [P, 2, 2, 2, N, P])
    vals = sb("vals", [P, HP, 2, N, P])
    prod = sb("prod", [P, 3, 4 * 512])
    o_row = sb("o_row", [P, 2, 2, N, P])
    o_col = sb("o_col", [P, 2, N * P])
    sums = sb("sums", [P, 4, PAIRS])
    soft = sb("soft", [P, 2, PAIRS])
    top = sb("top", [P, 2, N * 2])
    den = sb("den", [P, 2, N * 2])
    rden = sb("rden", [P, 2, N * 2])
    mag_eps = sb("mag_eps", [P, 1])
    acc = [ctx.enter_context(nc.psum_tensor(f"qkv{t}", [P, 512], F32)) for t in range(N)]
    turn = [ctx.enter_context(nc.psum_tensor(f"o_turn{t}", [P, 512], F32)) for t in range(2)]

    SCALE2 = 1.0 / HD

    w_in = [sem(f"qkv_in{i}") for i in range(4)]
    w_hi_done = sem("qkv_hi_done")
    w_lo_done = sem("qkv_lo_done")
    bias_in = sem("qk_bias_in")
    eps_set = sem("mag_eps_set")
    s_in = [sem("s_in_r"), sem("s_in_i")]
    s_hi_done = [sem("s_hi_r"), sem("s_hi_i")]
    s_lo_done = [sem("s_lo_r"), sem("s_lo_i")]
    acc_done = sem("qkv_done")
    qk_out = sem("qk_out")
    v_out = sem("v_out")
    qkp_done = sem("qkp_done")
    qkp_own = sem("qkp_own")
    pvp_done = sem("pvp_done")
    qk_red = sem("qk_red")
    pv_red = sem("pv_red")
    chain = sem("chain")
    mag_done, exp_done = sem("mag_done"), sem("exp_done")
    turned = sem("o_turned")
    col_done = sem("o_col_done")
    o_out = [sem("o_out_r"), sem("o_out_i")]

    SCORES = ((0, 0, 0), (1, 1, 1), (1, 0, 2), (0, 1, 0))

    def score_product(eng, s, a, b, slot, n):
        return eng.tensor_tensor(prod[:, slot, n * 512:(n + 1) * 512].rearrange("p (m f) -> p m f", m=N),
                                 qk[:, s, a, 0, n:n + 1, :].broadcast_to([P, N, P]), qk[:, s, b, 1, :, :], ALU.mult)

    def raw_w(i):
        return prod[:, :, :].rearrange("p s f -> p (s f)")[:, (i % 4) * HP * QKV:(i % 4 + 1) * HP * QKV]

    def tiles(eng, body):
        body(0)
        with eng.Fori(1, TILES) as tile:
            body(tile)

    def exists(tile, hp, lag):
        return not (isinstance(tile, int) and tile * HP + hp < lag)

    with nc.Block() as block:

        @block.sync
        def _(sp):
            sp.dma_start(qk_bias[:, :, :, :], dram["qk_bias"].partition_broadcast(P)).then_inc(bias_in, 16)
            sp.dma_start(v_cols[:, :, :], dram["v_cols"]).then_inc(bias_in, 16)

            for ri in range(2):
                sp.dma_start(s_raw[:, ri], dram["s_t"][ri, 0]).then_inc(s_in[ri], 16)
                for k in range(DK):
                    i = ri * DK + k
                    if i >= 4:
                        sp.wait_ge(w_lo_done, i - 3)
                    sp.dma_start(raw_w(i), dram["qkv_w"][ri, k]).then_inc(w_in[i % 4], 16)

            def col_store(v):
                for ri in range(2):
                    sp.wait_ge(col_done, v * 2 + ri + 1)
                    sp.dma_start(dram["o_t"][ri, bass.ds(v, 1)].rearrange("o p f -> (o p) f"), o_col[:, ri, :]
                                 ).then_inc(o_out[ri], 16)

            def next_s(tile):
                for ri in range(2):
                    sp.wait_ge(s_lo_done[ri], tile)
                    sp.dma_start(s_raw[:, ri], dram["s_t"][ri, bass.ds(tile, 1)].rearrange("o p k b -> (o p) k b")
                                 ).then_inc(s_in[ri], 16)

            next_s(1)
            col_store(0)
            with sp.Fori(2, TILES) as tile:
                next_s(tile)
                for hp in range(HP):
                    col_store(tile * HP + (hp + 1 - 2 * HP))
            for v in range((TILES - 2) * HP + 1, STEPS):
                col_store(v)
            for ri in range(2):
                sp.wait_ge(o_out[ri], 16 * STEPS)

        @block.scalar
        def _(act):
            for i in range(2 * DK):
                if i == 0:
                    act.wait_ge(s_in[0], 16)
                    act.activation(s_hi[:, 0], s_raw[:, 0], ACT.Copy).then_inc(s_hi_done[0], 1)
                if i == DK:
                    act.wait_ge(s_in[1], 16)
                    act.activation(s_hi[:, 1], s_raw[:, 1], ACT.Copy).then_inc(s_hi_done[1], 1)
                act.wait_ge(w_in[i % 4], 16 * (i // 4) + 16)
                act.activation(w_hi[:, i // DK, i % DK, :], raw_w(i), ACT.Copy).then_inc(w_hi_done, 1)
            act.wait_ge(bias_in, 32)
            act.wait_ge(eps_set, 1)

            def next_s_hi(tile, ri, u):
                act.wait_ge(s_in[ri], 16 * tile + 32)
                act.wait_ge(acc_done, u * 8 + (ri * 4 + 4))
                act.activation(s_hi[:, ri], s_raw[:, ri], ACT.Copy).then_inc(s_hi_done[ri], 1)

            def guarded(tile, fn):
                if isinstance(tile, int):
                    fn()
                else:
                    with act.If(tile < TILES - 1):
                        fn()

            def col_out(v, hp):
                for ri in range(2):
                    act.wait_ge(turned, v * 2 + ri + 1)
                    act.wait_ge(o_out[ri], v * 16)
                    act.activation(o_col[:, ri, :], turn[ri][:, :], ACT.Identity,
                                   bias=v_cols[:, ri, hp:hp + 1]).then_inc(col_done, 1)

            def root(v, s):
                act.wait_ge(chain, v * 9 + 4)
                act.activation(soft[:, s, :], soft[:, s, :], ACT.Sqrt, scale=SCALE2, bias=mag_eps[:, 0:1]
                               ).then_inc(mag_done, 1)

            def expo(v, s):
                act.wait_ge(chain, v * 9 + 6)
                act.activation(soft[:, s, :], soft[:, s, :], ACT.Exp).then_inc(exp_done, 1)

            def v_read(u, hp, ri, wait):
                if wait:
                    act.wait_ge(pvp_done, u * 8 - 24)
                for n in range(N):
                    act.wait_ge(qk_out, u * 8 + (ri * 4 + n + 5))
                    act.activation(vals[:, hp, ri, n, :], acc[n][:, 2 * P:3 * P], ACT.Copy).then_inc(v_out, 1)

            def tile_body(tile):
                for hp in range(HP):
                    u = tile * HP + hp
                    if hp == HP - 1:
                        guarded(tile, lambda: next_s_hi(tile, 0, u))
                    if exists(tile, hp, 1):
                        root(tile * HP + (hp - 1), 1 - hp % 2)
                    v_read(u, hp, 1, False)
                    if hp == HP - 1:
                        guarded(tile, lambda: next_s_hi(tile, 1, u))
                    if exists(tile, hp, 1):
                        expo(tile * HP + (hp - 1), 1 - hp % 2)
                    if hp == HP - 1:
                        guarded(tile, lambda: v_read(tile * HP + HP, 0, 0, True))
                    else:
                        v_read(tile * HP + (hp + 1), hp + 1, 0, exists(tile, hp + 1, HP))
                    if exists(tile, hp, 3):
                        col_out(tile * HP + (hp - 3), (hp - 3) % HP)
            v_read(0, 0, 0, False)
            tiles(act, tile_body)
            root(STEPS - 1, 1)
            expo(STEPS - 1, 1)
            for v in range(STEPS - 3, STEPS):
                col_out(v, v % HP)

        @block.tensor
        def _(pe):
            pe.wait_ge(w_lo_done, 1)

            def turn_out(v, s):
                for ri in range(2):
                    pe.wait_ge(pv_red, v * 2 + ri + 1)
                    if not (isinstance(v, int) and v == 0):
                        pe.wait_ge(col_done, v * 2 + ri - 1)
                    for n in range(N):
                        mm = pe.transpose(turn[ri][:, n * P:(n + 1) * P], o_row[:, s, ri, n, :], ident)
                    mm.then_inc(turned, 1)

            def tile_body(tile):
                for hp in range(HP):
                    u = tile * HP + hp
                    for ri in range(2):
                        if hp == 0:
                            pe.wait_ge(s_lo_done[ri], tile + 1)
                        for n in range(N):
                            pe.wait_ge(v_out, u * 8 + (ri * 4 + n + 1))
                            for k in range(DK):
                                if isinstance(tile, int) and hp == 0 and n == 0:
                                    pe.wait_ge(w_lo_done, ri * DK + k + 1)
                                m_hi = w_hi[:, ri, k, hp * QKV:(hp + 1) * QKV]
                                m_lo = w_lo[:, ri, k, hp * QKV:(hp + 1) * QKV]
                                t_hi, t_lo = s_hi[:, ri, n * DK + k, :], s_lo[:, ri, n * DK + k, :]
                                pe.matmul(acc[n][:, 0:QKV], t_hi, m_hi, start=(k == 0), stop=False)
                                pe.matmul(acc[n][:, 0:QKV], t_hi, m_lo, start=False, stop=False)
                                mm = pe.matmul(acc[n][:, 0:QKV], t_lo, m_hi, start=False, stop=(k == DK - 1))
                            mm.then_inc(acc_done, 1)
                    if exists(tile, hp, 3):
                        turn_out(tile * HP + (hp - 3), (hp - 3) % 2)
            tiles(pe, tile_body)
            for v in range(STEPS - 3, STEPS):
                turn_out(v, v % 2)

        @block.gpsimd
        def _(pool):
            pool.memset(mag_eps[:, :], 1e-8 * SCALE2).then_inc(eps_set, 1)
            pool.wait_ge(w_lo_done, 2 * DK)

            def scores(u, s, later, first):
                for c, (a, b, slot) in enumerate(SCORES[:3]):
                    if c == 0:
                        if later:
                            pool.wait_ge(qk_red, u * 4 - 2)
                        pool.wait_ge(qk_out, u * 8 + 8)
                    elif not first:
                        pool.wait_ge(pv_red, u * 2 + (c - 4))
                    if c == 1:
                        pool.wait_ge(qk_out, u * 8 + 12)
                    for n in range(N):
                        score_product(pool, s, a, b, slot, n).then_inc(qkp_done, 1)

            def weighted(v, hp, last):
                for ri in range(2):
                    if ri == 0:
                        pool.wait_ge(chain, v * 9 + 9)
                    if last:
                        pool.wait_ge(pv_red, v * 2 - 1 + ri)
                    else:
                        pool.wait_ge(qk_red, v * 4 + (7 + ri))
                    if ri == 0:
                        pool.wait_ge(v_out, v * 8 + 12)
                    for n in range(N):
                        pool.tensor_tensor(
                            prod[:, 1 + ri, n * 512:(n + 1) * 512].rearrange("p (g f) -> p g f", f=HD),
                            soft[:, hp % 2, n * 8:(n + 1) * 8].unsqueeze(2).broadcast_to([P, 8, HD]),
                            vals[:, hp, ri, :, :].rearrange("p m (h f) -> p (m h) f", f=HD), ALU.mult
                            ).then_inc(pvp_done, 1)

            def tile_body(tile):
                for hp in range(HP):
                    u = tile * HP + hp
                    scores(u, hp % 2, exists(tile, hp, 1), not exists(tile, hp, 2))
                    if exists(tile, hp, 1):
                        weighted(tile * HP + (hp - 1), (hp - 1) % HP, False)
            tiles(pool, tile_body)
            weighted(STEPS - 1, HP - 1, True)

        @block.vector
        def _(dve):
            dve.sem_inc(qk_out, 4)
            dve.sem_inc(v_out, 4)
            for i in range(2 * DK):
                if i % DK == 0:
                    ri = i // DK
                    dve.wait_ge(s_hi_done[ri], 1)
                    dve.tensor_tensor(s_lo[:, ri], s_raw[:, ri], s_hi[:, ri], ALU.subtract
                                      ).then_inc(s_lo_done[ri], 1)
                dve.wait_ge(w_hi_done, i + 1)
                dve.tensor_tensor(w_lo[:, i // DK, i % DK, :], raw_w(i), w_hi[:, i // DK, i % DK, :],
                                  ALU.subtract).then_inc(w_lo_done, 1)
            dve.wait_ge(bias_in, 32)

            def link(v, i, ins):
                ins.then_inc(chain, 1)
                if i not in (4, 6, 9):
                    dve.wait_ge(chain, v * 9 + i)

            def nmh(x):
                return x.rearrange("p (n m h) -> p n m h", n=N, m=N)

            def nhm(x):
                return x.rearrange("p (n m h) -> p n h m", n=N, m=N)

            def over_m(x):
                return x.rearrange("p (n h) -> p n h", n=N).unsqueeze(2).broadcast_to([P, N, N, 2])

            def chain_a(v, s):
                dve.wait_ge(qk_red, v * 4 + 4)
                link(v, 1, dve.tensor_tensor(sums[:, 0, :], sums[:, 0, :], sums[:, 1, :], ALU.add))
                link(v, 2, dve.tensor_tensor(sums[:, 2, :], sums[:, 2, :], sums[:, 3, :], ALU.subtract))
                link(v, 3, dve.tensor_tensor(sums[:, 1:4:2, :], sums[:, 0:3:2, :], sums[:, 0:3:2, :], ALU.mult))
                link(v, 4, dve.tensor_tensor(soft[:, s, :], sums[:, 1, :], sums[:, 3, :], ALU.add))

            def chain_b(v, s):
                dve.wait_ge(mag_done, v + 1)
                link(v, 5, dve.tensor_reduce(top[:, s, :].rearrange("p (n h) -> p n h", n=N), nhm(soft[:, s, :]),
                                             AX.X, ALU.max))
                link(v, 6, dve.tensor_tensor(nmh(soft[:, s, :]), nmh(soft[:, s, :]), over_m(top[:, s, :]),
                                             ALU.subtract))

            def chain_c(v, s):
                dve.wait_ge(exp_done, v + 1)
                link(v, 7, dve.tensor_reduce(den[:, s, :].rearrange("p (n h) -> p n h", n=N), nhm(soft[:, s, :]),
                                             AX.X, ALU.add))
                link(v, 8, dve.reciprocal(rden[:, s, :], den[:, s, :]))
                link(v, 9, dve.tensor_tensor(nmh(soft[:, s, :]), nmh(soft[:, s, :]), over_m(rden[:, s, :]), ALU.mult))

            def weighted_sums(v, s):
                for ri in range(2):
                    dve.wait_ge(pvp_done, v * 8 + (ri * 4 + 4))
                    if ri == 0 and not (isinstance(v, int) and v < 2):
                        dve.wait_ge(turned, v * 2 - 2)
                    dve.tensor_reduce(o_row[:, s, ri, :, :], prod[:, 1 + ri, :].rearrange(
                        "p (n m f) -> p n f m", n=N, m=N), AX.X, ALU.add).then_inc(pv_red, 1)

            def qk_read(u, hp, ri):
                for n in range(N):
                    dve.wait_ge(acc_done, u * 8 + (ri * 4 + n + 1))
                    dve.tensor_tensor(qk[:, hp % 2, ri, :, n, :],
                                      acc[n][:, 0:2 * P].rearrange("p (a f) -> p a f", a=2),
                                      qk_bias[:, ri, hp, :].rearrange("p (a f) -> p a f", a=2),
                                      ALU.add).then_inc(qk_out, 1)

            def next_s_lo(tile, ri):
                dve.wait_ge(s_hi_done[ri], tile + 2)
                dve.tensor_tensor(s_lo[:, ri], s_raw[:, ri], s_hi[:, ri], ALU.subtract).then_inc(s_lo_done[ri], 1)

            def guarded(tile, fn):
                if isinstance(tile, int):
                    fn()
                else:
                    with dve.If(tile < TILES - 1):
                        fn()

            def score_sums(u, s, cs):
                for c in cs:
                    if c == 3:
                        dve.wait_ge(qk_red, u * 4 + 1)
                        for n in range(N):
                            score_product(dve, s, 0, 1, 0, n).then_inc(qkp_own, 1)
                        dve.wait_ge(qkp_own, u * 4 + 4)
                    else:
                        dve.wait_ge(qkp_done, u * 12 + (4 * c + 4))
                    dve.tensor_reduce(sums[:, c, :], prod[:, (0, 1, 2, 0)[c], :].rearrange(
                        "p (g f) -> p g f", f=HD), AX.X, ALU.add).then_inc(qk_red, 1)

            def tile_body(tile):
                for hp in range(HP):
                    u = tile * HP + hp
                    s = hp % 2
                    if hp == HP - 1:
                        guarded(tile, lambda: next_s_lo(tile, 0))
                    qk_read(u, hp, 1)
                    if hp == HP - 1:
                        guarded(tile, lambda: next_s_lo(tile, 1))
                    if exists(tile, hp, 1):
                        chain_b(tile * HP + (hp - 1), 1 - s)
                    if exists(tile, hp, 2):
                        weighted_sums(tile * HP + (hp - 2), s)
                    if exists(tile, hp, 1):
                        chain_c(tile * HP + (hp - 1), 1 - s)
                    score_sums(u, s, (0,))
                    if hp == HP - 1:
                        guarded(tile, lambda: qk_read(tile * HP + HP, 0, 0))
                    else:
                        qk_read(tile * HP + (hp + 1), hp + 1, 0)
                    score_sums(u, s, (3, 1, 2))
                    chain_a(u, s)
            qk_read(0, 0, 0)
            tiles(dve, tile_body)
            chain_b(STEPS - 1, 1)
            chain_c(STEPS - 1, 1)
            weighted_sums(STEPS - 2, 0)
            weighted_sums(STEPS - 1, 1)


def project_stage(nc, ctx, dram):
    def sb(name, shape, dt=F32):
        return ctx.enter_context(nc.sbuf_tensor(name, shape, dt))

    def sem(name):
        return ctx.enter_context(nc.semaphore(name))

    w_raw = sb("wo_raw", [P, 2, DK, D])
    w_hi, w_lo = sb("wo_hi", [P, 2, DK, D], F32R), sb("wo_lo", [P, 2, DK, D], F32R)
    bo = sb("bo_cols_sb", [P, 2, DK])
    o_raw = sb("o_raw", [P, 2, DK, N * P])
    o_hi, o_lo = sb("o_hi", [P, 2, DK, N * P], F32R), sb("o_lo", [P, 2, DK, N * P], F32R)
    a_out = sb("a_out", [P, 2, N, DK, P])
    acc = [[ctx.enter_context(nc.psum_tensor(f"wo_acc{ri}{j}", [P, 512], F32)) for j in range(DK)] for ri in range(2)]

    w_in, w_hi_done, w_lo_done = [[sem(f"wo_{x}{ri}") for ri in range(2)] for x in ("in", "hi", "lo")]
    o_in, o_hi_done, o_lo_done = [[sem(f"o_{x}{ri}") for ri in range(2)] for x in ("in", "hi_done", "lo_done")]
    bo_in = sem("bo_in")
    acc_done, read_out = [[sem(f"wo_{x}{ri}") for ri in range(2)] for x in ("acc", "read")]
    a_stored = [sem("a_stored_r"), sem("a_stored_i")]

    with nc.Block() as block:

        @block.sync
        def _(sp):
            def load(tile, ri):
                sp.dma_start(o_raw[:, ri], dram["o_t"][ri, bass.ds(tile * HP, HP)].rearrange("k p f -> p k f")
                             ).then_inc(o_in[ri], 16)

            def store(tile, ri):
                sp.wait_ge(read_out[ri], tile * DK + DK)
                sp.dma_start(dram["a_t"][ri, bass.ds(tile, 1)].rearrange("o p n f -> (o p) n f"),
                             a_out[:, ri].rearrange("p n k b -> p n (k b)")).then_inc(a_stored[ri], 16)

            for ri in range(2):
                sp.dma_start(w_raw[:, ri], dram["wo_w"][ri]).then_inc(w_in[ri], 16)
                load(0, ri)
            sp.dma_start(bo[:, :, :], dram["bo_cols"]).then_inc(bo_in, 16)
            with sp.Fori(0, TILES - 1) as tile:
                for ri in range(2):
                    sp.wait_ge(o_lo_done[ri], tile + 1)
                    load(tile + 1, ri)
                for ri in range(2):
                    store(tile, ri)
            for ri in range(2):
                store(TILES - 1, ri)
            for ri in range(2):
                sp.wait_ge(a_stored[ri], 16 * TILES)

        @block.scalar
        def _(act):
            def split_high(tile, ri, first=False):
                act.wait_ge(o_in[ri], tile * 16 + 16)
                if not first:
                    act.wait_ge(acc_done[ri], tile * DK)
                act.activation(o_hi[:, ri], o_raw[:, ri], ACT.Copy).then_inc(o_hi_done[ri], 1)

            def read(tile, ri):
                act.wait_ge(a_stored[ri], tile * 16)
                for j in range(DK):
                    act.wait_ge(acc_done[ri], tile * DK + j + 1)
                    act.activation(a_out[:, ri, :, j, :], acc[ri][j][:, :].rearrange("p (n b) -> p n b", n=N),
                                   ACT.Identity, bias=bo[:, ri, j:j + 1]).then_inc(read_out[ri], 1)

            for ri in range(2):
                act.wait_ge(w_in[ri], 16)
                act.activation(w_hi[:, ri], w_raw[:, ri], ACT.Copy).then_inc(w_hi_done[ri], 1)
                split_high(0, ri, True)
            act.wait_ge(bo_in, 16)
            with act.Fori(0, TILES - 1) as tile:
                for ri in range(2):
                    split_high(tile + 1, ri)
                    read(tile, ri)
            for ri in range(2):
                read(TILES - 1, ri)

        @block.tensor
        def _(pe):
            for ri in range(2):
                pe.wait_ge(w_lo_done[ri], 1)
            with pe.Fori(0, TILES) as tile:
                for ri in range(2):
                    pe.wait_ge(o_lo_done[ri], tile + 1)
                    pe.wait_ge(read_out[ri], tile * DK)
                    for j in range(DK):
                        for k in range(DK):
                            s_hi, s_lo = w_hi[:, ri, k, j * P:(j + 1) * P], w_lo[:, ri, k, j * P:(j + 1) * P]
                            m_hi, m_lo = o_hi[:, ri, k, :], o_lo[:, ri, k, :]
                            pe.matmul(acc[ri][j][:, :], s_hi, m_hi, start=(k == 0), stop=False)
                            pe.matmul(acc[ri][j][:, :], s_hi, m_lo, start=False, stop=False)
                            mm = pe.matmul(acc[ri][j][:, :], s_lo, m_hi, start=False, stop=(k == DK - 1))
                        mm.then_inc(acc_done[ri], 1)

        @block.vector
        def _(dve):
            def split_low(tile, ri):
                dve.wait_ge(o_hi_done[ri], tile + 1)
                dve.tensor_tensor(o_lo[:, ri], o_raw[:, ri], o_hi[:, ri], ALU.subtract).then_inc(o_lo_done[ri], 1)

            for ri in range(2):
                dve.wait_ge(w_hi_done[ri], 1)
                dve.tensor_tensor(w_lo[:, ri], w_raw[:, ri], w_hi[:, ri], ALU.subtract).then_inc(w_lo_done[ri], 1)
                split_low(0, ri)
            with dve.Fori(1, TILES) as tile:
                for ri in range(2):
                    split_low(tile, ri)


def interact_stage(nc, ctx, dram):
    def sb(name, shape, dt=F32):
        return ctx.enter_context(nc.sbuf_tensor(name, shape, dt))

    def sem(name):
        return ctx.enter_context(nc.semaphore(name))

    H = D // 2
    WPIECES = 2 * N
    w_hi, w_lo = sb("int_hi", [P, 2, N, DK, D], F32R), sb("int_lo", [P, 2, N, DK, D], F32R)
    a_raw = sb("a_raw", [P, 2, 2, DK * P])
    a_hi = sb("a_hi2", [P, 2, 2, DK * P], F32R)
    a_lo = sb("a_lo2", [P, 2, 2, DK * P], F32R)
    ri_rows = sb("ri_rows", [P, 2, 2, N, D])
    r2 = sb("r2", [P, 2, D])
    cos, sin = sb("cos", [P, N, H]), sb("sin", [P, N, H])
    zero = sb("zero", [P, N, H])
    x = sb("x", [P, N, H])
    q = sb("q", [P, N, H])
    tt = sb("tt", [P, N, H])
    sup = sb("sup", [P, 2, D])
    norm = sb("norm", [P, 4])
    neg_half = sb("neg_half2", [P, 1])
    ids = sb("ids_sb", [P, TILES, N], I32)
    strength = sb("strength", [P, TILES, N * N])
    strength_t = sb("strength_t", [P, 2, N * N])
    tiny = sb("tiny", [P, 1])
    acc_r1, acc_r2, acc_i = [[ctx.enter_context(nc.psum_tensor(f"{x_}{s}", [P, D], F32)) for s in range(2)]
                             for x_ in ("acc_r1", "acc_r2", "acc_i")]

    w_in = [sem(f"int_in{i}") for i in range(4)]
    w_hi_done, w_lo_done = sem("int_hi_done"), sem("int_lo_done")
    ids_in, strength_in = sem("ids_in"), sem("strength_in")
    const_set = sem("const_set")
    a_in = [sem("a_in0"), sem("a_in1")]
    a_hi_done, a_lo_done = sem("a_hi_done"), sem("a_lo_done")
    r2_done, r1_done, i_done = sem("r2_done"), sem("r1_done"), sem("i_done")
    r2_out = sem("r2_out")
    r_out, i_out = sem("r_out"), sem("i_out")
    squared = sem("squared")
    summed = sem("summed")
    strength_now = sem("strength_now")
    log_done = sem("log_done")
    inv_done = sem("inv_done")
    cos_done, sin_done = sem("cos_done"), sem("sin_done")
    t_steps, p_steps, q_terms = sem("t_steps"), sem("p_steps"), sem("q_terms")
    q_steps = sem("q_steps")
    cp_done, sq_done = sem("cp_done"), sem("sq_done")
    f_steps = sem("f_steps")
    fr_done, fi_done = sem("fr_done"), sem("fi_done")
    red_done = sem("red_done")
    norm_steps = sem("norm_steps")
    rnorm_done = sem("rnorm_done")
    sup_ready = sem("sup_ready")
    sup_stored = sem("sup_stored")
    passed = sem("passed_i")

    def raw_w(i):
        return ri_rows[:, (i % 4) // 2, i % 2, :, :]

    def run(eng, body):
        body(0, 0, False)
        body(1, 1, True)
        with eng.Fori(1, TILES // 2) as pair:
            for s in range(2):
                body(pair * 2 + s, s, True)

    def others(j):
        return [i for i in range(N) if i != j]

    def s_col(s, i, j):
        return strength_t[:, s, i * N + j:i * N + j + 1]

    with nc.Block() as block:

        @block.sync
        def _(sp):
            sp.dma_start(ids[:, :, :], dram["ids"]).then_inc(ids_in, 16)

            def load(tile, n):
                sp.dma_start(a_raw[:, n % 2], dram["a_t"][:, bass.ds(tile, 1), :, n, :]
                             .rearrange("r o p f -> (o p) r f")).then_inc(a_in[n % 2], 16)

            load(0, 0)
            load(0, 1)
            for i in range(WPIECES):
                if i >= 4:
                    sp.wait_ge(w_lo_done, i - 3)
                sp.dma_start(raw_w(i), dram["int_w"][i]).then_inc(w_in[i % 4], 16)

            def store(tile):
                sp.wait_ge(sup_ready, tile + 1)
                sp.dma_start(dram["sup_d"][bass.ds(tile, 1)].rearrange("o p r f -> (o p) r f"), sup[:, :, :]
                             ).then_inc(sup_stored, 16)

            def body(tile, later):
                for n in range(N):
                    sp.wait_ge(a_lo_done, tile * N + n + 1)
                    load(tile if n < 2 else tile + 1, (n + 2) % N)
                if later:
                    store(tile - 1)

            body(0, False)
            with sp.Fori(1, TILES - 1) as tile:
                body(tile, True)
            for n in range(2):
                sp.wait_ge(a_lo_done, (TILES - 1) * N + n + 1)
                load(TILES - 1, n + 2)
            store(TILES - 2)
            store(TILES - 1)
            sp.wait_ge(sup_stored, 16 * TILES)

        @block.scalar
        def _(act):
            def split_high(g, n, first=False):
                s = n % 2
                act.wait_ge(a_in[s], (g - s) * 8 + 16)
                if not first:
                    act.wait_ge(i_done, g - 1)
                act.activation(a_hi[:, s], a_raw[:, s], ACT.Copy).then_inc(a_hi_done, 1)

            def squares(tile, s, h):
                v = tile * 2 + h
                if h == 0:
                    act.wait_ge(r_out, tile * N + N + 2)
                    act.wait_ge(i_out, tile * N + N + 2)
                act.wait_ge(fr_done, v)
                act.wait_ge(fi_done, v)
                act.activation(x[:, :, :], ri_rows[:, s, 0, :, h * H:(h + 1) * H], ACT.Square).then_inc(squared, 1)
                act.wait_ge(red_done, v * 2)
                act.activation(q[:, :, :], ri_rows[:, s, 1, :, h * H:(h + 1) * H], ACT.Square).then_inc(squared, 1)
                act.wait_ge(summed, v * 2 + 2)
                act.activation(x[:, :, :], x[:, :, :], ACT.Ln, bias=tiny[:, 0:1]).then_inc(log_done, 1)
                act.wait_ge(log_done, v + 1)
                act.activation(x[:, :, :], x[:, :, :], ACT.Exp, scale=-0.5).then_inc(inv_done, 1)

            def q_term(s, v, m):
                if m == 0:
                    act.wait_ge(sin_done, v + 1)
                elif m == 1:
                    act.wait_ge(t_steps, v * 12 + 12)
                else:
                    act.wait_ge(q_steps, v * 2 + 1)
                for j in range(N):
                    i = others(j)[m]
                    act.activation((q if m == 0 else zero)[:, j, :], sin[:, i, :], ACT.Copy, scale=s_col(s, i, j)
                                   ).then_inc(q_terms, 1)

            for i in range(WPIECES):
                act.wait_ge(w_in[i % 4], 16 * (i // 4) + 16)
                act.activation(w_hi[:, i // N, i % N], raw_w(i), ACT.Copy).then_inc(w_hi_done, 1)
            split_high(0, 0, True)
            act.wait_ge(const_set, 2)

            def body(tile, s, later, last=False):
                for n in range(N):
                    g = tile * N + n
                    if not (last and n == N - 1):
                        split_high(g + 1, n + 1, isinstance(tile, int) and g == 0)
                    act.wait_ge(r2_done, g + 1)
                    act.wait_ge(r_out, g + 1)
                    act.activation(r2[:, n % 2, :], acc_r2[n % 2][:, :], ACT.Copy).then_inc(r2_out, 1)
                    if later and n % 2 == 0:
                        squares(tile - 1, 1 - s, n // 2)
                        q_term(1 - s, (tile - 1) * 2 + n // 2, 0)
                        q_term(1 - s, (tile - 1) * 2 + n // 2, 1)
                    if later and n % 2 == 1:
                        q_term(1 - s, (tile - 1) * 2 + n // 2, 2)
                    act.wait_ge(i_done, g + 1)
                    if n == 0:
                        if isinstance(tile, int) and tile < 2:
                            act.wait_ge(w_lo_done, WPIECES)
                        else:
                            act.wait_ge(fi_done, tile * 2 - 2)
                    act.activation(ri_rows[:, s, 1, n, :], acc_i[n % 2][:, :], ACT.Copy).then_inc(i_out, 1)
            body(0, 0, False)
            body(1, 1, True)
            with act.Fori(1, TILES // 2 - 1) as pair:
                for s in range(2):
                    body(pair * 2 + s, s, True)
            body(TILES - 2, 0, True)
            body(TILES - 1, 1, True, True)
            for h in range(2):
                squares(TILES - 1, 1, h)
                for m in range(N - 1):
                    q_term(1, (TILES - 1) * 2 + h, m)

        @block.tensor
        def _(pe):
            pe.wait_ge(w_lo_done, WPIECES)

            with pe.Fori(0, TILES) as tile:
                for n in range(N):
                    g = tile * N + n
                    s = n % 2
                    pe.wait_ge(a_lo_done, g + 1)
                    pe.wait_ge(r_out, g + 1)
                    pe.wait_ge(i_out, g + 1)
                    for bank, parts, done in ((acc_r2[s], ((1, 1),), r2_done), (acc_r1[s], ((0, 0),), r1_done),
                                              (acc_i[s], ((0, 1), (1, 0)), i_done)):
                        for ai_, wi in parts:
                            for k in range(DK):
                                s_hi, s_lo = a_hi[:, s, ai_, k * P:(k + 1) * P], a_lo[:, s, ai_, k * P:(k + 1) * P]
                                m_hi, m_lo = w_hi[:, wi, n, k, :], w_lo[:, wi, n, k, :]
                                start = k == 0 and (ai_, wi) == parts[0]
                                stop = k == DK - 1 and (ai_, wi) == parts[-1]
                                pe.matmul(bank[:, :], s_hi, m_hi, start=start, stop=False)
                                pe.matmul(bank[:, :], s_hi, m_lo, start=False, stop=False)
                                mm = pe.matmul(bank[:, :], s_lo, m_hi, start=False, stop=stop)
                        mm.then_inc(done, 1)

        @block.gpsimd
        def _(pool):
            pool.memset(neg_half[:, :], -0.5).then_inc(const_set, 1)
            pool.memset(tiny[:, :], TINY).then_inc(const_set, 1)
            pool.wait_ge(ids_in, 16)
            for t in range(TILES):
                for f in range(N):
                    pool.indirect_dma_start(
                        out=strength[:, t, f * N:(f + 1) * N], out_offset=None, in_=dram[f"tbl_{f}"],
                        in_offset=bass.IndirectOffsetOnAxis(ap=ids[:, t, f:f + 1], axis=0)).then_inc(strength_in, 16)
            pool.wait_ge(const_set, 2)
            pool.wait_ge(strength_in, 16 * TILES * N)

            def split_low(g, s):
                pool.wait_ge(a_hi_done, g + 1)
                pool.tensor_tensor(a_lo[:, s], a_raw[:, s], a_hi[:, s], ALU.subtract).then_inc(a_lo_done, 1)

            def part_a(tile, s, h):
                v = tile * 2 + h
                pool.wait_ge(inv_done, v + 1)
                pool.tensor_tensor(sin[:, :, :], ri_rows[:, s, 1, :, h * H:(h + 1) * H], x[:, :, :], ALU.mult
                                   ).then_inc(sin_done, 1)

            def part_b(tile, s, h):
                v = tile * 2 + h
                for m in range(1, N - 1):
                    pool.wait_ge(q_terms, v * 12 + (m * 4 + 4))
                    pool.tensor_tensor(q[:, :, :], q[:, :, :], zero[:, :, :], ALU.add).then_inc(q_steps, 1)
                    pool.wait_ge(q_steps, v * 2 + m)
                pool.tensor_tensor(q[:, :, :], sin[:, :, :], q[:, :, :], ALU.mult).then_inc(sq_done, 1)
                pool.wait_ge(f_steps, v * 2 + 2)
                pool.tensor_tensor(q[:, :, :], ri_rows[:, s, 1, :, h * H:(h + 1) * H], x[:, :, :], ALU.mult
                                   ).then_inc(fi_done, 1)
                if h == 1:
                    pool.wait_ge(norm_steps, tile * 3 + 3)
                    pool.tensor_tensor(norm[:, 2:3], norm[:, 1:2], neg_half[:, 0:1], ALU.pow).then_inc(rnorm_done, 1)

            split_low(0, 0)

            def body(tile, s, later, last=False):
                for n in range(N):
                    if not (last and n == N - 1):
                        split_low(tile * N + n + 1, (n + 1) % 2)
                    if later:
                        (part_b if n % 2 else part_a)(tile - 1, 1 - s, n // 2)
            body(0, 0, False)
            body(1, 1, True)
            with pool.Fori(1, TILES // 2 - 1) as pair:
                for s in range(2):
                    body(pair * 2 + s, s, True)
            body(TILES - 2, 0, True)
            body(TILES - 1, 1, True, True)
            for h in range(2):
                part_a(TILES - 1, 1, h)
                part_b(TILES - 1, 1, h)

        @block.vector
        def _(dve):
            dve.sem_inc(r_out, 2)
            dve.sem_inc(i_out, 2)
            for i in range(WPIECES):
                dve.wait_ge(w_hi_done, i + 1)
                dve.tensor_tensor(w_lo[:, i // N, i % N], raw_w(i), w_hi[:, i // N, i % N], ALU.subtract
                                  ).then_inc(w_lo_done, 1)
            dve.wait_ge(strength_in, 16 * TILES * N)

            def read_r(tile, s, n):
                g = tile * N + n
                dve.wait_ge(r2_out, g + 1)
                dve.wait_ge(r1_done, g + 1)
                dve.tensor_tensor(ri_rows[:, s, 0, n, :], acc_r1[n % 2][:, :], r2[:, n % 2, :], ALU.subtract
                                  ).then_inc(r_out, 1)

            def part_a(tile, s, h):
                v = tile * 2 + h
                if h == 0:
                    dve.tensor_copy(strength_t[:, s, :], strength[:, bass.ds(tile, 1), :].rearrange("p o f -> p (o f)")
                                    ).then_inc(strength_now, 1)
                dve.wait_ge(squared, v * 2 + 2)
                dve.tensor_tensor(x[:, :, :], x[:, :, :], q[:, :, :], ALU.add).then_inc(summed, 1)
                dve.wait_ge(summed, v * 2 + 1)
                dve.tensor_scalar(zero[:, :, :], x[:, :, :], 0.0, None, ALU.is_equal).then_inc(summed, 1)
                dve.wait_ge(summed, v * 2 + 2)
                dve.wait_ge(strength_now, tile + 1)
                for m in range(N - 1):
                    if m > 0:
                        wait_apart(dve, t_steps, v * 12 + m * 4, passed)
                    for j in range(N):
                        i = others(j)[m]
                        if m == 0:
                            dve.tensor_scalar(tt[:, j, :], zero[:, i, :], s_col(s, i, j), s_col(s, j, j),
                                              ALU.mult, ALU.add).then_inc(t_steps, 1)
                        else:
                            dve.scalar_tensor_tensor(out=tt[:, j, :], in0=zero[:, i, :], scalar=s_col(s, i, j),
                                                     in1=tt[:, j, :], op0=ALU.mult, op1=ALU.add).then_inc(t_steps, 1)
                dve.wait_ge(inv_done, v + 1)
                dve.tensor_tensor(cos[:, :, :], ri_rows[:, s, 0, :, h * H:(h + 1) * H], x[:, :, :], ALU.mult
                                  ).then_inc(cos_done, 1)
                dve.wait_ge(cos_done, v + 1)
                wait_apart(dve, sin_done, v + 1, passed)
                for m in range(N - 1):
                    if m > 0:
                        wait_apart(dve, p_steps, v * 12 + m * 4, passed)
                    for j in range(N):
                        i = others(j)[m]
                        if m == 0:
                            dve.tensor_scalar(x[:, j, :], cos[:, i, :], s_col(s, i, j), None, ALU.mult
                                              ).then_inc(p_steps, 1)
                        else:
                            dve.scalar_tensor_tensor(out=x[:, j, :], in0=cos[:, i, :], scalar=s_col(s, i, j),
                                                     in1=x[:, j, :], op0=ALU.mult, op1=ALU.add).then_inc(p_steps, 1)

            def part_b(tile, s, h):
                v = tile * 2 + h
                dve.wait_ge(p_steps, v * 12 + 12)
                dve.tensor_tensor(x[:, :, :], cos[:, :, :], x[:, :, :], ALU.mult).then_inc(cp_done, 1)
                dve.wait_ge(sq_done, v + 1)
                dve.wait_ge(t_steps, v * 12 + 12)
                dve.tensor_tensor(tt[:, :, :], tt[:, :, :], q[:, :, :], ALU.add).then_inc(f_steps, 1)
                dve.wait_ge(cp_done, v + 1)
                dve.wait_ge(f_steps, v * 2 + 1)
                dve.tensor_tensor(x[:, :, :], x[:, :, :], tt[:, :, :], ALU.add).then_inc(f_steps, 1)
                dve.wait_ge(f_steps, v * 2 + 2)
                dve.tensor_tensor(tt[:, :, :], ri_rows[:, s, 0, :, h * H:(h + 1) * H], x[:, :, :], ALU.mult
                                  ).then_inc(fr_done, 1)
                if h == 0:
                    dve.wait_ge(sup_stored, tile * 16)
                dve.wait_ge(fr_done, v + 1)
                dve.tensor_reduce(sup[:, 0, h * H:(h + 1) * H], tt[:, :, :].rearrange("p n f -> p f n"),
                                  AX.X, ALU.add).then_inc(red_done, 1)
                dve.wait_ge(fi_done, v + 1)
                dve.tensor_reduce(sup[:, 1, h * H:(h + 1) * H], q[:, :, :].rearrange("p n f -> p f n"),
                                  AX.X, ALU.add).then_inc(red_done, 1)
                if h == 1:
                    dve.wait_ge(red_done, v * 2 + 2)
                    dve.tensor_tensor(tt[:, :, :].rearrange("p n f -> p (n f)"),
                                      sup[:, :, :].rearrange("p r f -> p (r f)"),
                                      sup[:, :, :].rearrange("p r f -> p (r f)"), ALU.mult).then_inc(norm_steps, 1)
                    dve.wait_ge(norm_steps, tile * 3 + 1)
                    dve.tensor_reduce(norm[:, 0:1], tt[:, :, :].rearrange("p n f -> p (n f)"), AX.X, ALU.add
                                      ).then_inc(norm_steps, 1)
                    dve.wait_ge(norm_steps, tile * 3 + 2)
                    dve.tensor_scalar(norm[:, 1:2], norm[:, 0:1], 1e-8, None, ALU.add).then_inc(norm_steps, 1)
                    dve.wait_ge(rnorm_done, tile + 1)
                    dve.tensor_scalar(sup[:, :, :], sup[:, :, :], norm[:, 2:3], None, ALU.mult).then_inc(sup_ready, 1)

            def body(tile, s, later):
                for n in range(N):
                    read_r(tile, s, n)
                    if later:
                        (part_b if n % 2 else part_a)(tile - 1, 1 - s, n // 2)
            run(dve, body)
            for h in range(2):
                part_a(TILES - 1, 1, h)
                part_b(TILES - 1, 1, h)


def measure_stage(nc, ctx, dram, consts):
    def sb(name, shape, dt=F32):
        return ctx.enter_context(nc.sbuf_tensor(name, shape, dt))

    def sem(name):
        return ctx.enter_context(nc.semaphore(name))

    ident = consts["ident"]
    D2 = 256
    w_raw = sb("m_raw", [P, 2, DK * D])
    meas_hi, meas_lo = sb("meas_hi", [P, 2, DK, D], F32R), sb("meas_lo", [P, 2, DK, D], F32R)
    post_hi, post_lo = sb("post_hi", [P, DK, D], F32R), sb("post_lo", [P, DK, D], F32R)
    top1_hi, top1_lo = sb("top1_hi", [P, DK, D], F32R), sb("top1_lo", [P, DK, D], F32R)
    top2_hi, top2_lo = sb("top2_hi", [P, DK, D2], F32R), sb("top2_lo", [P, DK, D2], F32R)
    post_b = sb("post_b_sb", [P, D])
    post_cols = sb("post_cols_sb", [P, 2, DK])
    top2_cols = sb("top2_cols_sb", [P, 2])
    top3_cols = sb("top3_cols_sb", [P, 2])
    sup_row = sb("sup_row", [P, TPH, 2, D])
    row = sb("row", [P, TPH, D])
    topx = sb("topx", [P, TPH, D])
    sup_hi, sup_lo = sb("sup_hi", [P, 2, DK, HALF], F32R), sb("sup_lo", [P, 2, DK, HALF], F32R)
    amp_hi, amp_lo = sb("amp_hi", [P, DK, HALF], F32R), sb("amp_lo", [P, DK, HALF], F32R)
    z_hi, z_lo = sb("z_hi", [P, DK, HALF], F32R), sb("z_lo", [P, DK, HALF], F32R)
    h_hi, h_lo = sb("h1_hi", [P, DK, HALF], F32R), sb("h1_lo", [P, DK, HALF], F32R)
    mr = sb("mr", [P, 2, HALF])
    mi = sb("mi", [P, 2, HALF])
    h2 = sb("h2", [P, 2, HALF])
    y_row = sb("y_row", [1, NHALF, HALF])
    stats = sb("post_stats", [P, TPH, 6])
    mv = sb("post_mv", [P, TPH, 2])
    var_eps, rstd = sb("post_var", [P, TPH]), sb("post_rstd", [P, TPH])
    neg_half = sb("neg_half3", [P, TPH])
    turn = [ctx.enter_context(nc.psum_tensor(f"m_turn{s}", [P, 512], F32)) for s in range(2)]
    acc_a, acc_b, acc_c = [[ctx.enter_context(nc.psum_tensor(f"m_acc_{x}{s}", [P, 512], F32)) for s in range(2)]
                           for x in "abc"]

    weights = [(dram["meas_w"][0], meas_hi[:, 0], meas_lo[:, 0]), (dram["meas_w"][1], meas_hi[:, 1], meas_lo[:, 1]),
               (dram["post_w"], post_hi[:, :, :], post_lo[:, :, :]),
               (dram["top1_w"], top1_hi[:, :, :], top1_lo[:, :, :]),
               (dram["top2_w"], top2_hi[:, :, :], top2_lo[:, :, :])]
    NW = len(weights)

    def raw(i):
        n = weights[i][1].shape[-1]
        return w_raw[:, i % 2, 0:DK * n].rearrange("p (k f) -> p k f", f=n)

    w_in = [sem("m_in0"), sem("m_in1")]
    w_hi_done, w_lo_done = sem("m_w_hi"), sem("m_w_lo")
    cols_in, sup_in, topx_in = sem("cols_in"), sem("sup_in"), sem("topx_in")
    turned = sem("m_turned")
    hi_done = sem("m_hi_done")
    lo_done = sem("m_lo_done")
    a_done, b_done, c_done = sem("ma_done"), sem("mb_done"), sem("mc_done")
    b_out, mi_done, mr_done = sem("mb_out"), sem("mi_done"), sem("mr_done")
    mr_squared, mag_summed, amp_done = sem("mr_squared"), sem("mag_summed"), sem("amp_done")
    amp_hi_done, amp_lo_done = sem("amp_hi_done"), sem("amp_lo_done")
    row_done, row_out = sem("row_done"), sem("row_out")
    stat_done, aggr_done, eps_done, rstd_done, half_set, normed = [
        sem(f"m_{x}") for x in ("stat", "aggr", "eps", "rstd", "half", "normed")]
    gelu_done = sem("m_gelu")
    h2_acc, h2_done, y_acc, y_out, y_stored = sem("h2_acc"), sem("h2_done"), sem("y_acc"), sem("y_out"), sem("y_stored")
    passed = sem("passed_m")
    TURNS = 2 * DK + DK + DK

    with nc.Block() as block:

        @block.sync
        def _(sp):
            def load_half(half):
                for t in range(TPH):
                    sp.dma_start(sup_row[:, t], dram["sup_d"][bass.ds(half * TPH + t, 1)]
                                 .rearrange("o p r f -> (o p) r f")).then_inc(sup_in, 16)
                sp.dma_start(topx[:, :, :], dram["top_x"][bass.ds(half, 1)].rearrange("o p t f -> (o p) t f")
                             ).then_inc(topx_in, 16)

            sp.dma_start(raw(0), weights[0][0]).then_inc(w_in[0], 16)
            load_half(0)
            sp.dma_start(raw(1), weights[1][0]).then_inc(w_in[1], 16)
            sp.dma_start(post_b[:, :], dram["post_row"].to_broadcast([P, D])).then_inc(cols_in, 16)
            sp.dma_start(post_cols[:, :, :], dram["post_cols"]).then_inc(cols_in, 16)
            sp.dma_start(top2_cols[:, :], dram["top2_cols"]).then_inc(cols_in, 16)
            sp.dma_start(top3_cols[:, :], dram["top3_cols"]).then_inc(cols_in, 16)
            for i in range(2, NW):
                sp.wait_ge(w_lo_done, i - 1)
                sp.dma_start(raw(i), weights[i][0]).then_inc(w_in[i % 2], 16)
            for half in range(1, NHALF):
                sp.wait_ge(turned, (half - 1) * TURNS + 2 * DK)
                sp.wait_ge(row_out, (half - 1) * 2 * TPH + 2 * TPH)
                load_half(half)
            for half in range(NHALF):
                sp.wait_ge(y_out, half + 1)
                sp.dma_start(dram["y"][half * HALF:(half + 1) * HALF, :].rearrange("f o -> o f"),
                             y_row[:, half, :]).then_inc(y_stored, 16)
            sp.wait_ge(y_stored, 16 * NHALF)

        @block.scalar
        def _(act):
            def turn_high(half, i, dst, fn):
                g = half * TURNS + i
                act.wait_ge(turned, g + 1)
                act.activation(dst, turn[i % 2][:, :], fn).then_inc(hi_done, 1)

            def split_weights(i):
                act.wait_ge(w_in[i % 2], 16 * (i // 2) + 16)
                act.activation(weights[i][1], raw(i), ACT.Copy).then_inc(w_hi_done, 1)

            for i in range(NW):
                split_weights(i)
            act.wait_ge(cols_in, 64)
            with act.Fori(0, NHALF) as half:
                act.wait_ge(c_done, half * DK)
                for i in range(2 * DK):
                    turn_high(half, i, sup_hi[:, i // DK, i % DK, :], ACT.Copy)
                for j in range(DK):
                    s = j % 2
                    u = half * DK + j
                    act.wait_ge(b_done, u + 1)
                    if j < 2:
                        act.wait_ge(amp_lo_done, half * DK)
                    else:
                        act.wait_ge(amp_lo_done, u - 1)
                    act.activation(mr[:, s, :], acc_b[s][:, :], ACT.Copy).then_inc(b_out, 1)
                    act.wait_ge(c_done, u + 1)
                    act.activation(mi[:, s, :], acc_c[s][:, :], ACT.Square).then_inc(mi_done, 1)
                    act.wait_ge(mr_done, u + 1)
                    act.activation(mr[:, s, :], mr[:, s, :], ACT.Square).then_inc(mr_squared, 1)
                    act.wait_ge(mag_summed, u + 1)
                    act.activation(mr[:, s, :], mr[:, s, :], ACT.Sqrt).then_inc(amp_done, 1)
                    act.wait_ge(amp_done, u + 1)
                    act.wait_ge(row_done, half * 2 * TPH)
                    act.activation(amp_hi[:, j, :], mr[:, s, :], ACT.Copy).then_inc(amp_hi_done, 1)
                for j in range(DK):
                    i = 2 * DK + j
                    act.wait_ge(turned, half * TURNS + (i + 1))
                    act.activation(turn[i % 2][:, :], turn[i % 2][:, :], ACT.Gelu, scale=post_cols[:, 0, j:j + 1],
                                   bias=post_cols[:, 1, j:j + 1]).then_inc(gelu_done, 1)
                    act.wait_ge(gelu_done, half * DK + (j + 1))
                    act.activation(z_hi[:, j, :], turn[i % 2][:, :], ACT.Copy).then_inc(hi_done, 1)
                for j in range(DK):
                    turn_high(half, 3 * DK + j, h_hi[:, j, :], ACT.Relu)
                for j in range(2):
                    act.wait_ge(h2_acc, half * 2 + (j + 1))
                    act.activation(h2[:, j, :], acc_b[j][:, :], ACT.Relu, bias=top2_cols[:, j:j + 1]
                                   ).then_inc(h2_done, 1)
                act.wait_ge(y_acc, half + 1)
                act.activation(y_row[:, bass.ds(half, 1), :].rearrange("p o f -> p (o f)"), acc_c[0][0:1, :], ACT.Copy
                               ).then_inc(y_out, 1)

        @block.gpsimd
        def _(pool):
            pool.memset(neg_half[:, :], -0.5).then_inc(half_set, 1)
            pool.wait_ge(half_set, 1)
            with pool.Fori(0, NHALF) as half:
                pool.wait_ge(eps_done, half + 1)
                pool.tensor_tensor(rstd[:, :], var_eps[:, :], neg_half[:, :], ALU.pow).then_inc(rstd_done, 1)

        @block.tensor
        def _(pe):
            def turn_tile(half, i, src):
                pe.wait_ge(lo_done, half * TURNS + (i + 1))
                for t in range(TPH):
                    mm = pe.transpose(turn[i % 2][:, t * P:(t + 1) * P], src(t), ident)
                mm.then_inc(turned, 1)

            def product(bank, terms, done):
                for i, (s_hi, s_lo, m_hi, m_lo) in enumerate(terms):
                    pe.matmul(bank, s_hi, m_hi, start=(i == 0), stop=False)
                    pe.matmul(bank, s_hi, m_lo, start=False, stop=False)
                    mm = pe.matmul(bank, s_lo, m_hi, start=False, stop=(i == len(terms) - 1))
                mm.then_inc(done, 1)

            with pe.Fori(0, NHALF) as half:
                pe.wait_ge(sup_in, half * (16 * TPH) + 16 * TPH)
                for i in range(2 * DK):
                    ri, k = i // DK, i % DK
                    turn_tile(half, i, lambda t: sup_row[:, t, ri, k * P:(k + 1) * P])
                pe.wait_ge(w_lo_done, NW)
                pe.wait_ge(lo_done, half * TURNS + (2 * DK + 2))

                def meas(w, r, j):
                    return [(meas_hi[:, w, k, j * P:(j + 1) * P], meas_lo[:, w, k, j * P:(j + 1) * P],
                             sup_hi[:, r, k, :], sup_lo[:, r, k, :]) for k in range(DK)]

                for j in range(DK):
                    s = j % 2
                    u = half * DK + j
                    pe.wait_ge(b_out, u - 1) if j >= 2 else pe.wait_ge(h2_done, half * 2)
                    product(acc_b[s][:, :], meas(1, 1, j), b_done)
                    pe.wait_ge(mr_done, u - 1) if j >= 2 else pe.wait_ge(row_out, half * 2 * TPH)
                    product(acc_a[s][:, :], meas(0, 0, j), a_done)
                    pe.wait_ge(mi_done, u - 1) if j >= 2 else pe.wait_ge(y_out, half)
                    product(acc_c[s][:, :], meas(1, 0, j) + meas(0, 1, j), c_done)

                pe.wait_ge(amp_lo_done, half * DK + DK)
                for t in range(TPH):
                    if t < 2:
                        pe.wait_ge(mr_done, half * DK + DK)
                    else:
                        pe.wait_ge(row_out, half * (2 * TPH) + (t - 1))
                    product(acc_a[t % 2][:, :], [(amp_hi[:, k, t * P:(t + 1) * P], amp_lo[:, k, t * P:(t + 1) * P],
                                                  post_hi[:, k, :], post_lo[:, k, :]) for k in range(DK)], row_done)
                pe.wait_ge(normed, half * TPH + TPH)
                for k in range(DK):
                    turn_tile(half, 2 * DK + k, lambda t: row[:, t, k * P:(k + 1) * P])
                pe.wait_ge(lo_done, half * TURNS + (3 * DK + 2))
                for t in range(TPH):
                    pe.wait_ge(row_out, half * (2 * TPH) + (TPH + max(t - 1, 0)))
                    product(acc_a[t % 2][:, :], [(z_hi[:, k, t * P:(t + 1) * P], z_lo[:, k, t * P:(t + 1) * P],
                                                  top1_hi[:, k, :], top1_lo[:, k, :]) for k in range(DK)], row_done)
                pe.wait_ge(row_out, half * (2 * TPH) + 2 * TPH)
                for k in range(DK):
                    turn_tile(half, 3 * DK + k, lambda t: row[:, t, k * P:(k + 1) * P])
                pe.wait_ge(lo_done, half * TURNS + (4 * DK + 2))
                for j in range(2):
                    if j == 0:
                        pe.wait_ge(b_out, half * DK + DK)
                    product(acc_b[j][:, :], [(top2_hi[:, k, j * P:(j + 1) * P], top2_lo[:, k, j * P:(j + 1) * P],
                                              h_hi[:, k, :], h_lo[:, k, :]) for k in range(DK)], h2_acc)
                pe.wait_ge(mi_done, half * DK + DK)
                pe.wait_ge(h2_done, half * 2 + 2)
                for j in range(2):
                    mm = pe.matmul(acc_c[0][0:1, :], top3_cols[:, j:j + 1], h2[:, j, :], start=(j == 0), stop=(j == 1))
                mm.then_inc(y_acc, 1)

        @block.vector
        def _(dve):
            dve.sem_inc(lo_done, 2)
            for i in range(NW):
                dve.wait_ge(w_hi_done, i + 1)
                dve.tensor_tensor(weights[i][2], raw(i), weights[i][1], ALU.subtract).then_inc(w_lo_done, 1)
            dve.wait_ge(cols_in, 64)
            with dve.Fori(0, NHALF) as half:
                def turn_low(i, hi, lo):
                    dve.wait_ge(hi_done, half * TURNS + (i + 1))
                    dve.tensor_tensor(lo, turn[i % 2][:, :], hi, ALU.subtract).then_inc(lo_done, 1)

                for i in range(2 * DK):
                    turn_low(i, sup_hi[:, i // DK, i % DK, :], sup_lo[:, i // DK, i % DK, :])
                for j in range(DK):
                    s = j % 2
                    u = half * DK + j
                    dve.wait_ge(b_out, u + 1)
                    dve.wait_ge(a_done, u + 1)
                    dve.tensor_tensor(mr[:, s, :], acc_a[s][:, :], mr[:, s, :], ALU.subtract).then_inc(mr_done, 1)
                    dve.wait_ge(mi_done, u + 1)
                    dve.wait_ge(mr_squared, u + 1)
                    dve.tensor_tensor(mr[:, s, :], mr[:, s, :], mi[:, s, :], ALU.add).then_inc(mag_summed, 1)
                    dve.wait_ge(amp_hi_done, u + 1)
                    dve.tensor_tensor(amp_lo[:, j, :], mr[:, s, :], amp_hi[:, j, :], ALU.subtract
                                      ).then_inc(amp_lo_done, 1)
                dve.wait_ge(turned, half * TURNS + 2 * DK)
                for t in range(TPH):
                    r = half * (2 * TPH) + t
                    dve.wait_ge(row_done, r + 1)
                    dve.tensor_tensor(row[:, t, :], acc_a[t % 2][:, :], post_b[:, :], ALU.add).then_inc(row_out, 1)
                    dve.wait_ge(row_out, r + 1)
                    dve.bn_stats(stats[:, t, :], row[:, t, :]).then_inc(stat_done, 1)
                wait_apart(dve, stat_done, half * TPH + TPH, passed)
                for t in range(TPH):
                    dve.bn_aggr(mv[:, t, :], stats[:, t, :]).then_inc(aggr_done, 1)
                dve.wait_ge(aggr_done, half * TPH + TPH)
                dve.tensor_scalar(var_eps[:, :], mv[:, :, 1], EPS, None, ALU.add).then_inc(eps_done, 1)
                dve.wait_ge(rstd_done, half + 1)
                for t in range(TPH):
                    dve.tensor_scalar(row[:, t, :], row[:, t, :], mv[:, t, 0:1], rstd[:, t:t + 1],
                                      ALU.subtract, ALU.mult).then_inc(normed, 1)
                for j in range(DK):
                    turn_low(2 * DK + j, z_hi[:, j, :], z_lo[:, j, :])
                dve.wait_ge(topx_in, half * 16 + 16)
                for t in range(TPH):
                    dve.wait_ge(row_done, half * (2 * TPH) + (TPH + t + 1))
                    dve.tensor_tensor(row[:, t, :], acc_a[t % 2][:, :], topx[:, t, :], ALU.add).then_inc(row_out, 1)
                for j in range(DK):
                    i = 3 * DK + j
                    wait_apart(dve, hi_done, half * TURNS + (i + 1), passed)
                    dve.scalar_tensor_tensor(out=h_lo[:, j, :], in0=turn[i % 2][:, :], scalar=0.0, in1=h_hi[:, j, :],
                                             op0=ALU.max, op1=ALU.subtract).then_inc(lo_done, 1)


def quantum_tower(nc, dram):
    with ExitStack() as ctx:
        ident = ctx.enter_context(nc.sbuf_tensor("ident", [P, P], F32))
        ones_set = ctx.enter_context(nc.semaphore("ones_set"))
        ident_set = ctx.enter_context(nc.semaphore("ident_set"))
        with nc.Block() as block:

            @block.gpsimd
            def _(pool):
                pool.memset(ident[:, :], 1.0).then_inc(ones_set, 1)
                pool.wait_ge(ones_set, 1)
                pool.affine_select(out=ident[:, :], in_=ident[:, :], pattern=[[-1, P]], compare_op=ALU.is_equal,
                                   fill=0.0, base=0, channel_multiplier=1).then_inc(ident_set, 1)
                pool.wait_ge(ident_set, 1)

        consts = {"ident": ident[:, :]}
        with ExitStack() as stage:
            encoder_stage(nc, stage, dram, consts)
        with ExitStack() as stage:
            attention_stage(nc, stage, dram, consts)
        with ExitStack() as stage:
            project_stage(nc, stage, dram)
        with ExitStack() as stage:
            interact_stage(nc, stage, dram)
        with ExitStack() as stage:
            measure_stage(nc, stage, dram, consts)


def layout(a):
    def k_major(w):
        return np.asarray(w).T

    def units(w):
        k, n = w.shape
        return w.reshape(k // (UNIT_K * P), UNIT_K, P, n // 512, 512).transpose(3, 0, 2, 1, 4)

    def cols(v):
        return np.asarray(v).reshape(-1, P).T

    pre = "L0_rec_"
    out = {}
    out["x_t"] = np.asarray(a["r_x"]).reshape(NHALF, HALF, KT, P).transpose(0, 3, 2, 1)
    w_top1 = np.asarray(a["W_top1"])
    out["enc_w"] = np.concatenate([
        units(w_top1[D:]), units(k_major(a[pre + "er_W1"])), units(k_major(a[pre + "ei_W1"])),
        units(k_major(a[pre + "er_W2"])), units(k_major(a[pre + "ei_W2"]))])
    out["enc_b1"] = np.concatenate([np.asarray(a[k]).reshape(-1, 512) for k in
                                    ("b_top1", pre + "er_b1", pre + "ei_b1")])
    out["ln_cols"] = np.stack([np.stack([cols(a[pre + e + "_g1"]), cols(a[pre + e + "_be1"])], 1)
                               for e in ("er", "ei")], 1)
    out["b2_cols"] = np.concatenate([cols(a[pre + "er_b2"]), cols(a[pre + "ei_b2"])], 1)
    def qkv(t):
        w = [k_major(a[pre + f"W{x}_{t}"]).reshape(DK, P, HP, P) for x in "qkv"]
        return np.stack(w, 3).reshape(DK, P, HP * 3 * P)

    out["qkv_w"] = np.stack([qkv("r"), qkv("i")])
    out["qk_bias"] = np.stack([np.stack([np.asarray(a[pre + f"b{x}_{t}"]).reshape(HP, P) for x in "qk"], 1)
                               .reshape(HP, 2 * P) for t in "ri"])
    out["v_cols"] = np.stack([cols(a[pre + "bv_r"]), cols(a[pre + "bv_i"])], 1)

    def k_tiles(w):
        return w.reshape(-1, P, w.shape[-1]).transpose(1, 0, 2)

    out["wo_w"] = np.stack([k_tiles(k_major(a[pre + f"Wo_{t}"])) for t in "ri"])
    out["bo_cols"] = np.stack([cols(a[pre + "bo_r"]), cols(a[pre + "bo_i"])], 1)
    out["int_w"] = np.stack([k_tiles(k_major(np.asarray(a[pre + f"int_W{t}"])[n])) for t in "ri" for n in range(N)])
    out["ids"] = np.asarray(a["ids"]).reshape(TILES, P, N).transpose(1, 0, 2)
    for f in range(N):
        out[f"tbl_{f}"] = np.asarray(a[f"tbl_{f}"])
    out["meas_w"] = np.stack([k_tiles(k_major(a[pre + f"meas_M{t}"])) for t in "ri"])
    out["post_w"] = k_tiles(k_major(a[pre + "post_W"]))
    out["post_row"] = np.asarray(a[pre + "post_b"]).reshape(1, D)
    out["post_cols"] = np.stack([cols(a[pre + "post_g"]), cols(a[pre + "post_be"])], 1)
    out["top1_w"] = k_tiles(w_top1[:D])
    out["top2_w"] = k_tiles(np.asarray(a["W_top2"]))
    out["top2_cols"] = cols(a["b_top2"])
    out["top3_cols"] = cols(np.asarray(a["W_top3"])[:, 0])
    return {k: np.ascontiguousarray(v) for k, v in out.items()}


def scratch_shapes():
    return {"s_t": (2, TILES, P, N * DK, P),
            "top_x": (NHALF, P, TPH, D),
            "o_t": (2, TILES * HP, P, N * P),
            "a_t": (2, TILES, P, N, DK * P),
            "sup_d": (TILES, P, 2, D)}


def kernel(**inputs):
    import concourse.bacc as bacc
    from concourse.bass_utils import run_bass_kernel_spmd

    nc = bacc.Bacc("TRN2", target_bir_lowering=False, num_devices=1, dynamic_dma_scratch_size=2048)
    arrays = layout(inputs)
    dram = {}
    for name, a in arrays.items():
        dram[name] = nc.dram_tensor(name, a.shape, mybir.dt.from_np(a.dtype), kind="ExternalInput").ap()
    for name, shape in scratch_shapes().items():
        dram[name] = nc.dram_tensor(name, shape, F32, kind="Internal").ap()
    dram["y"] = nc.dram_tensor("y", (B, 1), F32, kind="ExternalOutput").ap()
    quantum_tower(nc, dram)
    return run_bass_kernel_spmd(nc, [arrays], core_ids=[0]).results[0]["y"]
```

```python
from contextlib import ExitStack

import numpy as np

import concourse.bass as bass
from concourse import mybir

F32 = mybir.dt.float32
F32R = mybir.dt.float32r
I32 = mybir.dt.int32
ALU = mybir.AluOpType
ACT = mybir.ActivationFunctionType
AX = mybir.AxisListType

P = 128
B = 1024
IN = 2048
HID = 2048
D = 512
N = 4
HEADS = 8
HD = D // HEADS
HALF = 512
NHALF = B // HALF
TPH = HALF // P
TILES = B // P
KT = IN // P
DK = D // P
UNIT_K = 2
UNITS = KT // UNIT_K
CHUNKS = 17
HP = HEADS // 2
EPS = 1e-5
TINY = 1e-37
ZERO_ABOVE = 3e18


def wait_apart(eng, sem, value, passed):
    eng.wait_ge(sem, value)
    eng.sem_inc(passed, 1)


def encoder_stage(nc, ctx, dram, consts):
    def sb(name, shape, dt=F32):
        return ctx.enter_context(nc.sbuf_tensor(name, shape, dt))

    def sem(name):
        return ctx.enter_context(nc.semaphore(name))

    ident = consts["ident"]
    a_hi, a_lo = sb("a_hi", [P, KT, HALF], F32R), sb("a_lo", [P, KT, HALF], F32R)
    b_hi, b_lo = sb("b_hi", [P, KT, HALF], F32R), sb("b_lo", [P, KT, HALF], F32R)
    hid = [sb("hid_r", [P, TPH, HID]), sb("hid_i", [P, TPH, HID])]
    raw = sb("raw", [P, 2, UNIT_K, 512])
    w_hi, w_lo = sb("w_hi", [P, 2, UNIT_K, 512], F32R), sb("w_lo", [P, 2, UNIT_K, 512], F32R)
    bias1 = sb("bias1", [P, 512])
    normed = sb("normed", [P, TPH, P])
    stats = sb("stats", [P, TPH, 4, 6])
    mv = sb("mv", [P, TPH, 2])
    var_eps = sb("var_eps", [P, TPH])
    rstd = sb("rstd", [P, TPH])
    neg_half = sb("neg_half", [P, TPH])
    ln_cols = sb("ln_cols_sb", [P, 2, 2, KT])
    b2_cols = sb("b2_cols_sb", [P, 2 * N * DK])
    acc = [ctx.enter_context(nc.psum_tensor(f"acc{t}", [P, 512], F32)) for t in range(4)]
    turn = [ctx.enter_context(nc.psum_tensor(f"turn{t}", [P, 512], F32)) for t in range(2)]

    raw_full = [sem("raw_full0"), sem("raw_full1")]
    raw_free = sem("raw_free")
    x_hi_done, x_lo_done = sem("x_hi_done"), sem("x_lo_done")
    x_in = [sem(f"x_in{q}") for q in range(4)]
    w_hi_done = sem("w_hi_done")
    w_free = sem("w_free")
    acc_done = sem("acc_done")
    acc_free = sem("acc_free")
    bias_in = sem("bias_in")
    params_in = sem("params_in")
    stat_done = sem("stat_done")
    aggr_done = sem("aggr_done")
    eps_done = sem("eps_done")
    rstd_done = sem("rstd_done")
    half_set = sem("half_set")
    norm_done = sem("norm_done")
    turned = sem("turned")
    gelu_done = sem("gelu_done")
    h_hi_done = sem("h_hi_done")
    turn_free = sem("turn_free")
    top_out = sem("top_out")
    passed = consts["passed"]
    s_out = [sem("s_out_r"), sem("s_out_i")]

    TOP, L1, L2 = range(3)
    phases = [(0, None, TOP, None), (1, 0, L1, None), (5, 1, L1, 0), (9, 0, L2, 1), (13, 1, L2, None)]
    S_OUT = 16 * N * TPH
    XU = UNITS
    SU = UNITS * CHUNKS

    def load_x(sp, half):
        for q in range(4):
            sp.dma_start(hid[0][:, q, :], dram["x_t"][half, :, q * 4:(q + 1) * 4, :]).then_inc(x_in[q], 16)

    def store_s(sp, enc, half, n):
        for t in range(TPH):
            sp.dma_start(dram["s_t"][enc, bass.ds(half * TPH + t, 1), :, bass.ds(n * DK, DK), :]
                         .rearrange("o p k b -> (o p) k b"),
                         hid[enc][:, bass.ds(n, 1), :].rearrange("p o (k t b) -> p (o k) t b", k=DK, t=TPH)[:, :, t, :]
                         ).then_inc(s_out[enc], 16)

    def x_unit(u):
        return hid[0][:, u // 2, (u % 2) * UNIT_K * 512:(u % 2 + 1) * UNIT_K * 512]

    def loop(eng, count, body):
        body(0, True)
        if count > 1:
            with eng.Fori(1, count) as c:
                body(c, False)

    with nc.Block() as block:

        @block.sync
        def _(sp):
            sp.dma_start(ln_cols[:, :, :, :], dram["ln_cols"]).then_inc(params_in, 16)
            sp.dma_start(b2_cols[:, :], dram["b2_cols"]).then_inc(params_in, 16)
            load_x(sp, 0)
            with sp.Fori(0, NHALF) as half:
                for first, enc, kind, _ in phases:
                    def chunk(c, peeled):
                        ci = c + first
                        for u in range(UNITS):
                            sp.wait_ge(raw_free, half * SU + ci * UNITS + u + 1)
                            sp.dma_start(raw[:, u % 2], dram["enc_w"][ci, u]).then_inc(raw_full[u % 2], 16)
                            if u == 4 and kind != L2:
                                sp.wait_ge(acc_free, half * (4 * CHUNKS) + ci * 4 + 4)
                                sp.dma_start(bias1[:, :], dram["enc_b1"][bass.ds(ci, 1), :].to_broadcast([P, 512])
                                             ).then_inc(bias_in, 16)
                            if u == 5 and kind == L1 and enc == 0 and peeled:
                                sp.dma_start(dram["top_x"][half], hid[1][:, :, 0:512]).then_inc(top_out, 16)
                            if u == 5 and kind == L2 and not (peeled and enc == 0):
                                pe_, pc = (enc, c - 1) if not peeled else (0, 3)
                                sp.wait_ge(acc_free, half * (4 * CHUNKS) + ci * 4 + 4)
                                store_s(sp, pe_, half, pc)
                            if u == 6 and kind == L2 and enc == 1 and peeled:
                                with sp.If(half < NHALF - 1):
                                    sp.wait_ge(s_out[0], half * S_OUT + S_OUT)
                                    load_x(sp, NHALF - 1)
                    loop(sp, 1 if kind == TOP else 4, chunk)
                sp.wait_ge(acc_free, half * (4 * CHUNKS) + 4 * CHUNKS + 4)
                store_s(sp, 1, half, 3)
            sp.wait_ge(s_out[0], S_OUT * NHALF)
            sp.wait_ge(s_out[1], S_OUT * NHALF)
            sp.wait_ge(top_out, 16 * NHALF)

        @block.scalar
        def _(act):
            act.wait_ge(params_in, 32)
            with act.Fori(0, NHALF) as half:
                for u in range(XU):
                    act.wait_ge(x_in[u // 2], half * 16 + 16)
                    if u == 0:
                        act.wait_ge(acc_done, half * (4 * CHUNKS))
                    act.activation(a_hi[:, u * UNIT_K:(u + 1) * UNIT_K, :], x_unit(u), ACT.Copy
                                   ).then_inc(x_hi_done, 1)
                for first, enc, kind, turn_enc in phases:
                    def chunk(c, peeled):
                        ci = c + first
                        for u in range(UNITS):
                            act.wait_ge(raw_full[u % 2],
                                        half * (8 * SU) + ci * (8 * UNITS) + 16 * (u // 2) + 16)
                            if u == 1:
                                act.wait_ge(acc_done, half * (4 * CHUNKS) + ci * 4)
                            else:
                                act.wait_ge(w_free, half * (CHUNKS * (UNITS - 1)) + ci * (UNITS - 1) + max(u - 1, 0))
                            act.activation(w_hi[:, u % 2], raw[:, u % 2], ACT.Copy).then_inc(w_hi_done, 1)
                            if turn_enc is not None and u >= 4:
                                jj = u - 4
                                h_hi = b_hi if turn_enc == 0 else a_hi
                                g = half * (2 * KT) + c * 4 + (turn_enc * KT + jj)
                                kt = c * 4 + jj
                                act.wait_ge(turned, g + 1)
                                act.activation(turn[jj % 2][:, :], turn[jj % 2][:, :], ACT.Gelu,
                                               scale=ln_cols[:, turn_enc, 0, bass.ds(kt, 1)],
                                               bias=ln_cols[:, turn_enc, 1, bass.ds(kt, 1)]).then_inc(gelu_done, 1)
                                act.wait_ge(gelu_done, g + 1)
                                act.activation(h_hi[:, bass.ds(kt, 1), :], turn[jj % 2][:, :], ACT.Copy
                                               ).then_inc(h_hi_done, 1)
                    loop(act, 1 if kind == TOP else 4, chunk)

        @block.gpsimd
        def _(pool):
            pool.sem_inc(raw_free, 2)
            pool.memset(neg_half[:, :], -0.5).then_inc(half_set, 1)
            pool.wait_ge(half_set, 1)
            with pool.Fori(0, NHALF) as half:
                for first, enc, kind, turn_enc in phases:
                    def chunk(c, peeled):
                        ci = c + first
                        for u in range(UNITS):
                            if u == 2 and peeled and turn_enc is not None:
                                pool.wait_ge(eps_done, half * 2 + turn_enc + 1)
                                pool.tensor_tensor(rstd[:, :], var_eps[:, :], neg_half[:, :], ALU.pow
                                                   ).then_inc(rstd_done, 1)
                            pool.wait_ge(w_hi_done, half * (CHUNKS * UNITS) + ci * UNITS + u + 1)
                            pool.tensor_tensor(w_lo[:, u % 2], raw[:, u % 2], w_hi[:, u % 2], ALU.subtract
                                               ).then_inc(raw_free, 1)
                    loop(pool, 1 if kind == TOP else 4, chunk)

        @block.tensor
        def _(pe):
            with pe.Fori(0, NHALF) as half:
                for first, enc, kind, turn_enc in phases:
                    def chunk(c):
                        ci = c + first
                        for u in range(UNITS):
                            pe.wait_ge(raw_free, half * SU + ci * UNITS + (2 + u + 1))
                            if kind == TOP:
                                pe.wait_ge(x_lo_done, half * XU + u + 1)
                            if kind == L2:
                                pe.wait_ge(turn_free, half * (2 * KT) + (2 + enc * KT + UNIT_K * (u + 1)))
                            for kk in range(UNIT_K):
                                k = u * UNIT_K + kk
                                for t in range(4):
                                    if k == 0:
                                        pe.wait_ge(acc_free, half * (4 * CHUNKS) + ci * 4 + t + 1)
                                    if kind == L2:
                                        m_hi, m_lo = (b_hi, b_lo) if enc == 0 else (a_hi, a_lo)
                                        s_hi = w_hi[:, u % 2, kk, t * P:(t + 1) * P]
                                        s_lo = w_lo[:, u % 2, kk, t * P:(t + 1) * P]
                                        m_hi, m_lo = m_hi[:, k, :], m_lo[:, k, :]
                                    else:
                                        s_hi = a_hi[:, k, t * P:(t + 1) * P]
                                        s_lo = a_lo[:, k, t * P:(t + 1) * P]
                                        m_hi, m_lo = w_hi[:, u % 2, kk, :], w_lo[:, u % 2, kk, :]
                                    pe.matmul(acc[t][:, :], s_hi, m_hi, start=(k == 0), stop=False)
                                    pe.matmul(acc[t][:, :], s_hi, m_lo, start=False, stop=False)
                                    mm = pe.matmul(acc[t][:, :], s_lo, m_hi, start=False, stop=(k == KT - 1))
                                    if k == KT - 1:
                                        mm.then_inc(acc_done, 1)
                            if u < UNITS - 1:
                                mm.then_inc(w_free, 1)
                            if turn_enc is not None and 2 <= u < 6:
                                jj = u - 2
                                g = half * (2 * KT) + c * 4 + (turn_enc * KT + jj)
                                pe.wait_ge(norm_done, g * 4 + 4)
                                pe.wait_ge(turn_free, g + 1)
                                for t in range(TPH):
                                    mm = pe.transpose(turn[jj % 2][:, t * P:(t + 1) * P], normed[:, t, :], ident)
                                mm.then_inc(turned, 1)
                    if kind == TOP:
                        chunk(0)
                    else:
                        with pe.Fori(0, 4) as c:
                            chunk(c)

        @block.vector
        def _(dve):
            dve.sem_inc(acc_free, 4)
            dve.sem_inc(turn_free, 2)
            dve.wait_ge(params_in, 32)
            with dve.Fori(0, NHALF) as half:
                for u in range(XU):
                    dve.wait_ge(x_hi_done, half * XU + u + 1)
                    dve.tensor_tensor(a_lo[:, u * UNIT_K:(u + 1) * UNIT_K, :], x_unit(u),
                                      a_hi[:, u * UNIT_K:(u + 1) * UNIT_K, :], ALU.subtract).then_inc(x_lo_done, 1)
                for first, enc, kind, turn_enc in phases:
                    def norm(c, jj):
                        g = half * (2 * KT) + c * 4 + (turn_enc * KT + jj)
                        dve.wait_ge(turned, g)
                        for t in range(TPH):
                            dve.tensor_scalar(normed[:, t, :], hid[turn_enc][:, t, bass.ds(c * 512 + jj * P, P)],
                                              mv[:, t, 0:1], rstd[:, t:t + 1], ALU.subtract, ALU.mult
                                              ).then_inc(norm_done, 1)

                    def low(c, jj):
                        h_hi, h_lo = (b_hi, b_lo) if turn_enc == 0 else (a_hi, a_lo)
                        g = half * (2 * KT) + c * 4 + (turn_enc * KT + jj)
                        kt = c * 4 + jj
                        dve.wait_ge(h_hi_done, g + 1)
                        dve.tensor_tensor(h_lo[:, bass.ds(kt, 1), :], turn[jj % 2][:, :],
                                          h_hi[:, bass.ds(kt, 1), :], ALU.subtract).then_inc(turn_free, 1)

                    def chunk(c, peeled):
                        ci = c + first
                        done = half * (4 * CHUNKS) + ci * 4
                        if turn_enc is not None:
                            norm(c, 0)
                            for jj in range(1, 4):
                                norm(c, jj)
                                low(c, jj - 1)
                            low(c, 3)
                        if kind != L2:
                            dve.wait_ge(bias_in, (half * 9 + ci) * 16 + 16)
                        if kind == TOP:
                            dve.wait_ge(s_out[1], half * S_OUT)
                        if kind == L1 and peeled:
                            if enc == 1:
                                dve.wait_ge(top_out, half * 16 + 16)
                            else:
                                dve.wait_ge(s_out[0], half * S_OUT)
                        for t in range(4):
                            dve.wait_ge(acc_done, done + t + 1)
                            if kind == TOP:
                                dve.tensor_tensor(hid[1][:, t, 0:512], acc[t][:, :], bias1[:, :], ALU.add
                                                  ).then_inc(acc_free, 1)
                            elif kind == L1:
                                h = hid[enc][:, t, bass.ds(c * 512, 512)]
                                dve.tensor_tensor(h, acc[t][:, :], bias1[:, :], ALU.add).then_inc(acc_free, 1)
                                dve.wait_ge(acc_free, done + (4 + t + 1))
                                dve.bn_stats(stats[:, t, bass.ds(c, 1), :], h).then_inc(stat_done, 1)
                            else:
                                dve.tensor_scalar(hid[enc][:, bass.ds(c, 1), t * 512:(t + 1) * 512], acc[t][:, :],
                                                  b2_cols[:, bass.ds(c * DK + (enc * N * DK + t), 1)], None, ALU.add
                                                  ).then_inc(acc_free, 1)
                    if kind == TOP:
                        chunk(0, True)
                    elif kind == L1:
                        loop(dve, 4, chunk)
                        wait_apart(dve, stat_done, half * 32 + (enc * 16 + 16), passed)
                        for t in range(TPH):
                            dve.bn_aggr(mv[:, t, :], stats[:, t, :, :].rearrange("p c s -> p (c s)")
                                        ).then_inc(aggr_done, 1)
                        dve.wait_ge(aggr_done, half * 8 + (enc * 4 + 4))
                        dve.tensor_scalar(var_eps[:, :], mv[:, :, 1], EPS, None, ALU.add).then_inc(eps_done, 1)
                        dve.wait_ge(rstd_done, half * 2 + enc + 1)
                    else:
                        loop(dve, 4, chunk)


def attention_stage(nc, ctx, dram, consts):
    def sb(name, shape, dt=F32):
        return ctx.enter_context(nc.sbuf_tensor(name, shape, dt))

    def sem(name):
        return ctx.enter_context(nc.semaphore(name))

    ident = consts["ident"]
    QKV = 3 * P
    STEPS = TILES * HP
    PAIRS = N * N * 2
    w_hi, w_lo = sb("qkv_hi", [P, 2, DK, HP * QKV], F32R), sb("qkv_lo", [P, 2, DK, HP * QKV], F32R)
    qk_bias = sb("qk_bias_sb", [P, 2, HP, 2 * P])
    v_cols = sb("v_cols_sb", [P, 2, HP])
    s_raw = sb("s_raw", [P, N * DK, P])
    s_hi, s_lo = sb("s_hi", [P, 2, N * DK, P], F32R), sb("s_lo", [P, 2, N * DK, P], F32R)
    qk = sb("qk", [P, 2, 2, 2, N, P])
    vals = sb("vals", [P, HP, 2, N, P])
    prod = sb("prod", [P, 4, 4 * 512])
    o_row = sb("o_row", [P, 2, 2, N, P])
    o_col = sb("o_col", [P, 2, N * P])
    sums = sb("sums", [P, 4, PAIRS])
    soft = sb("soft", [P, 2, PAIRS])
    top = sb("top", [P, 2, N * 2])
    den = sb("den", [P, 2, N * 2])
    rden = sb("rden", [P, 2, N * 2])
    mag_eps = sb("mag_eps", [P, 1])
    acc = [[ctx.enter_context(nc.psum_tensor(f"qkv{ri}{n}", [P, 512], F32)) for n in range(N)] for ri in range(2)]

    SCALE2 = 1.0 / HD

    w_in = [sem(f"qkv_in{i}") for i in range(4)]
    w_hi_done = sem("qkv_hi_done")
    w_lo_done = sem("qkv_lo_done")
    bias_in = sem("qk_bias_in")
    eps_set = sem("mag_eps_set")
    s_in = [sem("s_in_r"), sem("s_in_i")]
    s_hi_done = [sem("s_hi_r"), sem("s_hi_i")]
    s_lo_done = [sem("s_lo_r"), sem("s_lo_i")]
    acc_done = sem("qkv_done")
    qk_out = sem("qk_out")
    v_out = sem("v_out")
    qkp_done = sem("qkp_done")
    qkp_own = sem("qkp_own")
    pv_done = [sem("pv_done_r"), sem("pv_done_i")]
    qk_red = sem("qk_red")
    pv_red = [sem("pv_red_r"), sem("pv_red_i")]
    chain = sem("chain")
    mag_done, exp_done = sem("mag_done"), sem("exp_done")
    o_out = [sem("o_out_r"), sem("o_out_i")]

    SCORES = ((0, 0, 0, 0), (1, 0, 1, 2), (1, 1, 3, 1), (0, 1, 3, 3))
    SUM_ORDER = (3, 0, 1, 2)

    def summed(u, c):
        return u * 4 + (SUM_ORDER.index(c) + 1)


    def score_product(eng, s, a, b, slot, n):
        return eng.tensor_tensor(prod[:, slot, n * 512:(n + 1) * 512].rearrange("p (m f) -> p m f", m=N),
                                 qk[:, s, a, 0, n:n + 1, :].broadcast_to([P, N, P]), qk[:, s, b, 1, :, :], ALU.mult)

    def raw_w(i):
        return prod[:, :, :].rearrange("p s f -> p (s f)")[:, (i % 4) * HP * QKV:(i % 4 + 1) * HP * QKV]

    def tiles(eng, body):
        body(0)
        with eng.Fori(1, TILES) as tile:
            body(tile)

    def exists(tile, hp, lag):
        return not (isinstance(tile, int) and tile * HP + hp < lag)

    with nc.Block() as block:

        @block.sync
        def _(sp):
            sp.dma_start(qk_bias[:, :, :, :], dram["qk_bias"].partition_broadcast(P)).then_inc(bias_in, 16)
            sp.dma_start(v_cols[:, :, :], dram["v_cols"]).then_inc(bias_in, 16)

            for ri in range(2):
                if ri == 1:
                    sp.wait_ge(s_lo_done[0], 1)
                sp.dma_start(s_raw[:, :, :], dram["s_t"][ri, 0]).then_inc(s_in[ri], 16)
                for k in range(DK):
                    i = ri * DK + k
                    if i >= 4:
                        sp.wait_ge(w_lo_done, i - 3)
                    sp.dma_start(raw_w(i), dram["qkv_w"][ri, k]).then_inc(w_in[i % 4], 16)

            def col_store(v):
                for ri in range(2):
                    sp.wait_ge(v_out, v * 8 + (32 + ri * 4 + 4))
                    sp.dma_start(dram["o_t"][ri, bass.ds(v, 1)].rearrange("o p f -> (o p) f"), o_col[:, ri, :]
                                 ).then_inc(o_out[ri], 16)

            def next_s(tile, ri):
                if ri == 0:
                    sp.wait_ge(s_lo_done[1], tile)
                else:
                    sp.wait_ge(s_lo_done[0], tile + 1)
                sp.dma_start(s_raw[:, :, :], dram["s_t"][ri, bass.ds(tile, 1)].rearrange("o p k b -> (o p) k b")
                             ).then_inc(s_in[ri], 16)

            next_s(1, 0)
            col_store(0)
            next_s(1, 1)
            with sp.Fori(2, TILES) as tile:
                next_s(tile, 0)
                for hp in range(HP):
                    col_store(tile * HP + (hp + 1 - 2 * HP))
                next_s(tile, 1)
            for v in range((TILES - 2) * HP + 1, STEPS):
                col_store(v)
            for ri in range(2):
                sp.wait_ge(o_out[ri], 16 * STEPS)

        @block.scalar
        def _(act):
            for i in range(2 * DK):
                if i == 0:
                    act.wait_ge(s_in[0], 16)
                    act.activation(s_hi[:, 0], s_raw[:, :, :], ACT.Copy).then_inc(s_hi_done[0], 1)
                if i == DK:
                    act.wait_ge(s_in[1], 16)
                    act.activation(s_hi[:, 1], s_raw[:, :, :], ACT.Copy).then_inc(s_hi_done[1], 1)
                act.wait_ge(w_in[i % 4], 16 * (i // 4) + 16)
                act.activation(w_hi[:, i // DK, i % DK, :], raw_w(i), ACT.Copy).then_inc(w_hi_done, 1)
            act.wait_ge(bias_in, 32)
            act.wait_ge(eps_set, 1)

            def next_s_hi(tile, ri, u):
                act.wait_ge(s_in[ri], 16 * tile + 32)
                act.wait_ge(acc_done, u * 8 + (ri * 4 + 4))
                act.activation(s_hi[:, ri], s_raw[:, :, :], ACT.Copy).then_inc(s_hi_done[ri], 1)

            def guarded(tile, fn):
                if isinstance(tile, int):
                    fn()
                else:
                    with act.If(tile < TILES - 1):
                        fn()

            def root(v, s):
                act.wait_ge(chain, v * 9 + 4)
                act.activation(soft[:, s, :], soft[:, s, :], ACT.Sqrt, scale=SCALE2, bias=mag_eps[:, 0:1]
                               ).then_inc(mag_done, 1)

            def expo(v, s):
                act.wait_ge(chain, v * 9 + 6)
                act.activation(soft[:, s, :], soft[:, s, :], ACT.Exp).then_inc(exp_done, 1)

            def weighted_imag(v, hp, ns):
                if ns[0] == 0:
                    act.wait_ge(chain, v * 9 + 9)
                    act.wait_ge(v_out, v * 8 + 16)
                    if not (isinstance(v, int) and v == 0):
                        act.wait_ge(pv_red[1], v)
                for n in ns:
                    for m in range(N):
                        for h in range(2):
                            at = m * P + h * HD
                            w = n * 2 * N + m * 2 + h
                            ins = act.activation(prod[:, 2, n * 512 + at:n * 512 + at + HD],
                                                 vals[:, hp, 1, m, h * HD:(h + 1) * HD], ACT.Copy,
                                                 scale=soft[:, hp % 2, w:w + 1])
                    ins.then_inc(pv_done[1], 1)

            def v_read(u, hp, ri, wait):
                if wait:
                    act.wait_ge(pv_done[ri], u * 4 - 12)
                for n in range(N):
                    act.wait_ge(qk_out, u * 8 + (ri * 4 + n + 5))
                    ins = act.activation(vals[:, hp, ri, n, :], acc[ri][n][:, 2 * P:3 * P], ACT.Copy)
                    if isinstance(u, int) and u < 3:
                        ins.then_inc(v_out, 1)
                    else:
                        if n == 0:
                            act.wait_ge(o_out[ri], (u - 3) * 16)
                        col_read(ri, n, (hp - 3) % HP)

            def col_read(ri, n, hp):
                act.activation(o_col[:, ri, n * P:(n + 1) * P], acc[ri][n][:, QKV:QKV + P], ACT.Identity,
                               bias=v_cols[:, ri, hp:hp + 1]).then_inc(v_out, 1)

            def tile_body(tile):
                for hp in range(HP):
                    u = tile * HP + hp
                    if hp == HP - 1:
                        guarded(tile, lambda: next_s_hi(tile, 0, u))
                    if exists(tile, hp, 1):
                        root(tile * HP + (hp - 1), 1 - hp % 2)
                    v_read(u, hp, 1, exists(tile, hp, HP))
                    if exists(tile, hp, 1):
                        expo(tile * HP + (hp - 1), 1 - hp % 2)
                        weighted_imag(tile * HP + (hp - 1), (hp - 1) % HP, (0, 1))
                    if hp == HP - 1:
                        guarded(tile, lambda: v_read(tile * HP + HP, 0, 0, True))
                    else:
                        v_read(tile * HP + (hp + 1), hp + 1, 0, exists(tile, hp + 1, HP))
                    if hp == HP - 1:
                        guarded(tile, lambda: next_s_hi(tile, 1, u))
                    if exists(tile, hp, 1):
                        weighted_imag(tile * HP + (hp - 1), (hp - 1) % HP, (2, 3))
            v_read(0, 0, 0, False)
            tiles(act, tile_body)
            root(STEPS - 1, 1)
            expo(STEPS - 1, 1)
            weighted_imag(STEPS - 1, HP - 1, range(N))
            for v in range(STEPS - 3, STEPS):
                for ri in range(2):
                    act.wait_ge(o_out[ri], v * 16)
                    for n in range(N):
                        act.wait_ge(acc_done, (v + 3) * 8 + (ri * 4 + n + 1))
                        col_read(ri, n, v % HP)

        @block.tensor
        def _(pe):
            pe.wait_ge(w_lo_done, 1)

            def turn_out(v, s, ri, n):
                if n == 0:
                    pe.wait_ge(pv_red[ri], v + 1)
                return pe.transpose(acc[ri][n][:, QKV:QKV + P], o_row[:, s, ri, n, :], ident)

            def tile_body(tile):
                for hp in range(HP):
                    u = tile * HP + hp
                    for ri in range(2):
                        if hp == 0:
                            pe.wait_ge(s_lo_done[ri], tile + 1)
                        for n in range(N):
                            pe.wait_ge(v_out, u * 8 + (ri * 4 + n + 1))
                            for k in range(DK):
                                if isinstance(tile, int) and hp == 0 and n == 0:
                                    pe.wait_ge(w_lo_done, ri * DK + k + 1)
                                m_hi = w_hi[:, ri, k, hp * QKV:(hp + 1) * QKV]
                                m_lo = w_lo[:, ri, k, hp * QKV:(hp + 1) * QKV]
                                t_hi, t_lo = s_hi[:, ri, n * DK + k, :], s_lo[:, ri, n * DK + k, :]
                                pe.matmul(acc[ri][n][:, 0:QKV], t_hi, m_hi, start=(k == 0), stop=False)
                                pe.matmul(acc[ri][n][:, 0:QKV], t_hi, m_lo, start=False, stop=False)
                                mm = pe.matmul(acc[ri][n][:, 0:QKV], t_lo, m_hi, start=False, stop=(k == DK - 1))
                            if exists(tile, hp, 3):
                                mm = turn_out(tile * HP + (hp - 3), (hp - 3) % 2, ri, n)
                            mm.then_inc(acc_done, 1)
            tiles(pe, tile_body)
            for v in range(STEPS - 3, STEPS):
                for ri in range(2):
                    for n in range(N):
                        pe.wait_ge(v_out, (v + 3) * 8 + (ri * 4 + n + 1))
                        turn_out(v, v % 2, ri, n).then_inc(acc_done, 1)

        @block.gpsimd
        def _(pool):
            pool.memset(mag_eps[:, :], 1e-8 * SCALE2).then_inc(eps_set, 1)
            pool.wait_ge(w_lo_done, 2 * DK)

            def scores(u, s, c, wait):
                a, b, slot, _ = SCORES[c]
                if c == 0:
                    pool.wait_ge(qk_out, u * 8 + 8)
                    if wait:
                        pool.wait_ge(qk_red, summed(u - 1, 0))
                elif c == 1:
                    pool.wait_ge(qk_out, u * 8 + 12)
                    if wait:
                        pool.wait_ge(pv_red[0], u - 1)
                else:
                    pool.wait_ge(qk_red, summed(u, 3))
                for n in range(N):
                    score_product(pool, s, a, b, slot, n).then_inc(qkp_done, 1)

            def weighted(v, hp, last):
                pool.wait_ge(chain, v * 9 + 9)
                if last:
                    pool.wait_ge(pv_red[0], v)
                else:
                    pool.wait_ge(qk_red, summed(v + 1, 1))
                pool.wait_ge(v_out, v * 8 + 12)
                for n in range(N):
                    pool.tensor_tensor(
                        prod[:, 1, n * 512:(n + 1) * 512].rearrange("p (g f) -> p g f", f=HD),
                        soft[:, hp % 2, n * 8:(n + 1) * 8].unsqueeze(2).broadcast_to([P, 8, HD]),
                        vals[:, hp, 0, :, :].rearrange("p m (h f) -> p (m h) f", f=HD), ALU.mult
                        ).then_inc(pv_done[0], 1)

            def next_s_lo(tile):
                pool.wait_ge(s_hi_done[1], tile + 2)
                pool.tensor_tensor(s_lo[:, 1], s_raw[:, :, :], s_hi[:, 1], ALU.subtract).then_inc(s_lo_done[1], 1)

            def tile_body(tile):
                for hp in range(HP):
                    u = tile * HP + hp
                    scores(u, hp % 2, 0, exists(tile, hp, 1))
                    scores(u, hp % 2, 1, exists(tile, hp, 2))
                    scores(u, hp % 2, 2, True)
                    if hp == HP - 1:
                        if isinstance(tile, int):
                            next_s_lo(tile)
                        else:
                            with pool.If(tile < TILES - 1):
                                next_s_lo(tile)
                    if exists(tile, hp, 1):
                        weighted(tile * HP + (hp - 1), (hp - 1) % HP, False)
            tiles(pool, tile_body)
            weighted(STEPS - 1, HP - 1, True)

        @block.vector
        def _(dve):
            dve.sem_inc(qk_out, 4)
            dve.sem_inc(v_out, 8)
            for i in range(2 * DK):
                if i % DK == 0:
                    ri = i // DK
                    dve.wait_ge(s_hi_done[ri], 1)
                    dve.tensor_tensor(s_lo[:, ri], s_raw[:, :, :], s_hi[:, ri], ALU.subtract
                                      ).then_inc(s_lo_done[ri], 1)
                dve.wait_ge(w_hi_done, i + 1)
                dve.tensor_tensor(w_lo[:, i // DK, i % DK, :], raw_w(i), w_hi[:, i // DK, i % DK, :],
                                  ALU.subtract).then_inc(w_lo_done, 1)
            dve.wait_ge(bias_in, 32)
            dve.wait_ge(w_lo_done, 2 * DK)

            def link(v, i, ins):
                ins.then_inc(chain, 1)
                if i not in (4, 6, 9):
                    dve.wait_ge(chain, v * 9 + i)

            def nmh(x):
                return x.rearrange("p (n m h) -> p n m h", n=N, m=N)

            def nhm(x):
                return x.rearrange("p (n m h) -> p n h m", n=N, m=N)

            def over_m(x):
                return x.rearrange("p (n h) -> p n h", n=N).unsqueeze(2).broadcast_to([P, N, N, 2])

            def chain_a(v, s):
                dve.wait_ge(qk_red, v * 4 + 4)
                link(v, 1, dve.tensor_tensor(sums[:, 0, :], sums[:, 0, :], sums[:, 1, :], ALU.add))
                link(v, 2, dve.tensor_tensor(sums[:, 2, :], sums[:, 2, :], sums[:, 3, :], ALU.subtract))
                link(v, 3, dve.tensor_tensor(sums[:, 1:4:2, :], sums[:, 0:3:2, :], sums[:, 0:3:2, :], ALU.mult))
                link(v, 4, dve.tensor_tensor(soft[:, s, :], sums[:, 1, :], sums[:, 3, :], ALU.add))

            def chain_b(v, s):
                dve.wait_ge(mag_done, v + 1)
                link(v, 5, dve.tensor_reduce(top[:, s, :].rearrange("p (n h) -> p n h", n=N), nhm(soft[:, s, :]),
                                             AX.X, ALU.max))
                link(v, 6, dve.tensor_tensor(nmh(soft[:, s, :]), nmh(soft[:, s, :]), over_m(top[:, s, :]),
                                             ALU.subtract))

            def chain_c(v, s):
                dve.wait_ge(exp_done, v + 1)
                link(v, 7, dve.tensor_reduce(den[:, s, :].rearrange("p (n h) -> p n h", n=N), nhm(soft[:, s, :]),
                                             AX.X, ALU.add))
                link(v, 8, dve.reciprocal(rden[:, s, :], den[:, s, :]))
                link(v, 9, dve.tensor_tensor(nmh(soft[:, s, :]), nmh(soft[:, s, :]), over_m(rden[:, s, :]), ALU.mult))

            def weighted_sum(v, s, ri):
                dve.wait_ge(pv_done[ri], v * 4 + 4)
                if not (isinstance(v, int) and v < 2):
                    dve.wait_ge(acc_done, v * 8 + 16)
                dve.tensor_reduce(o_row[:, s, ri, :, :], prod[:, 1 + ri, :].rearrange(
                    "p (n m f) -> p n f m", n=N, m=N), AX.X, ALU.add).then_inc(pv_red[ri], 1)

            def qk_read(u, hp, ri):
                for n in range(N):
                    dve.wait_ge(acc_done, u * 8 + (ri * 4 + n + 1))
                    dve.tensor_tensor(qk[:, hp % 2, ri, :, n, :],
                                      acc[ri][n][:, 0:2 * P].rearrange("p (a f) -> p a f", a=2),
                                      qk_bias[:, ri, hp, :].rearrange("p (a f) -> p a f", a=2),
                                      ALU.add).then_inc(qk_out, 1)

            def next_s_lo(tile):
                dve.wait_ge(s_hi_done[0], tile + 2)
                dve.tensor_tensor(s_lo[:, 0], s_raw[:, :, :], s_hi[:, 0], ALU.subtract).then_inc(s_lo_done[0], 1)

            def guarded(tile, fn):
                if isinstance(tile, int):
                    fn()
                else:
                    with dve.If(tile < TILES - 1):
                        fn()

            def own_product(u, s, wait):
                dve.wait_ge(qk_out, u * 8 + 12)
                if wait:
                    dve.wait_ge(qk_red, summed(u - 1, 2))
                for n in range(N):
                    score_product(dve, s, 0, 1, 3, n).then_inc(qkp_own, 1)

            def score_sum(u, c):
                if c == 3:
                    dve.wait_ge(qkp_own, u * 4 + 4)
                else:
                    dve.wait_ge(qkp_done, u * 12 + (4 * c + 4))
                _, _, slot, place = SCORES[c]
                dve.tensor_reduce(sums[:, place, :], prod[:, slot, :].rearrange("p (g f) -> p g f", f=HD),
                                  AX.X, ALU.add).then_inc(qk_red, 1)

            def tile_body(tile):
                for hp in range(HP):
                    u = tile * HP + hp
                    s = hp % 2
                    if exists(tile, hp, 2):
                        weighted_sum(tile * HP + (hp - 2), s, 0)
                    if hp == HP - 1:
                        guarded(tile, lambda: next_s_lo(tile))
                    qk_read(u, hp, 1)
                    if exists(tile, hp, 1):
                        chain_b(tile * HP + (hp - 1), 1 - s)
                    own_product(u, s, exists(tile, hp, 1))
                    if exists(tile, hp, 1):
                        chain_c(tile * HP + (hp - 1), 1 - s)
                    score_sum(u, 3)
                    score_sum(u, 0)
                    if hp == HP - 1:
                        guarded(tile, lambda: qk_read(tile * HP + HP, 0, 0))
                    else:
                        qk_read(tile * HP + (hp + 1), hp + 1, 0)
                    score_sum(u, 1)
                    score_sum(u, 2)
                    if exists(tile, hp, 1):
                        weighted_sum(tile * HP + (hp - 1), 1 - s, 1)
                    chain_a(u, s)
            qk_read(0, 0, 0)
            tiles(dve, tile_body)
            chain_b(STEPS - 1, 1)
            chain_c(STEPS - 1, 1)
            weighted_sum(STEPS - 2, 0, 0)
            weighted_sum(STEPS - 1, 1, 0)
            weighted_sum(STEPS - 1, 1, 1)


def project_stage(nc, ctx, dram, consts):
    def sb(name, shape, dt=F32):
        return ctx.enter_context(nc.sbuf_tensor(name, shape, dt))

    def sem(name):
        return ctx.enter_context(nc.semaphore(name))

    w_raw = sb("wo_raw", [P, 2, DK, D])
    w_hi, w_lo = sb("wo_hi", [P, 2, DK, D], F32R), sb("wo_lo", [P, 2, DK, D], F32R)
    bo = sb("bo_cols_sb", [P, 2, DK])
    o_raw = sb("o_raw", [P, 2, DK, N * P])
    o_hi, o_lo = sb("o_hi", [P, 2, DK, N * P], F32R), sb("o_lo", [P, 2, DK, N * P], F32R)
    a_out = sb("a_out", [P, 2, 2, N, DK, P], F32R)
    acc = [[ctx.enter_context(nc.psum_tensor(f"wo_acc{ri}{j}", [P, 512], F32)) for j in range(DK)] for ri in range(2)]

    w_in, w_hi_done, w_lo_done = [[sem(f"wo_{x}{ri}") for ri in range(2)] for x in ("in", "hi", "lo")]
    o_in, o_hi_done, o_lo_done = [[sem(f"o_{x}{ri}") for ri in range(2)] for x in ("in", "hi_done", "lo_done")]
    bo_in = sem("bo_in")
    passed = consts["passed"]
    acc_done, read_out = [[sem(f"wo_{x}{ri}") for ri in range(2)] for x in ("acc", "read")]
    a_hi_out = [sem("a_hi_out_r"), sem("a_hi_out_i")]
    a_stored = [sem("a_stored_r"), sem("a_stored_i")]

    with nc.Block() as block:

        @block.sync
        def _(sp):
            def load(tile, ri):
                sp.dma_start(o_raw[:, ri], dram["o_t"][ri, bass.ds(tile * HP, HP)].rearrange("k p f -> p k f")
                             ).then_inc(o_in[ri], 16)

            def store(tile, ri):
                sp.wait_ge(read_out[ri], tile * DK + DK)
                for part in range(2):
                    sp.dma_start(dram["a_t"][bass.ds(tile, 1), :, :, part, ri, :].rearrange("o n p f -> (o p) n f"),
                                 a_out[:, ri, part].rearrange("p n k b -> p n (k b)").bitcast(F32)).then_inc(a_stored[ri], 16)

            for ri in range(2):
                sp.dma_start(w_raw[:, ri], dram["wo_w"][ri]).then_inc(w_in[ri], 16)
                load(0, ri)
            sp.dma_start(bo[:, :, :], dram["bo_cols"]).then_inc(bo_in, 16)
            with sp.Fori(0, TILES - 1) as tile:
                for ri in range(2):
                    sp.wait_ge(o_lo_done[ri], tile + 1)
                    load(tile + 1, ri)
                for ri in range(2):
                    store(tile, ri)
            for ri in range(2):
                store(TILES - 1, ri)
            for ri in range(2):
                sp.wait_ge(a_stored[ri], 32 * TILES)

        @block.scalar
        def _(act):
            def split_high(tile, ri, first=False):
                act.wait_ge(o_in[ri], tile * 16 + 16)
                if not first:
                    act.wait_ge(acc_done[ri], tile * DK)
                act.activation(o_hi[:, ri], o_raw[:, ri], ACT.Copy).then_inc(o_hi_done[ri], 1)

            def read(tile, ri):
                act.wait_ge(a_stored[ri], tile * 32)
                for j in range(DK):
                    act.wait_ge(acc_done[ri], tile * DK + j + 1)
                    act.activation(a_out[:, ri, 0, :, j, :], acc[ri][j][:, :].rearrange("p (n b) -> p n b", n=N),
                                   ACT.Identity, bias=bo[:, ri, j:j + 1]).then_inc(a_hi_out[ri], 1)

            for ri in range(2):
                act.wait_ge(w_in[ri], 16)
                act.activation(w_hi[:, ri], w_raw[:, ri], ACT.Copy).then_inc(w_hi_done[ri], 1)
                split_high(0, ri, True)
            act.wait_ge(bo_in, 16)
            with act.Fori(0, TILES - 1) as tile:
                for ri in range(2):
                    split_high(tile + 1, ri)
                    read(tile, ri)
            for ri in range(2):
                read(TILES - 1, ri)

        @block.tensor
        def _(pe):
            for ri in range(2):
                pe.wait_ge(w_lo_done[ri], 1)
            with pe.Fori(0, TILES) as tile:
                for ri in range(2):
                    pe.wait_ge(o_lo_done[ri], tile + 1)
                    pe.wait_ge(read_out[ri], tile * DK)
                    for j in range(DK):
                        for k in range(DK):
                            s_hi, s_lo = w_hi[:, ri, k, j * P:(j + 1) * P], w_lo[:, ri, k, j * P:(j + 1) * P]
                            m_hi, m_lo = o_hi[:, ri, k, :], o_lo[:, ri, k, :]
                            pe.matmul(acc[ri][j][:, :], s_hi, m_hi, start=(k == 0), stop=False)
                            pe.matmul(acc[ri][j][:, :], s_hi, m_lo, start=False, stop=False)
                            mm = pe.matmul(acc[ri][j][:, :], s_lo, m_hi, start=False, stop=(k == DK - 1))
                        mm.then_inc(acc_done[ri], 1)

        @block.vector
        def _(dve):
            def split_low(tile, ri):
                dve.wait_ge(o_hi_done[ri], tile + 1)
                dve.tensor_tensor(o_lo[:, ri], o_raw[:, ri], o_hi[:, ri], ALU.subtract).then_inc(o_lo_done[ri], 1)

            for ri in range(2):
                dve.wait_ge(w_hi_done[ri], 1)
                dve.tensor_tensor(w_lo[:, ri], w_raw[:, ri], w_hi[:, ri], ALU.subtract).then_inc(w_lo_done[ri], 1)
                split_low(0, ri)
            dve.wait_ge(bo_in, 16)

            def read_low(tile, ri):
                for j in range(DK):
                    wait_apart(dve, a_hi_out[ri], tile * DK + j + 1, passed)
                    dve.scalar_tensor_tensor(out=a_out[:, ri, 1, :, j, :],
                                             in0=acc[ri][j][:, :].rearrange("p (n b) -> p n b", n=N),
                                             scalar=bo[:, ri, j:j + 1], in1=a_out[:, ri, 0, :, j, :],
                                             op0=ALU.add, op1=ALU.subtract).then_inc(read_out[ri], 1)

            with dve.Fori(0, TILES - 1) as tile:
                for ri in range(2):
                    split_low(tile + 1, ri)
                    read_low(tile, ri)
            for ri in range(2):
                read_low(TILES - 1, ri)


def interact_stage(nc, ctx, dram, consts):
    def sb(name, shape, dt=F32):
        return ctx.enter_context(nc.sbuf_tensor(name, shape, dt))

    def sem(name):
        return ctx.enter_context(nc.semaphore(name))

    H = D // 2
    WPIECES = 2 * N
    w_hi, w_lo = sb("int_hi", [P, N, 2, DK, D], F32R), sb("int_lo", [P, N, 2, DK, D], F32R)
    a_in_sb = sb("a_in_sb", [P, 2, 2, 2, DK * P], F32R)
    ri_rows = sb("ri_rows", [P, 2, 2, N, D])
    r2 = sb("r2", [P, 2, D])
    cos, sin = sb("cos", [P, N, H]), sb("sin", [P, N, H])
    zero = sb("zero", [P, N, H])
    x = [sb(f"x{h}", [P, N, H]) for h in range(2)]
    y = sb("y_sq", [P, N, H])
    q = sb("q", [P, N, H])
    tt = sb("tt", [P, N, H])
    sup = sb("sup", [P, 2, D])
    norm = sb("norm", [P, 4])
    neg_half = sb("neg_half2", [P, 1])
    ids = sb("ids_sb", [P, TILES, N], I32)
    strength = sb("strength", [P, TILES, N * N])
    strength_t = sb("strength_t", [P, 2, N * N])
    tiny = sb("tiny", [P, 1])
    acc_r1, acc_r2, acc_i = [[ctx.enter_context(nc.psum_tensor(f"{x_}{s}", [P, D], F32)) for s in range(2)]
                             for x_ in ("acc_r1", "acc_r2", "acc_i")]

    w_in = [sem(f"int_in{i}") for i in range(4)]
    w_hi_done, w_lo_done = sem("int_hi_done"), sem("int_lo_done")
    ids_in, strength_in = sem("ids_in"), sem("strength_in")
    const_set = sem("const_set")
    a_in = [sem("a_in0"), sem("a_in1")]
    r2_done, r1_done, i_done = sem("r2_done"), sem("r1_done"), sem("i_done")
    r2_out = sem("r2_out")
    r_out, i_out = sem("r_out"), sem("i_out")
    squared = sem("squared")
    summed = sem("summed")
    log_done = sem("log_done")
    inv_done = sem("inv_done")
    strength_now = sem("strength_now")
    cos_done, sin_done, zero_done = sem("cos_done"), sem("sin_done"), sem("zero_done")
    t_steps, p_steps, q_terms = sem("t_steps"), sem("p_steps"), sem("q_terms")
    q_steps = sem("q_steps")
    cp_done = sem("cp_done")
    tq_done = sem("tq_done")
    f_done = sem("f_done")
    fr_done, fi_done = sem("fr_done"), sem("fi_done")
    red_done = sem("red_done")
    norm_steps = sem("norm_steps")
    rnorm_done = sem("rnorm_done")
    sup_ready = sem("sup_ready")
    sup_stored = sem("sup_stored")
    passed = consts["passed"]

    def raw_w(i):
        return ri_rows[:, (i % 4) // 2, i % 2, :, :]

    def run(eng, invert, gather, fold, unit, begin=None):
        def body(tile, s, one, two):
            for n in range(N):
                if begin is not None:
                    begin(tile, s, n)
                if n % 2 == 0 and one:
                    invert(tile - 1, 1 - s, n // 2)
                    if n == 2:
                        fold(tile - 1, 1 - s, 0)
                    elif two:
                        fold(tile - 2, s, 1)
                if n % 2 == 1 and one:
                    gather(tile - 1, 1 - s, n // 2)
                unit(tile, s, n)
        body(0, 0, False, False)
        body(1, 1, True, False)
        with eng.Fori(1, TILES // 2) as pair:
            for s in range(2):
                body(pair * 2 + s, s, True, True)
        invert(TILES - 1, 1, 0)
        fold(TILES - 2, 0, 1)
        gather(TILES - 1, 1, 0)
        invert(TILES - 1, 1, 1)
        fold(TILES - 1, 1, 0)
        gather(TILES - 1, 1, 1)
        fold(TILES - 1, 1, 1)

    def others(j):
        return [i for i in range(N) if i != j]

    def s_col(s, i, j):
        return strength_t[:, s, i * N + j:i * N + j + 1]

    def half_rows(s, ri, h):
        return ri_rows[:, s, ri, :, h * H:(h + 1) * H]

    with nc.Block() as block:

        @block.sync
        def _(sp):
            sp.dma_start(ids[:, :, :], dram["ids"]).then_inc(ids_in, 16)
            sp.dma_start(raw_w(0), dram["int_w"][0]).then_inc(w_in[0], 16)
            for i in range(1, WPIECES):
                if i >= 4:
                    sp.wait_ge(w_lo_done, i - 3)
                sp.dma_start(raw_w(i), dram["int_w"][i]).then_inc(w_in[i % 4], 16)

            def store(tile):
                sp.wait_ge(sup_ready, tile + 1)
                sp.dma_start(dram["sup_d"][bass.ds(tile, 1)].rearrange("o p r f -> (o p) r f"), sup[:, :, :]
                             ).then_inc(sup_stored, 16)

            with sp.Fori(0, TILES) as tile:
                store(tile)
            sp.wait_ge(sup_stored, 16 * TILES)

        @block.scalar
        def _(act):
            def split(n):
                for i in (2 * n, 2 * n + 1):
                    act.wait_ge(w_in[i % 4], 16 * (i // 4) + 16)
                    act.activation(w_hi[:, n, i % 2], raw_w(i), ACT.Copy).then_inc(w_hi_done, 1)
                if n == 3:
                    act.wait_ge(const_set, 2)

            def invert(tile, s, h):
                v = tile * 2 + h
                if h == 0:
                    act.wait_ge(r_out, tile * N + N + 2)
                    act.wait_ge(i_out, tile * N + N + 2)
                if not (isinstance(tile, int) and tile == 0):
                    act.wait_ge(fr_done, v - 1)
                    act.wait_ge(fi_done, v - 1)
                act.activation(x[h][:, :, :], half_rows(s, 0, h), ACT.Square).then_inc(squared, 1)
                if not (isinstance(tile, int) and v == 0):
                    act.wait_ge(q_steps, v * 3 - 2)
                act.activation(y[:, :, :], half_rows(s, 1, h), ACT.Square).then_inc(squared, 1)
                act.wait_ge(summed, v + 1)
                act.activation(x[h][:, :, :], x[h][:, :, :], ACT.Ln, bias=tiny[:, 0:1]).then_inc(log_done, 1)
                act.wait_ge(log_done, v + 1)
                act.activation(x[h][:, :, :], x[h][:, :, :], ACT.Exp, scale=-0.5).then_inc(inv_done, 1)

            def gather(tile, s, h):
                v = tile * 2 + h
                act.wait_ge(strength_now, tile + 1)
                act.wait_ge(sin_done, v + 1)
                act.wait_ge(red_done, v * 2)
                for place, m in ((q, 0), (y, 1), (zero, 2)):
                    if m == 2:
                        act.wait_ge(t_steps, v * 12 + 12)
                    for j in range(N):
                        i = others(j)[m]
                        act.activation(place[:, j, :], sin[:, i, :], ACT.Copy, scale=s_col(s, i, j)
                                       ).then_inc(q_terms, 1)

            def unit(tile, s, n):
                g = tile * N + n
                act.wait_ge(r2_done, g + 1)
                act.wait_ge(r_out, g + 1)
                act.activation(r2[:, n % 2, :], acc_r2[n % 2][:, :], ACT.Copy).then_inc(r2_out, 1)
                act.wait_ge(i_done, g + 1)
                if n == 0:
                    if isinstance(tile, int) and tile < 2:
                        act.wait_ge(w_lo_done, WPIECES)
                    else:
                        act.wait_ge(fi_done, tile * 2 - 2)
                act.activation(ri_rows[:, s, 1, n, :], acc_i[n % 2][:, :], ACT.Copy).then_inc(i_out, 1)

            for n in range(N):
                split(n)
            run(act, invert, gather, lambda tile, s, h: None, unit)

        @block.tensor
        def _(pe):
            def unit(tile, n, first):
                g = tile * N + n
                s = n % 2
                if first:
                    pe.wait_ge(w_lo_done, 2 * n + 2)
                pe.wait_ge(a_in[s], tile * 32 + 16 * (n // 2) + 16)
                pe.wait_ge(r_out, g + 1)
                pe.wait_ge(i_out, g + 1)
                for bank, parts, done in ((acc_r2[s], ((1, 1),), r2_done), (acc_r1[s], ((0, 0),), r1_done),
                                          (acc_i[s], ((0, 1), (1, 0)), i_done)):
                    for ai_, wi in parts:
                        for k in range(DK):
                            s_hi, s_lo = [a_in_sb[:, s, c, ai_, k * P:(k + 1) * P] for c in range(2)]
                            m_hi, m_lo = w_hi[:, n, wi, k, :], w_lo[:, n, wi, k, :]
                            start = k == 0 and (ai_, wi) == parts[0]
                            stop = k == DK - 1 and (ai_, wi) == parts[-1]
                            pe.matmul(bank[:, :], s_hi, m_hi, start=start, stop=False)
                            pe.matmul(bank[:, :], s_hi, m_lo, start=False, stop=False)
                            mm = pe.matmul(bank[:, :], s_lo, m_hi, start=False, stop=stop)
                    mm.then_inc(done, 1)

            for n in range(N):
                unit(0, n, True)
            with pe.Fori(1, TILES) as tile:
                for n in range(N):
                    unit(tile, n, False)

        @block.gpsimd
        def _(pool):
            pool.memset(neg_half[:, :], -0.5).then_inc(const_set, 1)
            pool.memset(tiny[:, :], TINY).then_inc(const_set, 1)
            def load(tile, n):
                pool.dma_start(a_in_sb[:, n % 2].rearrange("p c r f -> p (c r f)"),
                               dram["a_t"][bass.ds(tile, 1), n].rearrange("o p c r f -> (o p) (c r f)")
                               ).then_inc(a_in[n % 2], 16)

            load(0, 0)
            pool.wait_ge(ids_in, 16)
            for t in range(TILES):
                for f in range(N):
                    pool.indirect_dma_start(
                        out=strength[:, t, f * N:(f + 1) * N], out_offset=None, in_=dram[f"tbl_{f}"],
                        in_offset=bass.IndirectOffsetOnAxis(ap=ids[:, t, f:f + 1], axis=0)).then_inc(strength_in, 16)
            pool.wait_ge(const_set, 2)

            def gather(tile, s, h):
                v = tile * 2 + h
                pool.wait_ge(inv_done, v + 1)
                pool.tensor_tensor(sin[:, :, :], half_rows(s, 1, h), x[h][:, :, :], ALU.mult).then_inc(sin_done, 1)
                for m, term in ((1, y), (2, zero)):
                    pool.wait_ge(q_terms, v * 12 + (m * 4 + 4))
                    pool.tensor_tensor(q[:, :, :], q[:, :, :], term[:, :, :], ALU.add).then_inc(q_steps, 1)
                    pool.wait_ge(q_steps, v * 3 + m)
                pool.tensor_tensor(q[:, :, :], sin[:, :, :], q[:, :, :], ALU.mult).then_inc(q_steps, 1)
                pool.wait_ge(q_steps, v * 3 + 3)
                pool.tensor_tensor(tt[:, :, :], tt[:, :, :], q[:, :, :], ALU.add).then_inc(tq_done, 1)

            def fold(tile, s, h):
                v = tile * 2 + h
                pool.wait_ge(f_done, v + 1)
                pool.tensor_tensor(q[:, :, :], half_rows(s, 1, h), x[h][:, :, :], ALU.mult).then_inc(fi_done, 1)
                if h == 1:
                    pool.wait_ge(norm_steps, tile * 3 + 3)
                    pool.tensor_tensor(norm[:, 2:3], norm[:, 1:2], neg_half[:, 0:1], ALU.pow).then_inc(rnorm_done, 1)

            def begin(tile, s, n):
                if not (isinstance(tile, int) and tile + n == 0):
                    wait_apart(pool, i_done, tile * N + n, passed)
                if n < N - 1:
                    load(tile, n + 1)
                elif isinstance(tile, int) or s == 0:
                    load(tile + 1, 0)
                else:
                    with pool.If(tile < TILES - 1):
                        load(tile + 1, 0)

            run(pool, lambda tile, s, h: None, gather, fold, lambda tile, s, n: None, begin)

        @block.vector
        def _(dve):
            dve.sem_inc(r_out, 2)
            dve.sem_inc(i_out, 2)
            for i in range(WPIECES):
                dve.wait_ge(w_hi_done, i + 1)
                dve.tensor_tensor(w_lo[:, i // 2, i % 2], raw_w(i), w_hi[:, i // 2, i % 2], ALU.subtract
                                  ).then_inc(w_lo_done, 1)
            dve.wait_ge(w_lo_done, WPIECES)
            dve.wait_ge(strength_in, 16 * TILES * N)

            def unit(tile, s, n):
                g = tile * N + n
                dve.wait_ge(r2_out, g + 1)
                dve.wait_ge(r1_done, g + 1)
                dve.tensor_tensor(ri_rows[:, s, 0, n, :], acc_r1[n % 2][:, :], r2[:, n % 2, :], ALU.subtract
                                  ).then_inc(r_out, 1)

            def invert(tile, s, h):
                v = tile * 2 + h
                dve.wait_ge(squared, v * 2 + 2)
                dve.tensor_tensor(x[h][:, :, :], x[h][:, :, :], y[:, :, :], ALU.add).then_inc(summed, 1)

            def gather(tile, s, h):
                v = tile * 2 + h
                if h == 0:
                    dve.tensor_copy(strength_t[:, s, :], strength[:, bass.ds(tile, 1), :].rearrange("p o f -> p (o f)")
                                    ).then_inc(strength_now, 1)
                dve.wait_ge(inv_done, v + 1)
                wait_apart(dve, q_steps, v * 3, passed)
                dve.tensor_scalar(zero[:, :, :], x[h][:, :, :], ZERO_ABOVE, None, ALU.is_gt).then_inc(zero_done, 1)
                dve.tensor_tensor(cos[:, :, :], half_rows(s, 0, h), x[h][:, :, :], ALU.mult).then_inc(cos_done, 1)
                dve.wait_ge(zero_done, v + 1)
                dve.wait_ge(strength_now, tile + 1)
                for m in range(N - 1):
                    if m > 0:
                        wait_apart(dve, t_steps, v * 12 + m * 4, passed)
                    for j in range(N):
                        i = others(j)[m]
                        if m == 0:
                            dve.tensor_scalar(tt[:, j, :], zero[:, i, :], s_col(s, i, j), s_col(s, j, j),
                                              ALU.mult, ALU.add).then_inc(t_steps, 1)
                        else:
                            dve.scalar_tensor_tensor(out=tt[:, j, :], in0=zero[:, i, :], scalar=s_col(s, i, j),
                                                     in1=tt[:, j, :], op0=ALU.mult, op1=ALU.add).then_inc(t_steps, 1)
                dve.wait_ge(cos_done, v + 1)
                wait_apart(dve, sin_done, v + 1, passed)
                for m in range(N - 1):
                    if m > 0:
                        wait_apart(dve, p_steps, v * 12 + m * 4, passed)
                    for j in range(N):
                        i = others(j)[m]
                        if m == 0:
                            dve.tensor_scalar(x[h][:, j, :], cos[:, i, :], s_col(s, i, j), None, ALU.mult
                                              ).then_inc(p_steps, 1)
                        else:
                            dve.scalar_tensor_tensor(out=x[h][:, j, :], in0=cos[:, i, :], scalar=s_col(s, i, j),
                                                     in1=x[h][:, j, :], op0=ALU.mult, op1=ALU.add).then_inc(p_steps, 1)
                dve.wait_ge(p_steps, v * 12 + 12)
                dve.tensor_tensor(x[h][:, :, :], cos[:, :, :], x[h][:, :, :], ALU.mult).then_inc(cp_done, 1)

            def fold(tile, s, h):
                v = tile * 2 + h
                dve.wait_ge(cp_done, v + 1)
                dve.wait_ge(tq_done, v + 1)
                dve.tensor_tensor(x[h][:, :, :], x[h][:, :, :], tt[:, :, :], ALU.add).then_inc(f_done, 1)
                dve.wait_ge(f_done, v + 1)
                dve.tensor_tensor(tt[:, :, :], half_rows(s, 0, h), x[h][:, :, :], ALU.mult).then_inc(fr_done, 1)
                if h == 0:
                    dve.wait_ge(sup_stored, tile * 16)
                dve.wait_ge(fr_done, v + 1)
                dve.tensor_reduce(sup[:, 0, h * H:(h + 1) * H], tt[:, :, :].rearrange("p n f -> p f n"),
                                  AX.X, ALU.add).then_inc(red_done, 1)
                dve.wait_ge(fi_done, v + 1)
                dve.tensor_reduce(sup[:, 1, h * H:(h + 1) * H], q[:, :, :].rearrange("p n f -> p f n"),
                                  AX.X, ALU.add).then_inc(red_done, 1)
                if h == 1:
                    dve.wait_ge(red_done, v * 2 + 2)
                    dve.tensor_tensor(tt[:, :, :].rearrange("p n f -> p (n f)"),
                                      sup[:, :, :].rearrange("p r f -> p (r f)"),
                                      sup[:, :, :].rearrange("p r f -> p (r f)"), ALU.mult).then_inc(norm_steps, 1)
                    dve.wait_ge(norm_steps, tile * 3 + 1)
                    dve.tensor_reduce(norm[:, 0:1], tt[:, :, :].rearrange("p n f -> p (n f)"), AX.X, ALU.add
                                      ).then_inc(norm_steps, 1)
                    dve.wait_ge(norm_steps, tile * 3 + 2)
                    dve.tensor_scalar(norm[:, 1:2], norm[:, 0:1], 1e-8, None, ALU.add).then_inc(norm_steps, 1)
                    dve.wait_ge(rnorm_done, tile + 1)
                    dve.tensor_scalar(sup[:, :, :], sup[:, :, :], norm[:, 2:3], None, ALU.mult).then_inc(sup_ready, 1)

            run(dve, invert, gather, fold, unit)


def measure_stage(nc, ctx, dram, consts):
    def sb(name, shape, dt=F32):
        return ctx.enter_context(nc.sbuf_tensor(name, shape, dt))

    def sem(name):
        return ctx.enter_context(nc.semaphore(name))

    ident = consts["ident"]
    D2 = 256
    w_raw = sb("m_raw", [P, 2, DK * D])
    meas_hi, meas_lo = sb("meas_hi", [P, 2, DK, D], F32R), sb("meas_lo", [P, 2, DK, D], F32R)
    post_hi, post_lo = sb("post_hi", [P, DK, D], F32R), sb("post_lo", [P, DK, D], F32R)
    top1_hi, top1_lo = sb("top1_hi", [P, DK, D], F32R), sb("top1_lo", [P, DK, D], F32R)
    top2_hi, top2_lo = sb("top2_hi", [P, DK, D2], F32R), sb("top2_lo", [P, DK, D2], F32R)
    post_b = sb("post_b_sb", [P, D])
    post_cols = sb("post_cols_sb", [P, 2, DK])
    top2_cols = sb("top2_cols_sb", [P, 2])
    top3_cols = sb("top3_cols_sb", [P, 2])
    sup_row = sb("sup_row", [P, TPH, 2, D])
    row = sb("row", [P, TPH, D])
    topx = sb("topx", [P, TPH, D])
    sup_hi, sup_lo = sb("sup_hi", [P, 2, DK, HALF], F32R), sb("sup_lo", [P, 2, DK, HALF], F32R)
    amp_hi, amp_lo = sb("amp_hi", [P, DK, HALF], F32R), sb("amp_lo", [P, DK, HALF], F32R)
    z_hi, z_lo = sb("z_hi", [P, DK, HALF], F32R), sb("z_lo", [P, DK, HALF], F32R)
    h_hi, h_lo = sb("h1_hi", [P, DK, HALF], F32R), sb("h1_lo", [P, DK, HALF], F32R)
    mr = sb("mr", [P, 2, HALF])
    mi = sb("mi", [P, 2, HALF])
    h2 = sb("h2", [P, 2, HALF])
    y_row = sb("y_row", [1, NHALF, HALF])
    stats = sb("post_stats", [P, TPH, 6])
    mv = sb("post_mv", [P, TPH, 2])
    var_eps, rstd = sb("post_var", [P, TPH]), sb("post_rstd", [P, TPH])
    neg_half = sb("neg_half3", [P, TPH])
    turn = [ctx.enter_context(nc.psum_tensor(f"m_turn{s}", [P, 512], F32)) for s in range(2)]
    acc_a, acc_b, acc_c = [[ctx.enter_context(nc.psum_tensor(f"m_acc_{x}{s}", [P, 512], F32)) for s in range(2)]
                           for x in "abc"]

    weights = [(dram["meas_w"][0], meas_hi[:, 0], meas_lo[:, 0]), (dram["meas_w"][1], meas_hi[:, 1], meas_lo[:, 1]),
               (dram["post_w"], post_hi[:, :, :], post_lo[:, :, :]),
               (dram["top1_w"], top1_hi[:, :, :], top1_lo[:, :, :]),
               (dram["top2_w"], top2_hi[:, :, :], top2_lo[:, :, :])]
    NW = len(weights)

    def raw(i):
        n = weights[i][1].shape[-1]
        return w_raw[:, i % 2, 0:DK * n].rearrange("p (k f) -> p k f", f=n)

    w_in = [sem("m_in0"), sem("m_in1")]
    w_hi_done, w_lo_done = sem("m_w_hi"), sem("m_w_lo")
    cols_in, sup_in, topx_in = sem("cols_in"), sem("sup_in"), sem("topx_in")
    turned = sem("m_turned")
    hi_done = sem("m_hi_done")
    lo_done = sem("m_lo_done")
    a_done, b_done, c_done = sem("ma_done"), sem("mb_done"), sem("mc_done")
    b_out, mi_done, mr_done = sem("mb_out"), sem("mi_done"), sem("mr_done")
    mr_squared, mag_summed, amp_done = sem("mr_squared"), sem("mag_summed"), sem("amp_done")
    amp_hi_done, amp_lo_done = sem("amp_hi_done"), sem("amp_lo_done")
    row_done, row_out = sem("row_done"), sem("row_out")
    stat_done, aggr_done, eps_done, rstd_done, half_set, normed = [
        sem(f"m_{x}") for x in ("stat", "aggr", "eps", "rstd", "half", "normed")]
    gelu_done = sem("m_gelu")
    h2_acc, h2_done, y_acc, y_out, y_stored = sem("h2_acc"), sem("h2_done"), sem("y_acc"), sem("y_out"), sem("y_stored")
    passed = consts["passed"]
    TURNS = 2 * DK + DK + DK

    with nc.Block() as block:

        @block.sync
        def _(sp):
            def load_half(half):
                for t in range(TPH):
                    sp.dma_start(sup_row[:, t], dram["sup_d"][bass.ds(half * TPH + t, 1)]
                                 .rearrange("o p r f -> (o p) r f")).then_inc(sup_in, 16)
                sp.dma_start(topx[:, :, :], dram["top_x"][bass.ds(half, 1)].rearrange("o p t f -> (o p) t f")
                             ).then_inc(topx_in, 16)

            sp.dma_start(raw(0), weights[0][0]).then_inc(w_in[0], 16)
            load_half(0)
            sp.dma_start(raw(1), weights[1][0]).then_inc(w_in[1], 16)
            sp.dma_start(post_b[:, :], dram["post_row"].to_broadcast([P, D])).then_inc(cols_in, 16)
            sp.dma_start(post_cols[:, :, :], dram["post_cols"]).then_inc(cols_in, 16)
            sp.dma_start(top2_cols[:, :], dram["top2_cols"]).then_inc(cols_in, 16)
            sp.dma_start(top3_cols[:, :], dram["top3_cols"]).then_inc(cols_in, 16)
            for i in range(2, NW):
                sp.wait_ge(w_lo_done, i - 1)
                sp.dma_start(raw(i), weights[i][0]).then_inc(w_in[i % 2], 16)
            for half in range(1, NHALF):
                sp.wait_ge(turned, (half - 1) * TURNS + 2 * DK)
                sp.wait_ge(row_out, (half - 1) * 2 * TPH + 2 * TPH)
                load_half(half)
            for half in range(NHALF):
                sp.wait_ge(y_out, half + 1)
                sp.dma_start(dram["y"][half * HALF:(half + 1) * HALF, :].rearrange("f o -> o f"),
                             y_row[:, half, :]).then_inc(y_stored, 16)
            sp.wait_ge(y_stored, 16 * NHALF)

        @block.scalar
        def _(act):
            def turn_high(half, i, dst, fn):
                g = half * TURNS + i
                act.wait_ge(turned, g + 1)
                act.activation(dst, turn[i % 2][:, :], fn).then_inc(hi_done, 1)

            def split_weights(i):
                act.wait_ge(w_in[i % 2], 16 * (i // 2) + 16)
                act.activation(weights[i][1], raw(i), ACT.Copy).then_inc(w_hi_done, 1)

            for i in range(NW):
                split_weights(i)
            act.wait_ge(cols_in, 64)
            with act.Fori(0, NHALF) as half:
                act.wait_ge(c_done, half * DK)
                for i in range(2 * DK):
                    turn_high(half, i, sup_hi[:, i // DK, i % DK, :], ACT.Copy)
                for j in range(DK):
                    s = j % 2
                    u = half * DK + j
                    act.wait_ge(b_done, u + 1)
                    if j < 2:
                        act.wait_ge(amp_lo_done, half * DK)
                    else:
                        act.wait_ge(amp_lo_done, u - 1)
                    act.activation(mr[:, s, :], acc_b[s][:, :], ACT.Copy).then_inc(b_out, 1)
                    act.wait_ge(c_done, u + 1)
                    act.activation(mi[:, s, :], acc_c[s][:, :], ACT.Square).then_inc(mi_done, 1)
                    act.wait_ge(mr_done, u + 1)
                    act.activation(mr[:, s, :], mr[:, s, :], ACT.Square).then_inc(mr_squared, 1)
                    act.wait_ge(mag_summed, u + 1)
                    act.activation(mr[:, s, :], mr[:, s, :], ACT.Sqrt).then_inc(amp_done, 1)
                    act.wait_ge(amp_done, u + 1)
                    act.wait_ge(row_done, half * 2 * TPH)
                    act.activation(amp_hi[:, j, :], mr[:, s, :], ACT.Copy).then_inc(amp_hi_done, 1)
                for j in range(DK):
                    i = 2 * DK + j
                    act.wait_ge(turned, half * TURNS + (i + 1))
                    act.activation(turn[i % 2][:, :], turn[i % 2][:, :], ACT.Gelu, scale=post_cols[:, 0, j:j + 1],
                                   bias=post_cols[:, 1, j:j + 1]).then_inc(gelu_done, 1)
                    act.wait_ge(gelu_done, half * DK + (j + 1))
                    act.activation(z_hi[:, j, :], turn[i % 2][:, :], ACT.Copy).then_inc(hi_done, 1)
                for j in range(DK):
                    turn_high(half, 3 * DK + j, h_hi[:, j, :], ACT.Relu)
                for j in range(2):
                    act.wait_ge(h2_acc, half * 2 + (j + 1))
                    act.activation(h2[:, j, :], acc_b[j][:, :], ACT.Relu, bias=top2_cols[:, j:j + 1]
                                   ).then_inc(h2_done, 1)
                act.wait_ge(y_acc, half + 1)
                act.activation(y_row[:, bass.ds(half, 1), :].rearrange("p o f -> p (o f)"), acc_c[0][0:1, :], ACT.Copy
                               ).then_inc(y_out, 1)

        @block.gpsimd
        def _(pool):
            pool.memset(neg_half[:, :], -0.5).then_inc(half_set, 1)
            pool.wait_ge(half_set, 1)
            with pool.Fori(0, NHALF) as half:
                pool.wait_ge(eps_done, half + 1)
                pool.tensor_tensor(rstd[:, :], var_eps[:, :], neg_half[:, :], ALU.pow).then_inc(rstd_done, 1)

        @block.tensor
        def _(pe):
            def turn_tile(half, i, src):
                pe.wait_ge(lo_done, half * TURNS + (i + 1))
                for t in range(TPH):
                    mm = pe.transpose(turn[i % 2][:, t * P:(t + 1) * P], src(t), ident)
                mm.then_inc(turned, 1)

            def product(bank, terms, done):
                for i, (s_hi, s_lo, m_hi, m_lo) in enumerate(terms):
                    pe.matmul(bank, s_hi, m_hi, start=(i == 0), stop=False)
                    pe.matmul(bank, s_hi, m_lo, start=False, stop=False)
                    mm = pe.matmul(bank, s_lo, m_hi, start=False, stop=(i == len(terms) - 1))
                mm.then_inc(done, 1)

            with pe.Fori(0, NHALF) as half:
                pe.wait_ge(sup_in, half * (16 * TPH) + 16 * TPH)
                for i in range(2 * DK):
                    ri, k = i // DK, i % DK
                    turn_tile(half, i, lambda t: sup_row[:, t, ri, k * P:(k + 1) * P])
                pe.wait_ge(w_lo_done, NW)
                pe.wait_ge(lo_done, half * TURNS + (2 * DK + 2))

                def meas(w, r, j):
                    return [(meas_hi[:, w, k, j * P:(j + 1) * P], meas_lo[:, w, k, j * P:(j + 1) * P],
                             sup_hi[:, r, k, :], sup_lo[:, r, k, :]) for k in range(DK)]

                for j in range(DK):
                    s = j % 2
                    u = half * DK + j
                    pe.wait_ge(b_out, u - 1) if j >= 2 else pe.wait_ge(h2_done, half * 2)
                    product(acc_b[s][:, :], meas(1, 1, j), b_done)
                    pe.wait_ge(mr_done, u - 1) if j >= 2 else pe.wait_ge(row_out, half * 2 * TPH)
                    product(acc_a[s][:, :], meas(0, 0, j), a_done)
                    pe.wait_ge(mi_done, u - 1) if j >= 2 else pe.wait_ge(y_out, half)
                    product(acc_c[s][:, :], meas(1, 0, j) + meas(0, 1, j), c_done)

                pe.wait_ge(amp_lo_done, half * DK + DK)
                for t in range(TPH):
                    if t < 2:
                        pe.wait_ge(mr_done, half * DK + DK)
                    else:
                        pe.wait_ge(row_out, half * (2 * TPH) + (t - 1))
                    product(acc_a[t % 2][:, :], [(amp_hi[:, k, t * P:(t + 1) * P], amp_lo[:, k, t * P:(t + 1) * P],
                                                  post_hi[:, k, :], post_lo[:, k, :]) for k in range(DK)], row_done)
                pe.wait_ge(normed, half * TPH + TPH)
                for k in range(DK):
                    turn_tile(half, 2 * DK + k, lambda t: row[:, t, k * P:(k + 1) * P])
                pe.wait_ge(lo_done, half * TURNS + (3 * DK + 2))
                for t in range(TPH):
                    pe.wait_ge(row_out, half * (2 * TPH) + (TPH + max(t - 1, 0)))
                    product(acc_a[t % 2][:, :], [(z_hi[:, k, t * P:(t + 1) * P], z_lo[:, k, t * P:(t + 1) * P],
                                                  top1_hi[:, k, :], top1_lo[:, k, :]) for k in range(DK)], row_done)
                pe.wait_ge(row_out, half * (2 * TPH) + 2 * TPH)
                for k in range(DK):
                    turn_tile(half, 3 * DK + k, lambda t: row[:, t, k * P:(k + 1) * P])
                pe.wait_ge(lo_done, half * TURNS + (4 * DK + 2))
                for j in range(2):
                    if j == 0:
                        pe.wait_ge(b_out, half * DK + DK)
                    product(acc_b[j][:, :], [(top2_hi[:, k, j * P:(j + 1) * P], top2_lo[:, k, j * P:(j + 1) * P],
                                              h_hi[:, k, :], h_lo[:, k, :]) for k in range(DK)], h2_acc)
                pe.wait_ge(mi_done, half * DK + DK)
                pe.wait_ge(h2_done, half * 2 + 2)
                for j in range(2):
                    mm = pe.matmul(acc_c[0][0:1, :], top3_cols[:, j:j + 1], h2[:, j, :], start=(j == 0), stop=(j == 1))
                mm.then_inc(y_acc, 1)

        @block.vector
        def _(dve):
            dve.sem_inc(lo_done, 2)
            for i in range(NW):
                dve.wait_ge(w_hi_done, i + 1)
                dve.tensor_tensor(weights[i][2], raw(i), weights[i][1], ALU.subtract).then_inc(w_lo_done, 1)
            dve.wait_ge(cols_in, 64)
            with dve.Fori(0, NHALF) as half:
                def turn_low(i, hi, lo):
                    dve.wait_ge(hi_done, half * TURNS + (i + 1))
                    dve.tensor_tensor(lo, turn[i % 2][:, :], hi, ALU.subtract).then_inc(lo_done, 1)

                for i in range(2 * DK):
                    turn_low(i, sup_hi[:, i // DK, i % DK, :], sup_lo[:, i // DK, i % DK, :])
                for j in range(DK):
                    s = j % 2
                    u = half * DK + j
                    dve.wait_ge(b_out, u + 1)
                    dve.wait_ge(a_done, u + 1)
                    dve.tensor_tensor(mr[:, s, :], acc_a[s][:, :], mr[:, s, :], ALU.subtract).then_inc(mr_done, 1)
                    dve.wait_ge(mi_done, u + 1)
                    dve.wait_ge(mr_squared, u + 1)
                    dve.tensor_tensor(mr[:, s, :], mr[:, s, :], mi[:, s, :], ALU.add).then_inc(mag_summed, 1)
                    dve.wait_ge(amp_hi_done, u + 1)
                    dve.tensor_tensor(amp_lo[:, j, :], mr[:, s, :], amp_hi[:, j, :], ALU.subtract
                                      ).then_inc(amp_lo_done, 1)
                dve.wait_ge(turned, half * TURNS + 2 * DK)
                for t in range(TPH):
                    r = half * (2 * TPH) + t
                    dve.wait_ge(row_done, r + 1)
                    dve.tensor_tensor(row[:, t, :], acc_a[t % 2][:, :], post_b[:, :], ALU.add).then_inc(row_out, 1)
                    dve.wait_ge(row_out, r + 1)
                    dve.bn_stats(stats[:, t, :], row[:, t, :]).then_inc(stat_done, 1)
                wait_apart(dve, stat_done, half * TPH + TPH, passed)
                for t in range(TPH):
                    dve.bn_aggr(mv[:, t, :], stats[:, t, :]).then_inc(aggr_done, 1)
                dve.wait_ge(aggr_done, half * TPH + TPH)
                dve.tensor_scalar(var_eps[:, :], mv[:, :, 1], EPS, None, ALU.add).then_inc(eps_done, 1)
                dve.wait_ge(rstd_done, half + 1)
                for t in range(TPH):
                    dve.tensor_scalar(row[:, t, :], row[:, t, :], mv[:, t, 0:1], rstd[:, t:t + 1],
                                      ALU.subtract, ALU.mult).then_inc(normed, 1)
                for j in range(DK):
                    turn_low(2 * DK + j, z_hi[:, j, :], z_lo[:, j, :])
                dve.wait_ge(topx_in, half * 16 + 16)
                for t in range(TPH):
                    dve.wait_ge(row_done, half * (2 * TPH) + (TPH + t + 1))
                    dve.tensor_tensor(row[:, t, :], acc_a[t % 2][:, :], topx[:, t, :], ALU.add).then_inc(row_out, 1)
                for j in range(DK):
                    i = 3 * DK + j
                    wait_apart(dve, hi_done, half * TURNS + (i + 1), passed)
                    dve.scalar_tensor_tensor(out=h_lo[:, j, :], in0=turn[i % 2][:, :], scalar=0.0, in1=h_hi[:, j, :],
                                             op0=ALU.max, op1=ALU.subtract).then_inc(lo_done, 1)


def quantum_tower(nc, dram):
    with ExitStack() as ctx:
        ident = ctx.enter_context(nc.sbuf_tensor("ident", [P, P], F32))
        ones_set = ctx.enter_context(nc.semaphore("ones_set"))
        ident_set = ctx.enter_context(nc.semaphore("ident_set"))
        with nc.Block() as block:

            @block.gpsimd
            def _(pool):
                pool.memset(ident[:, :], 1.0).then_inc(ones_set, 1)
                pool.wait_ge(ones_set, 1)
                pool.affine_select(out=ident[:, :], in_=ident[:, :], pattern=[[-1, P]], compare_op=ALU.is_equal,
                                   fill=0.0, base=0, channel_multiplier=1).then_inc(ident_set, 1)
                pool.wait_ge(ident_set, 1)

        consts = {"ident": ident[:, :], "passed": ctx.enter_context(nc.semaphore("passed"))}
        with ExitStack() as stage:
            encoder_stage(nc, stage, dram, consts)
        with ExitStack() as stage:
            attention_stage(nc, stage, dram, consts)
        with ExitStack() as stage:
            project_stage(nc, stage, dram, consts)
        with ExitStack() as stage:
            interact_stage(nc, stage, dram, consts)
        with ExitStack() as stage:
            measure_stage(nc, stage, dram, consts)


def layout(a):
    def k_major(w):
        return np.asarray(w).T

    def units(w):
        k, n = w.shape
        return w.reshape(k // (UNIT_K * P), UNIT_K, P, n // 512, 512).transpose(3, 0, 2, 1, 4)

    def cols(v):
        return np.asarray(v).reshape(-1, P).T

    pre = "L0_rec_"
    out = {}
    out["x_t"] = np.asarray(a["r_x"]).reshape(NHALF, HALF, KT, P).transpose(0, 3, 2, 1)
    w_top1 = np.asarray(a["W_top1"])
    out["enc_w"] = np.concatenate([
        units(w_top1[D:]), units(k_major(a[pre + "er_W1"])), units(k_major(a[pre + "ei_W1"])),
        units(k_major(a[pre + "er_W2"])), units(k_major(a[pre + "ei_W2"]))])
    out["enc_b1"] = np.concatenate([np.asarray(a[k]).reshape(-1, 512) for k in
                                    ("b_top1", pre + "er_b1", pre + "ei_b1")])
    out["ln_cols"] = np.stack([np.stack([cols(a[pre + e + "_g1"]), cols(a[pre + e + "_be1"])], 1)
                               for e in ("er", "ei")], 1)
    out["b2_cols"] = np.concatenate([cols(a[pre + "er_b2"]), cols(a[pre + "ei_b2"])], 1)
    def qkv(t):
        w = [k_major(a[pre + f"W{x}_{t}"]).reshape(DK, P, HP, P) for x in "qkv"]
        return np.stack(w, 3).reshape(DK, P, HP * 3 * P)

    out["qkv_w"] = np.stack([qkv("r"), qkv("i")])
    out["qk_bias"] = np.stack([np.stack([np.asarray(a[pre + f"b{x}_{t}"]).reshape(HP, P) for x in "qk"], 1)
                               .reshape(HP, 2 * P) for t in "ri"])
    out["v_cols"] = np.stack([cols(a[pre + "bv_r"]), cols(a[pre + "bv_i"])], 1)

    def k_tiles(w):
        return w.reshape(-1, P, w.shape[-1]).transpose(1, 0, 2)

    out["wo_w"] = np.stack([k_tiles(k_major(a[pre + f"Wo_{t}"])) for t in "ri"])
    out["bo_cols"] = np.stack([cols(a[pre + "bo_r"]), cols(a[pre + "bo_i"])], 1)
    out["int_w"] = np.stack([k_tiles(k_major(np.asarray(a[pre + f"int_W{t}"])[n])) for n in range(N) for t in "ri"])
    out["ids"] = np.asarray(a["ids"]).reshape(TILES, P, N).transpose(1, 0, 2)
    for f in range(N):
        out[f"tbl_{f}"] = np.asarray(a[f"tbl_{f}"])
    out["meas_w"] = np.stack([k_tiles(k_major(a[pre + f"meas_M{t}"])) for t in "ri"])
    out["post_w"] = k_tiles(k_major(a[pre + "post_W"]))
    out["post_row"] = np.asarray(a[pre + "post_b"]).reshape(1, D)
    out["post_cols"] = np.stack([cols(a[pre + "post_g"]), cols(a[pre + "post_be"])], 1)
    out["top1_w"] = k_tiles(w_top1[:D])
    out["top2_w"] = k_tiles(np.asarray(a["W_top2"]))
    out["top2_cols"] = cols(a["b_top2"])
    out["top3_cols"] = cols(np.asarray(a["W_top3"])[:, 0])
    return {k: np.ascontiguousarray(v) for k, v in out.items()}


def scratch_shapes():
    return {"s_t": (2, TILES, P, N * DK, P),
            "top_x": (NHALF, P, TPH, D),
            "o_t": (2, TILES * HP, P, N * P),
            "a_t": (TILES + 1, N, P, 2, 2, DK * P),
            "sup_d": (TILES, P, 2, D)}


def kernel(**inputs):
    import concourse.bacc as bacc
    from concourse.bass_utils import run_bass_kernel_spmd

    nc = bacc.Bacc("TRN2", target_bir_lowering=False, num_devices=1, dynamic_dma_scratch_size=2048)
    arrays = layout(inputs)
    dram = {}
    for name, a in arrays.items():
        dram[name] = nc.dram_tensor(name, a.shape, mybir.dt.from_np(a.dtype), kind="ExternalInput").ap()
    for name, shape in scratch_shapes().items():
        dram[name] = nc.dram_tensor(name, shape, F32, kind="Internal").ap()
    dram["y"] = nc.dram_tensor("y", (B, 1), F32, kind="ExternalOutput").ap()
    quantum_tower(nc, dram)
    return run_bass_kernel_spmd(nc, [arrays], core_ids=[0]).results[0]["y"]
```

```python
from contextlib import ExitStack

import numpy as np

import concourse.bass as bass
from concourse import mybir

F32 = mybir.dt.float32
F32R = mybir.dt.float32r
I32 = mybir.dt.int32
ALU = mybir.AluOpType
ACT = mybir.ActivationFunctionType
AX = mybir.AxisListType

P = 128
B = 1024
IN = 2048
HID = 2048
D = 512
N = 4
HEADS = 8
HD = D // HEADS
HALF = 512
NHALF = B // HALF
TPH = HALF // P
TILES = B // P
KT = IN // P
DK = D // P
UNIT_K = 2
UNITS = KT // UNIT_K
CHUNKS = 17
HP = HEADS // 2
EPS = 1e-5
TINY = 1e-37
ZERO_ABOVE = 3e18


def wait_apart(eng, sem, value, passed):
    eng.wait_ge(sem, value)
    eng.sem_inc(passed, 1)


def encoder_stage(nc, ctx, dram, consts):
    def sb(name, shape, dt=F32):
        return ctx.enter_context(nc.sbuf_tensor(name, shape, dt))

    def sem(name):
        return ctx.enter_context(nc.semaphore(name))

    ident = consts["ident"]
    a_hi, a_lo = sb("a_hi", [P, KT, HALF], F32R), sb("a_lo", [P, KT, HALF], F32R)
    b_hi, b_lo = sb("b_hi", [P, KT, HALF], F32R), sb("b_lo", [P, KT, HALF], F32R)
    hid = [sb("hid_r", [P, TPH, HID]), sb("hid_i", [P, TPH, HID])]
    raw = sb("raw", [P, 2, UNIT_K, 512])
    w_hi, w_lo = sb("w_hi", [P, 2, UNIT_K, 512], F32R), sb("w_lo", [P, 2, UNIT_K, 512], F32R)
    bias1 = sb("bias1", [P, 512])
    normed = sb("normed", [P, TPH, P])
    stats = sb("stats", [P, TPH, 4, 6])
    mv = sb("mv", [P, TPH, 2])
    var_eps = sb("var_eps", [P, TPH])
    rstd = sb("rstd", [P, TPH])
    neg_half = sb("neg_half", [P, TPH])
    ln_cols = sb("ln_cols_sb", [P, 2, 2, KT])
    b2_cols = sb("b2_cols_sb", [P, 2 * N * DK])
    acc = [ctx.enter_context(nc.psum_tensor(f"acc{t}", [P, 512], F32)) for t in range(4)]
    turn = [ctx.enter_context(nc.psum_tensor(f"turn{t}", [P, 512], F32)) for t in range(2)]

    raw_full = [sem("raw_full0"), sem("raw_full1")]
    raw_free = sem("raw_free")
    x_hi_done, x_lo_done = sem("x_hi_done"), sem("x_lo_done")
    x_in = [sem(f"x_in{q}") for q in range(4)]
    w_hi_done = sem("w_hi_done")
    w_free = sem("w_free")
    acc_done = sem("acc_done")
    acc_free = sem("acc_free")
    bias_in = sem("bias_in")
    params_in = sem("params_in")
    stat_done = sem("stat_done")
    aggr_done = sem("aggr_done")
    eps_done = sem("eps_done")
    rstd_done = sem("rstd_done")
    half_set = sem("half_set")
    norm_done = sem("norm_done")
    turned = sem("turned")
    gelu_done = sem("gelu_done")
    h_hi_done = sem("h_hi_done")
    turn_free = sem("turn_free")
    top_out = sem("top_out")
    passed = consts["passed"]
    s_out = [sem("s_out_r"), sem("s_out_i")]

    TOP, L1, L2 = range(3)
    phases = [(0, None, TOP, None), (1, 0, L1, None), (5, 1, L1, 0), (9, 0, L2, 1), (13, 1, L2, None)]
    S_OUT = 16 * N * TPH
    XU = UNITS
    SU = UNITS * CHUNKS

    def load_x(sp, half):
        for q in range(4):
            sp.dma_start(hid[0][:, q, :], dram["x_t"][half, :, q * 4:(q + 1) * 4, :]).then_inc(x_in[q], 16)

    def store_s(sp, enc, half, n):
        for t in range(TPH):
            sp.dma_start(dram["s_t"][enc, bass.ds(half * TPH + t, 1), :, bass.ds(n * DK, DK), :]
                         .rearrange("o p k b -> (o p) k b"),
                         hid[enc][:, bass.ds(n, 1), :].rearrange("p o (k t b) -> p (o k) t b", k=DK, t=TPH)[:, :, t, :]
                         ).then_inc(s_out[enc], 16)

    def x_unit(u):
        return hid[0][:, u // 2, (u % 2) * UNIT_K * 512:(u % 2 + 1) * UNIT_K * 512]

    def loop(eng, count, body):
        body(0, True)
        if count > 1:
            with eng.Fori(1, count) as c:
                body(c, False)

    with nc.Block() as block:

        @block.sync
        def _(sp):
            sp.dma_start(ln_cols[:, :, :, :], dram["ln_cols"]).then_inc(params_in, 16)
            sp.dma_start(b2_cols[:, :], dram["b2_cols"]).then_inc(params_in, 16)
            load_x(sp, 0)
            with sp.Fori(0, NHALF) as half:
                for first, enc, kind, _ in phases:
                    def chunk(c, peeled):
                        ci = c + first
                        for u in range(UNITS):
                            sp.wait_ge(raw_free, half * SU + ci * UNITS + u + 1)
                            sp.dma_start(raw[:, u % 2], dram["enc_w"][ci, u]).then_inc(raw_full[u % 2], 16)
                            if u == 4 and kind != L2:
                                sp.wait_ge(acc_free, half * (4 * CHUNKS) + ci * 4 + 4)
                                sp.dma_start(bias1[:, :], dram["enc_b1"][bass.ds(ci, 1), :].to_broadcast([P, 512])
                                             ).then_inc(bias_in, 16)
                            if u == 5 and kind == L1 and enc == 0 and peeled:
                                sp.dma_start(dram["top_x"][half], hid[1][:, :, 0:512]).then_inc(top_out, 16)
                            if u == 5 and kind == L2 and not (peeled and enc == 0):
                                pe_, pc = (enc, c - 1) if not peeled else (0, 3)
                                sp.wait_ge(acc_free, half * (4 * CHUNKS) + ci * 4 + 4)
                                store_s(sp, pe_, half, pc)
                            if u == 6 and kind == L2 and enc == 1 and peeled:
                                with sp.If(half < NHALF - 1):
                                    sp.wait_ge(s_out[0], half * S_OUT + S_OUT)
                                    load_x(sp, NHALF - 1)
                    loop(sp, 1 if kind == TOP else 4, chunk)
                sp.wait_ge(acc_free, half * (4 * CHUNKS) + 4 * CHUNKS + 4)
                store_s(sp, 1, half, 3)
            sp.wait_ge(s_out[0], S_OUT * NHALF)
            sp.wait_ge(s_out[1], S_OUT * NHALF)
            sp.wait_ge(top_out, 16 * NHALF)

        @block.scalar
        def _(act):
            act.wait_ge(params_in, 32)
            with act.Fori(0, NHALF) as half:
                for u in range(XU):
                    act.wait_ge(x_in[u // 2], half * 16 + 16)
                    if u == 0:
                        act.wait_ge(acc_done, half * (4 * CHUNKS))
                    act.activation(a_hi[:, u * UNIT_K:(u + 1) * UNIT_K, :], x_unit(u), ACT.Copy
                                   ).then_inc(x_hi_done, 1)
                for first, enc, kind, turn_enc in phases:
                    def chunk(c, peeled):
                        ci = c + first
                        for u in range(UNITS):
                            act.wait_ge(raw_full[u % 2],
                                        half * (8 * SU) + ci * (8 * UNITS) + 16 * (u // 2) + 16)
                            if u == 1:
                                act.wait_ge(acc_done, half * (4 * CHUNKS) + ci * 4)
                            else:
                                act.wait_ge(w_free, half * (CHUNKS * (UNITS - 1)) + ci * (UNITS - 1) + max(u - 1, 0))
                            act.activation(w_hi[:, u % 2], raw[:, u % 2], ACT.Copy).then_inc(w_hi_done, 1)
                            if turn_enc is not None and u >= 4:
                                jj = u - 4
                                h_hi = b_hi if turn_enc == 0 else a_hi
                                g = half * (2 * KT) + c * 4 + (turn_enc * KT + jj)
                                kt = c * 4 + jj
                                act.wait_ge(turned, g + 1)
                                act.activation(turn[jj % 2][:, :], turn[jj % 2][:, :], ACT.Gelu,
                                               scale=ln_cols[:, turn_enc, 0, bass.ds(kt, 1)],
                                               bias=ln_cols[:, turn_enc, 1, bass.ds(kt, 1)]).then_inc(gelu_done, 1)
                                act.wait_ge(gelu_done, g + 1)
                                act.activation(h_hi[:, bass.ds(kt, 1), :], turn[jj % 2][:, :], ACT.Copy
                                               ).then_inc(h_hi_done, 1)
                    loop(act, 1 if kind == TOP else 4, chunk)

        @block.gpsimd
        def _(pool):
            pool.sem_inc(raw_free, 2)
            pool.memset(neg_half[:, :], -0.5).then_inc(half_set, 1)
            pool.wait_ge(half_set, 1)
            with pool.Fori(0, NHALF) as half:
                for first, enc, kind, turn_enc in phases:
                    def chunk(c, peeled):
                        ci = c + first
                        for u in range(UNITS):
                            if u == 2 and peeled and turn_enc is not None:
                                pool.wait_ge(eps_done, half * 2 + turn_enc + 1)
                                pool.tensor_tensor(rstd[:, :], var_eps[:, :], neg_half[:, :], ALU.pow
                                                   ).then_inc(rstd_done, 1)
                            pool.wait_ge(w_hi_done, half * (CHUNKS * UNITS) + ci * UNITS + u + 1)
                            pool.tensor_tensor(w_lo[:, u % 2], raw[:, u % 2], w_hi[:, u % 2], ALU.subtract
                                               ).then_inc(raw_free, 1)
                    loop(pool, 1 if kind == TOP else 4, chunk)

        @block.tensor
        def _(pe):
            with pe.Fori(0, NHALF) as half:
                for first, enc, kind, turn_enc in phases:
                    def chunk(c):
                        ci = c + first
                        for u in range(UNITS):
                            pe.wait_ge(raw_free, half * SU + ci * UNITS + (2 + u + 1))
                            if kind == TOP:
                                pe.wait_ge(x_lo_done, half * XU + u + 1)
                            if kind == L2:
                                pe.wait_ge(turn_free, half * (2 * KT) + (2 + enc * KT + UNIT_K * (u + 1)))
                            for kk in range(UNIT_K):
                                k = u * UNIT_K + kk
                                for t in range(4):
                                    if k == 0:
                                        pe.wait_ge(acc_free, half * (4 * CHUNKS) + ci * 4 + t + 1)
                                    if kind == L2:
                                        m_hi, m_lo = (b_hi, b_lo) if enc == 0 else (a_hi, a_lo)
                                        s_hi = w_hi[:, u % 2, kk, t * P:(t + 1) * P]
                                        s_lo = w_lo[:, u % 2, kk, t * P:(t + 1) * P]
                                        m_hi, m_lo = m_hi[:, k, :], m_lo[:, k, :]
                                    else:
                                        s_hi = a_hi[:, k, t * P:(t + 1) * P]
                                        s_lo = a_lo[:, k, t * P:(t + 1) * P]
                                        m_hi, m_lo = w_hi[:, u % 2, kk, :], w_lo[:, u % 2, kk, :]
                                    pe.matmul(acc[t][:, :], s_hi, m_hi, start=(k == 0), stop=False)
                                    pe.matmul(acc[t][:, :], s_hi, m_lo, start=False, stop=False)
                                    mm = pe.matmul(acc[t][:, :], s_lo, m_hi, start=False, stop=(k == KT - 1))
                                    if k == KT - 1:
                                        mm.then_inc(acc_done, 1)
                            if u < UNITS - 1:
                                mm.then_inc(w_free, 1)
                            if turn_enc is not None and 2 <= u < 6:
                                jj = u - 2
                                g = half * (2 * KT) + c * 4 + (turn_enc * KT + jj)
                                pe.wait_ge(norm_done, g * 4 + 4)
                                pe.wait_ge(turn_free, g + 1)
                                for t in range(TPH):
                                    mm = pe.transpose(turn[jj % 2][:, t * P:(t + 1) * P], normed[:, t, :], ident)
                                mm.then_inc(turned, 1)
                    if kind == TOP:
                        chunk(0)
                    else:
                        with pe.Fori(0, 4) as c:
                            chunk(c)

        @block.vector
        def _(dve):
            dve.sem_inc(acc_free, 4)
            dve.sem_inc(turn_free, 2)
            dve.wait_ge(params_in, 32)
            with dve.Fori(0, NHALF) as half:
                for u in range(XU):
                    dve.wait_ge(x_hi_done, half * XU + u + 1)
                    dve.tensor_tensor(a_lo[:, u * UNIT_K:(u + 1) * UNIT_K, :], x_unit(u),
                                      a_hi[:, u * UNIT_K:(u + 1) * UNIT_K, :], ALU.subtract).then_inc(x_lo_done, 1)
                for first, enc, kind, turn_enc in phases:
                    def norm(c, jj):
                        g = half * (2 * KT) + c * 4 + (turn_enc * KT + jj)
                        dve.wait_ge(turned, g)
                        for t in range(TPH):
                            dve.tensor_scalar(normed[:, t, :], hid[turn_enc][:, t, bass.ds(c * 512 + jj * P, P)],
                                              mv[:, t, 0:1], rstd[:, t:t + 1], ALU.subtract, ALU.mult
                                              ).then_inc(norm_done, 1)

                    def low(c, jj):
                        h_hi, h_lo = (b_hi, b_lo) if turn_enc == 0 else (a_hi, a_lo)
                        g = half * (2 * KT) + c * 4 + (turn_enc * KT + jj)
                        kt = c * 4 + jj
                        dve.wait_ge(h_hi_done, g + 1)
                        dve.tensor_tensor(h_lo[:, bass.ds(kt, 1), :], turn[jj % 2][:, :],
                                          h_hi[:, bass.ds(kt, 1), :], ALU.subtract).then_inc(turn_free, 1)

                    def chunk(c, peeled):
                        ci = c + first
                        done = half * (4 * CHUNKS) + ci * 4
                        if turn_enc is not None:
                            norm(c, 0)
                            for jj in range(1, 4):
                                norm(c, jj)
                                low(c, jj - 1)
                            low(c, 3)
                        if kind != L2:
                            dve.wait_ge(bias_in, (half * 9 + ci) * 16 + 16)
                        if kind == TOP:
                            dve.wait_ge(s_out[1], half * S_OUT)
                        if kind == L1 and peeled:
                            if enc == 1:
                                dve.wait_ge(top_out, half * 16 + 16)
                            else:
                                dve.wait_ge(s_out[0], half * S_OUT)
                        for t in range(4):
                            dve.wait_ge(acc_done, done + t + 1)
                            if kind == TOP:
                                dve.tensor_tensor(hid[1][:, t, 0:512], acc[t][:, :], bias1[:, :], ALU.add
                                                  ).then_inc(acc_free, 1)
                            elif kind == L1:
                                h = hid[enc][:, t, bass.ds(c * 512, 512)]
                                dve.tensor_tensor(h, acc[t][:, :], bias1[:, :], ALU.add).then_inc(acc_free, 1)
                                dve.wait_ge(acc_free, done + (4 + t + 1))
                                dve.bn_stats(stats[:, t, bass.ds(c, 1), :], h).then_inc(stat_done, 1)
                            else:
                                dve.tensor_scalar(hid[enc][:, bass.ds(c, 1), t * 512:(t + 1) * 512], acc[t][:, :],
                                                  b2_cols[:, bass.ds(c * DK + (enc * N * DK + t), 1)], None, ALU.add
                                                  ).then_inc(acc_free, 1)
                    if kind == TOP:
                        chunk(0, True)
                    elif kind == L1:
                        loop(dve, 4, chunk)
                        wait_apart(dve, stat_done, half * 32 + (enc * 16 + 16), passed)
                        for t in range(TPH):
                            dve.bn_aggr(mv[:, t, :], stats[:, t, :, :].rearrange("p c s -> p (c s)")
                                        ).then_inc(aggr_done, 1)
                        dve.wait_ge(aggr_done, half * 8 + (enc * 4 + 4))
                        dve.tensor_scalar(var_eps[:, :], mv[:, :, 1], EPS, None, ALU.add).then_inc(eps_done, 1)
                        dve.wait_ge(rstd_done, half * 2 + enc + 1)
                    else:
                        loop(dve, 4, chunk)


def attention_stage(nc, ctx, dram, consts):
    def sb(name, shape, dt=F32):
        return ctx.enter_context(nc.sbuf_tensor(name, shape, dt))

    def sem(name):
        return ctx.enter_context(nc.semaphore(name))

    ident = consts["ident"]
    QKV = 3 * P
    STEPS = TILES * HP
    LAG = 4
    PAIRS = N * N * 2
    w_hi, w_lo = sb("qkv_hi", [P, 2, DK, HP * QKV], F32R), sb("qkv_lo", [P, 2, DK, HP * QKV], F32R)
    qk_bias = sb("qk_bias_sb", [P, 2, HP, 2 * P])
    v_cols = sb("v_cols_sb", [P, 2, HP])
    s_raw = sb("s_raw", [P, N * DK, P])
    s_hi, s_lo = sb("s_hi", [P, 2, N * DK, P], F32R), sb("s_lo", [P, 2, N * DK, P], F32R)
    qk = sb("qk", [P, 2, 2, 2, N, P])
    vals = sb("vals", [P, HP, 2, N, P])
    comb = sb("comb", [P, 2, 2, N, P])
    prod = sb("prod", [P, 3, 4 * 512])
    o_row = sb("o_row", [P, 2, 2, N, P])
    o_col = sb("o_col", [P, 2, N * P])
    sums = sb("sums", [P, 3, PAIRS])
    soft = sb("soft", [P, 2, PAIRS])
    top = sb("top", [P, 2, N * 2])
    den = sb("den", [P, 2, N * 2])
    rden = sb("rden", [P, 2, N * 2])
    mag_eps = sb("mag_eps", [P, 1])
    acc = [[ctx.enter_context(nc.psum_tensor(f"qkv{ri}{n}", [P, 512], F32)) for n in range(N)] for ri in range(2)]

    SCALE2 = 1.0 / HD

    w_in = [sem(f"qkv_in{i}") for i in range(4)]
    w_hi_done = sem("qkv_hi_done")
    w_lo_done = sem("qkv_lo_done")
    bias_in = sem("qk_bias_in")
    eps_set = sem("mag_eps_set")
    s_in = [sem("s_in_r"), sem("s_in_i")]
    s_hi_done = [sem("s_hi_r"), sem("s_hi_i")]
    s_lo_done = [sem("s_lo_r"), sem("s_lo_i")]
    acc_done = sem("qkv_done")
    qk_out = sem("qk_out")
    v_out = sem("v_out")
    qkp_done = sem("qkp_done")
    qkp_own = sem("qkp_own")
    comb_done = sem("comb_done")
    pv_done = [sem("pv_done_r"), sem("pv_done_i")]
    qk_red = sem("qk_red")
    pv_red = [sem("pv_red_r"), sem("pv_red_i")]
    chain = sem("chain")
    mag_done, exp_done = sem("mag_done"), sem("exp_done")
    o_out = [sem("o_out_r"), sem("o_out_i")]

    SLOT = (0, 1, 0)
    OWN = 3

    def summed(u, c):
        return u * 3 + (c + 1)

    def score_product(eng, s, c, n):
        qn = (comb[:, s, 0], qk[:, s, 1, 0], qk[:, s, 0, 0])[c][:, n:n + 1, :]
        k = (qk[:, s, 0, 1], comb[:, s, 1], qk[:, s, 1, 1])[c]
        return eng.tensor_tensor(prod[:, SLOT[c], n * 512:(n + 1) * 512].rearrange("p (m f) -> p m f", m=N),
                                 qn.broadcast_to([P, N, P]), k, ALU.mult)

    def raw_w(i):
        return prod[:, :, :].rearrange("p s f -> p (s f)")[:, (i % 4) * HP * QKV:(i % 4 + 1) * HP * QKV]

    def tiles(eng, body):
        body(0)
        with eng.Fori(1, TILES) as tile:
            body(tile)

    def exists(tile, hp, lag):
        return not (isinstance(tile, int) and tile * HP + hp < lag)

    with nc.Block() as block:

        @block.sync
        def _(sp):
            sp.dma_start(qk_bias[:, :, :, :], dram["qk_bias"].partition_broadcast(P)).then_inc(bias_in, 16)
            sp.dma_start(v_cols[:, :, :], dram["v_cols"]).then_inc(bias_in, 16)

            for ri in range(2):
                if ri == 1:
                    sp.wait_ge(s_lo_done[0], 1)
                sp.dma_start(s_raw[:, :, :], dram["s_t"][ri, 0]).then_inc(s_in[ri], 16)
                for k in range(DK):
                    i = ri * DK + k
                    if i >= 4:
                        sp.wait_ge(w_lo_done, i - 3)
                    sp.dma_start(raw_w(i), dram["qkv_w"][ri, k]).then_inc(w_in[i % 4], 16)

            def col_store(v):
                for ri in range(2):
                    sp.wait_ge(v_out, v * 8 + (8 * LAG + 8 + ri * 4 + 4))
                    sp.dma_start(dram["o_t"][ri, bass.ds(v, 1)].rearrange("o p f -> (o p) f"), o_col[:, ri, :]
                                 ).then_inc(o_out[ri], 16)

            def next_s(tile, ri):
                if ri == 0:
                    sp.wait_ge(s_lo_done[1], tile)
                else:
                    sp.wait_ge(s_lo_done[0], tile + 1)
                sp.dma_start(s_raw[:, :, :], dram["s_t"][ri, bass.ds(tile, 1)].rearrange("o p k b -> (o p) k b")
                             ).then_inc(s_in[ri], 16)

            next_s(1, 0)
            next_s(1, 1)
            with sp.Fori(2, TILES) as tile:
                next_s(tile, 0)
                for hp in range(HP):
                    col_store(tile * HP + (hp - 2 * HP))
                next_s(tile, 1)
            for v in range((TILES - 2) * HP, STEPS):
                col_store(v)
            for ri in range(2):
                sp.wait_ge(o_out[ri], 16 * STEPS)

        @block.scalar
        def _(act):
            for i in range(2 * DK):
                if i == 0:
                    act.wait_ge(s_in[0], 16)
                    act.activation(s_hi[:, 0], s_raw[:, :, :], ACT.Copy).then_inc(s_hi_done[0], 1)
                if i == DK:
                    act.wait_ge(s_in[1], 16)
                    act.activation(s_hi[:, 1], s_raw[:, :, :], ACT.Copy).then_inc(s_hi_done[1], 1)
                act.wait_ge(w_in[i % 4], 16 * (i // 4) + 16)
                act.activation(w_hi[:, i // DK, i % DK, :], raw_w(i), ACT.Copy).then_inc(w_hi_done, 1)
            act.wait_ge(bias_in, 32)
            act.wait_ge(eps_set, 1)

            def next_s_hi(tile, ri, u):
                act.wait_ge(s_in[ri], 16 * tile + 32)
                act.wait_ge(acc_done, u * 8 + (ri * 4 + 4))
                act.activation(s_hi[:, ri], s_raw[:, :, :], ACT.Copy).then_inc(s_hi_done[ri], 1)

            def guarded(tile, fn):
                if isinstance(tile, int):
                    fn()
                else:
                    with act.If(tile < TILES - 1):
                        fn()

            def root(v, s):
                act.wait_ge(chain, v * 9 + 4)
                act.activation(soft[:, s, :], soft[:, s, :], ACT.Sqrt, scale=SCALE2, bias=mag_eps[:, 0:1]
                               ).then_inc(mag_done, 1)

            def expo(v, s):
                act.wait_ge(chain, v * 9 + 6)
                act.activation(soft[:, s, :], soft[:, s, :], ACT.Exp).then_inc(exp_done, 1)

            def weighted_imag(v, hp, ns):
                if ns[0] == 0:
                    act.wait_ge(chain, v * 9 + 9)
                    act.wait_ge(v_out, v * 8 + 16)
                    if not (isinstance(v, int) and v == 0):
                        act.wait_ge(pv_red[1], v)
                for n in ns:
                    for m in range(N):
                        for h in range(2):
                            at = m * P + h * HD
                            w = n * 2 * N + m * 2 + h
                            ins = act.activation(prod[:, 2, n * 512 + at:n * 512 + at + HD],
                                                 vals[:, hp, 1, m, h * HD:(h + 1) * HD], ACT.Copy,
                                                 scale=soft[:, hp % 2, w:w + 1])
                    ins.then_inc(pv_done[1], 1)

            def v_read(u, hp, ri, wait):
                if wait:
                    act.wait_ge(pv_done[ri], u * 4 - 12)
                for n in range(N):
                    act.wait_ge(qk_out, u * 8 + (ri * 4 + n + 5))
                    ins = act.activation(vals[:, hp, ri, n, :], acc[ri][n][:, 2 * P:3 * P], ACT.Copy)
                    if isinstance(u, int) and u < LAG:
                        ins.then_inc(v_out, 1)
                    else:
                        if n == 0:
                            act.wait_ge(o_out[ri], (u - LAG) * 16)
                        col_read(ri, n, (hp - LAG) % HP)

            def col_read(ri, n, hp):
                act.activation(o_col[:, ri, n * P:(n + 1) * P], acc[ri][n][:, QKV:QKV + P], ACT.Identity,
                               bias=v_cols[:, ri, hp:hp + 1]).then_inc(v_out, 1)

            def tile_body(tile):
                for hp in range(HP):
                    u = tile * HP + hp
                    v_read(u, hp, 1, exists(tile, hp, HP))
                    if hp == HP - 1:
                        guarded(tile, lambda: next_s_hi(tile, 1, u))
                    if exists(tile, hp, 1):
                        root(tile * HP + (hp - 1), 1 - hp % 2)
                    if exists(tile, hp, 1):
                        expo(tile * HP + (hp - 1), 1 - hp % 2)
                    if hp == HP - 2:
                        guarded(tile, lambda: next_s_hi(tile, 0, tile * HP + (HP - 1)))
                    if exists(tile, hp, 1):
                        weighted_imag(tile * HP + (hp - 1), (hp - 1) % HP, (0, 1))
                    if hp == HP - 1:
                        guarded(tile, lambda: v_read(tile * HP + HP, 0, 0, True))
                    else:
                        v_read(tile * HP + (hp + 1), hp + 1, 0, exists(tile, hp + 1, HP))
                    if exists(tile, hp, 1):
                        weighted_imag(tile * HP + (hp - 1), (hp - 1) % HP, (2, 3))
            v_read(0, 0, 0, False)
            tiles(act, tile_body)
            root(STEPS - 1, 1)
            expo(STEPS - 1, 1)
            weighted_imag(STEPS - 1, HP - 1, range(N))
            for v in range(STEPS - LAG, STEPS):
                for ri in range(2):
                    act.wait_ge(o_out[ri], v * 16)
                    for n in range(N):
                        act.wait_ge(acc_done, (v + LAG) * 8 + (ri * 4 + n + 1))
                        col_read(ri, n, v % HP)

        @block.tensor
        def _(pe):
            pe.wait_ge(w_lo_done, 1)

            def turn_out(v, s, ri, n):
                if n == 0:
                    pe.wait_ge(pv_red[ri], v + 1)
                return pe.transpose(acc[ri][n][:, QKV:QKV + P], o_row[:, s, ri, n, :], ident)

            def tile_body(tile):
                for hp in range(HP):
                    u = tile * HP + hp
                    for ri in range(2):
                        if hp == 0:
                            pe.wait_ge(s_lo_done[ri], tile + 1)
                        for n in range(N):
                            pe.wait_ge(v_out, u * 8 + (ri * 4 + n + 1))
                            for k in range(DK):
                                if isinstance(tile, int) and hp == 0 and n == 0:
                                    pe.wait_ge(w_lo_done, ri * DK + k + 1)
                                m_hi = w_hi[:, ri, k, hp * QKV:(hp + 1) * QKV]
                                m_lo = w_lo[:, ri, k, hp * QKV:(hp + 1) * QKV]
                                t_hi, t_lo = s_hi[:, ri, n * DK + k, :], s_lo[:, ri, n * DK + k, :]
                                pe.matmul(acc[ri][n][:, 0:QKV], t_hi, m_hi, start=(k == 0), stop=False)
                                pe.matmul(acc[ri][n][:, 0:QKV], t_hi, m_lo, start=False, stop=False)
                                mm = pe.matmul(acc[ri][n][:, 0:QKV], t_lo, m_hi, start=False, stop=(k == DK - 1))
                            if exists(tile, hp, LAG):
                                mm = turn_out(tile * HP + (hp - LAG), (hp - LAG) % 2, ri, n)
                            mm.then_inc(acc_done, 1)
            tiles(pe, tile_body)
            for v in range(STEPS - LAG, STEPS):
                for ri in range(2):
                    for n in range(N):
                        pe.wait_ge(v_out, (v + LAG) * 8 + (ri * 4 + n + 1))
                        turn_out(v, v % 2, ri, n).then_inc(acc_done, 1)

        @block.gpsimd
        def _(pool):
            pool.memset(mag_eps[:, :], 1e-8 * SCALE2).then_inc(eps_set, 1)
            pool.wait_ge(w_lo_done, 2 * DK)

            def scores(u, s, c, wait):
                if c == 0:
                    pool.wait_ge(comb_done, u * 3 + 3)
                    if wait:
                        pool.wait_ge(qk_red, summed(u - 1, 2))
                elif c == 1:
                    if wait:
                        pool.wait_ge(pv_red[0], u - 1)
                else:
                    pool.wait_ge(qk_red, summed(u, 0))
                for n in range(OWN if c == 2 else N):
                    score_product(pool, s, c, n).then_inc(qkp_done, 1)

            def weighted(v, hp, last):
                pool.wait_ge(chain, v * 9 + 9)
                if last:
                    pool.wait_ge(pv_red[0], v)
                else:
                    pool.wait_ge(qk_red, summed(v + 1, 1))
                pool.wait_ge(v_out, v * 8 + 12)
                for n in range(N):
                    pool.tensor_tensor(
                        prod[:, 1, n * 512:(n + 1) * 512].rearrange("p (g f) -> p g f", f=HD),
                        soft[:, hp % 2, n * 8:(n + 1) * 8].unsqueeze(2).broadcast_to([P, 8, HD]),
                        vals[:, hp, 0, :, :].rearrange("p m (h f) -> p (m h) f", f=HD), ALU.mult
                        ).then_inc(pv_done[0], 1)

            def tile_body(tile):
                for hp in range(HP):
                    u = tile * HP + hp
                    scores(u, hp % 2, 0, exists(tile, hp, 1))
                    scores(u, hp % 2, 1, exists(tile, hp, 2))
                    scores(u, hp % 2, 2, True)
                    if exists(tile, hp, 1):
                        weighted(tile * HP + (hp - 1), (hp - 1) % HP, False)
            tiles(pool, tile_body)
            weighted(STEPS - 1, HP - 1, True)

        @block.vector
        def _(dve):
            dve.sem_inc(qk_out, 4)
            dve.sem_inc(v_out, 8)
            for i in range(2 * DK):
                if i % DK == 0:
                    ri = i // DK
                    dve.wait_ge(s_hi_done[ri], 1)
                    dve.tensor_tensor(s_lo[:, ri], s_raw[:, :, :], s_hi[:, ri], ALU.subtract
                                      ).then_inc(s_lo_done[ri], 1)
                dve.wait_ge(w_hi_done, i + 1)
                dve.tensor_tensor(w_lo[:, i // DK, i % DK, :], raw_w(i), w_hi[:, i // DK, i % DK, :],
                                  ALU.subtract).then_inc(w_lo_done, 1)
            dve.wait_ge(bias_in, 32)
            dve.wait_ge(w_lo_done, 2 * DK)

            def link(v, i, ins):
                ins.then_inc(chain, 1)
                if i not in (4, 6, 9):
                    dve.wait_ge(chain, v * 9 + i)

            def nmh(x):
                return x.rearrange("p (n m h) -> p n m h", n=N, m=N)

            def nhm(x):
                return x.rearrange("p (n m h) -> p n h m", n=N, m=N)

            def over_m(x):
                return x.rearrange("p (n h) -> p n h", n=N).unsqueeze(2).broadcast_to([P, N, N, 2])

            def chain_a(v, s):
                dve.wait_ge(qk_red, v * 3 + 3)
                link(v, 1, dve.tensor_tensor(sums[:, 1, :], sums[:, 0, :], sums[:, 1, :], ALU.subtract))
                link(v, 2, dve.tensor_tensor(sums[:, 2, :], sums[:, 0, :], sums[:, 2, :], ALU.subtract))
                link(v, 3, dve.tensor_tensor(sums[:, 1:3, :], sums[:, 1:3, :], sums[:, 1:3, :], ALU.mult))
                link(v, 4, dve.tensor_tensor(soft[:, s, :], sums[:, 1, :], sums[:, 2, :], ALU.add))

            def chain_b(v, s):
                dve.wait_ge(mag_done, v + 1)
                link(v, 5, dve.tensor_reduce(top[:, s, :].rearrange("p (n h) -> p n h", n=N), nhm(soft[:, s, :]),
                                             AX.X, ALU.max))
                link(v, 6, dve.tensor_tensor(nmh(soft[:, s, :]), nmh(soft[:, s, :]), over_m(top[:, s, :]),
                                             ALU.subtract))

            def chain_c(v, s):
                dve.wait_ge(exp_done, v + 1)
                link(v, 7, dve.tensor_reduce(den[:, s, :].rearrange("p (n h) -> p n h", n=N), nhm(soft[:, s, :]),
                                             AX.X, ALU.add))
                link(v, 8, dve.reciprocal(rden[:, s, :], den[:, s, :]))
                link(v, 9, dve.tensor_tensor(nmh(soft[:, s, :]), nmh(soft[:, s, :]), over_m(rden[:, s, :]), ALU.mult))

            def weighted_sum(v, s, ri):
                dve.wait_ge(pv_done[ri], v * 4 + 4)
                if not (isinstance(v, int) and v < 2):
                    dve.wait_ge(acc_done, v * 8 + (8 * (LAG - 2) + 8))
                dve.tensor_reduce(o_row[:, s, ri, :, :], prod[:, 1 + ri, :].rearrange(
                    "p (n m f) -> p n f m", n=N, m=N), AX.X, ALU.add).then_inc(pv_red[ri], 1)

            def qk_read(u, hp, ri):
                for n in range(N):
                    dve.wait_ge(acc_done, u * 8 + (ri * 4 + n + 1))
                    dve.tensor_tensor(qk[:, hp % 2, ri, :, n, :],
                                      acc[ri][n][:, 0:2 * P].rearrange("p (a f) -> p a f", a=2),
                                      qk_bias[:, ri, hp, :].rearrange("p (a f) -> p a f", a=2),
                                      ALU.add).then_inc(qk_out, 1)

            def next_s_lo(tile, ri):
                dve.wait_ge(s_hi_done[ri], tile + 2)
                dve.tensor_tensor(s_lo[:, ri], s_raw[:, :, :], s_hi[:, ri], ALU.subtract).then_inc(s_lo_done[ri], 1)

            def guarded(tile, fn):
                if isinstance(tile, int):
                    fn()
                else:
                    with dve.If(tile < TILES - 1):
                        fn()

            def combine(u, s):
                dve.wait_ge(qk_out, u * 8 + 12)
                qr, qi, kr, ki = qk[:, s, 0, 0], qk[:, s, 1, 0], qk[:, s, 0, 1], qk[:, s, 1, 1]
                dve.tensor_tensor(comb[:, s, 1], kr, ki, ALU.subtract).then_inc(comb_done, 1)
                dve.tensor_tensor(comb[:, s, 0], qr, qi, ALU.add).then_inc(comb_done, 1)
                dve.wait_ge(comb_done, u * 3 + 1)
                dve.tensor_tensor(ki, kr, ki, ALU.add).then_inc(comb_done, 1)

            def own_product(u, s):
                dve.wait_ge(comb_done, u * 3 + 3)
                dve.wait_ge(qk_red, summed(u, 0))
                for n in range(OWN, N):
                    score_product(dve, s, 2, n).then_inc(qkp_own, 1)

            def score_sum(u, c):
                dve.wait_ge(qkp_done, u * (2 * N + OWN) + (2 * N + OWN if c == 2 else 4 * c + 4))
                if c == 2:
                    dve.wait_ge(qkp_own, u + 1)
                dve.tensor_reduce(sums[:, c, :], prod[:, SLOT[c], :].rearrange("p (g f) -> p g f", f=HD),
                                  AX.X, ALU.add).then_inc(qk_red, 1)

            def tile_body(tile):
                for hp in range(HP):
                    u = tile * HP + hp
                    s = hp % 2
                    if exists(tile, hp, 2):
                        weighted_sum(tile * HP + (hp - 2), s, 0)
                    if hp == HP - 1:
                        guarded(tile, lambda: next_s_lo(tile, 1))
                    if exists(tile, hp, 1):
                        chain_b(tile * HP + (hp - 1), 1 - s)
                    if exists(tile, hp, 2):
                        weighted_sum(tile * HP + (hp - 2), s, 1)
                    if exists(tile, hp, 1):
                        chain_c(tile * HP + (hp - 1), 1 - s)
                    score_sum(u, 0)
                    own_product(u, s)
                    if hp == HP - 1:
                        guarded(tile, lambda: qk_read(tile * HP + HP, 0, 0))
                    else:
                        qk_read(tile * HP + (hp + 1), hp + 1, 0)
                    score_sum(u, 1)
                    if hp == HP - 2:
                        guarded(tile, lambda: next_s_lo(tile, 0))
                    if hp == HP - 1:
                        guarded(tile, lambda: qk_read(tile * HP + HP, 0, 1))
                        guarded(tile, lambda: combine(tile * HP + HP, 0))
                    else:
                        qk_read(tile * HP + (hp + 1), hp + 1, 1)
                        combine(tile * HP + (hp + 1), 1 - s)
                    score_sum(u, 2)
                    chain_a(u, s)
            qk_read(0, 0, 0)
            qk_read(0, 0, 1)
            combine(0, 0)
            tiles(dve, tile_body)
            chain_b(STEPS - 1, 1)
            chain_c(STEPS - 1, 1)
            weighted_sum(STEPS - 2, 0, 0)
            weighted_sum(STEPS - 2, 0, 1)
            weighted_sum(STEPS - 1, 1, 0)
            weighted_sum(STEPS - 1, 1, 1)


def project_stage(nc, ctx, dram, consts):
    def sb(name, shape, dt=F32):
        return ctx.enter_context(nc.sbuf_tensor(name, shape, dt))

    def sem(name):
        return ctx.enter_context(nc.semaphore(name))

    w_raw = sb("wo_raw", [P, 2, DK, D])
    w_hi, w_lo = sb("wo_hi", [P, 2, DK, D], F32R), sb("wo_lo", [P, 2, DK, D], F32R)
    bo = sb("bo_cols_sb", [P, 2, DK])
    o_raw = sb("o_raw", [P, 2, DK, N * P])
    o_hi, o_lo = sb("o_hi", [P, 2, DK, N * P], F32R), sb("o_lo", [P, 2, DK, N * P], F32R)
    a_out = sb("a_out", [P, 2, 2, N, DK, P], F32R)
    acc = [[ctx.enter_context(nc.psum_tensor(f"wo_acc{ri}{j}", [P, 512], F32)) for j in range(DK)] for ri in range(2)]

    w_in, w_hi_done, w_lo_done = [[sem(f"wo_{x}{ri}") for ri in range(2)] for x in ("in", "hi", "lo")]
    o_in, o_hi_done, o_lo_done = [[sem(f"o_{x}{ri}") for ri in range(2)] for x in ("in", "hi_done", "lo_done")]
    bo_in = sem("bo_in")
    passed = consts["passed"]
    acc_done, read_out = [[sem(f"wo_{x}{ri}") for ri in range(2)] for x in ("acc", "read")]
    a_hi_out = [sem("a_hi_out_r"), sem("a_hi_out_i")]
    a_stored = [sem("a_stored_r"), sem("a_stored_i")]

    with nc.Block() as block:

        @block.sync
        def _(sp):
            def load(tile, ri):
                sp.dma_start(o_raw[:, ri], dram["o_t"][ri, bass.ds(tile * HP, HP)].rearrange("k p f -> p k f")
                             ).then_inc(o_in[ri], 16)

            for ri in range(2):
                sp.dma_start(w_raw[:, ri], dram["wo_w"][ri]).then_inc(w_in[ri], 16)
                load(0, ri)
            sp.dma_start(bo[:, :, :], dram["bo_cols"]).then_inc(bo_in, 16)
            with sp.Fori(0, TILES - 1) as tile:
                for ri in range(2):
                    sp.wait_ge(o_lo_done[ri], tile + 1)
                    load(tile + 1, ri)

        @block.gpsimd
        def _(pool):
            def store(tile, ri):
                wait_apart(pool, read_out[ri], tile * DK + DK, passed)
                for part in range(2):
                    pool.dma_start(dram["a_t"][bass.ds(tile, 1), :, :, part, ri, :].rearrange("o n p f -> (o p) n f"),
                                 a_out[:, ri, part].rearrange("p n k b -> p n (k b)").bitcast(F32)).then_inc(a_stored[ri], 16)

            with pool.Fori(0, TILES) as tile:
                for ri in range(2):
                    store(tile, ri)
            for ri in range(2):
                pool.wait_ge(a_stored[ri], 32 * TILES)

        @block.scalar
        def _(act):
            def split_high(tile, ri, first=False):
                act.wait_ge(o_in[ri], tile * 16 + 16)
                if not first:
                    act.wait_ge(acc_done[ri], tile * DK)
                act.activation(o_hi[:, ri], o_raw[:, ri], ACT.Copy).then_inc(o_hi_done[ri], 1)

            def read(tile, ri):
                act.wait_ge(a_stored[ri], tile * 32)
                for j in range(DK):
                    act.wait_ge(acc_done[ri], tile * DK + j + 1)
                    act.activation(a_out[:, ri, 0, :, j, :], acc[ri][j][:, :].rearrange("p (n b) -> p n b", n=N),
                                   ACT.Identity, bias=bo[:, ri, j:j + 1]).then_inc(a_hi_out[ri], 1)

            for ri in range(2):
                act.wait_ge(w_in[ri], 16)
                act.activation(w_hi[:, ri], w_raw[:, ri], ACT.Copy).then_inc(w_hi_done[ri], 1)
                split_high(0, ri, True)
            act.wait_ge(bo_in, 16)
            with act.Fori(0, TILES - 1) as tile:
                for ri in range(2):
                    split_high(tile + 1, ri)
                    read(tile, ri)
            for ri in range(2):
                read(TILES - 1, ri)

        @block.tensor
        def _(pe):
            with pe.Fori(0, TILES) as tile:
                for ri in range(2):
                    pe.wait_ge(w_lo_done[ri], 1)
                    pe.wait_ge(o_lo_done[ri], tile + 1)
                    pe.wait_ge(read_out[ri], tile * DK)
                    for j in range(DK):
                        for k in range(DK):
                            s_hi, s_lo = w_hi[:, ri, k, j * P:(j + 1) * P], w_lo[:, ri, k, j * P:(j + 1) * P]
                            m_hi, m_lo = o_hi[:, ri, k, :], o_lo[:, ri, k, :]
                            pe.matmul(acc[ri][j][:, :], s_hi, m_hi, start=(k == 0), stop=False)
                            pe.matmul(acc[ri][j][:, :], s_hi, m_lo, start=False, stop=False)
                            mm = pe.matmul(acc[ri][j][:, :], s_lo, m_hi, start=False, stop=(k == DK - 1))
                        mm.then_inc(acc_done[ri], 1)

        @block.vector
        def _(dve):
            def split_low(tile, ri):
                dve.wait_ge(o_hi_done[ri], tile + 1)
                dve.tensor_tensor(o_lo[:, ri], o_raw[:, ri], o_hi[:, ri], ALU.subtract).then_inc(o_lo_done[ri], 1)

            for ri in range(2):
                dve.wait_ge(w_hi_done[ri], 1)
                dve.tensor_tensor(w_lo[:, ri], w_raw[:, ri], w_hi[:, ri], ALU.subtract).then_inc(w_lo_done[ri], 1)
                split_low(0, ri)
            dve.wait_ge(bo_in, 16)

            def read_low(tile, ri):
                for j in range(DK):
                    wait_apart(dve, a_hi_out[ri], tile * DK + j + 1, passed)
                    dve.scalar_tensor_tensor(out=a_out[:, ri, 1, :, j, :],
                                             in0=acc[ri][j][:, :].rearrange("p (n b) -> p n b", n=N),
                                             scalar=bo[:, ri, j:j + 1], in1=a_out[:, ri, 0, :, j, :],
                                             op0=ALU.add, op1=ALU.subtract).then_inc(read_out[ri], 1)

            with dve.Fori(0, TILES - 1) as tile:
                for ri in range(2):
                    split_low(tile + 1, ri)
                    read_low(tile, ri)
            for ri in range(2):
                read_low(TILES - 1, ri)


def interact_stage(nc, ctx, dram, consts):
    def sb(name, shape, dt=F32):
        return ctx.enter_context(nc.sbuf_tensor(name, shape, dt))

    def sem(name):
        return ctx.enter_context(nc.semaphore(name))

    H = D // 2
    WPIECES = 2 * N
    w_hi, w_lo = sb("int_hi", [P, N, 2, DK, D], F32R), sb("int_lo", [P, N, 2, DK, D], F32R)
    a_in_sb = sb("a_in_sb", [P, 2, 2, 2, DK * P], F32R)
    ri_rows = sb("ri_rows", [P, 2, 2, N, D])
    r2 = sb("r2", [P, 2, D])
    cos, sin = sb("cos", [P, N, H]), sb("sin", [P, N, H])
    zero = sb("zero", [P, N, H])
    x = [sb(f"x{h}", [P, N, H]) for h in range(2)]
    y = sb("y_sq", [P, N, H])
    q = sb("q", [P, N, H])
    tt = sb("tt", [P, N, H])
    sup = sb("sup", [P, 2, D])
    norm = sb("norm", [P, 4])
    neg_half = sb("neg_half2", [P, 1])
    ids = sb("ids_sb", [P, TILES, N], I32)
    strength = sb("strength", [P, TILES, N * N])
    strength_t = sb("strength_t", [P, 2, N * N])
    tiny = sb("tiny", [P, 1])
    acc_r1, acc_r2, acc_i = [[ctx.enter_context(nc.psum_tensor(f"{x_}{s}", [P, D], F32)) for s in range(2)]
                             for x_ in ("acc_r1", "acc_r2", "acc_i")]

    w_in = [sem(f"int_in{i}") for i in range(2)]
    w_hi_done, w_lo_done = sem("int_hi_done"), sem("int_lo_done")
    ids_in, strength_in = sem("ids_in"), sem("strength_in")
    const_set = sem("const_set")
    a_in = [sem("a_in0"), sem("a_in1")]
    r2_done, r1_done, i_done = sem("r2_done"), sem("r1_done"), sem("i_done")
    r2_out = sem("r2_out")
    r_out, i_out = sem("r_out"), sem("i_out")
    squared = sem("squared")
    summed = sem("summed")
    log_done = sem("log_done")
    inv_done = sem("inv_done")
    strength_now = sem("strength_now")
    cos_done, sin_done, zero_done = sem("cos_done"), sem("sin_done"), sem("zero_done")
    t_first, t_steps = sem("t_first"), sem("t_steps")
    p_steps, q_terms = sem("p_steps"), sem("q_terms")
    q_steps = sem("q_steps")
    cp_done = sem("cp_done")
    pt_done = sem("pt_done")
    f_done = sem("f_done")
    fr_done, fi_done = sem("fr_done"), sem("fi_done")
    red_done = sem("red_done")
    norm_steps = sem("norm_steps")
    rnorm_done = sem("rnorm_done")
    sup_ready = sem("sup_ready")
    sup_stored = sem("sup_stored")
    passed = consts["passed"]

    def raw_w(i):
        return ri_rows[:, 1, i % 2, :, :]

    def run(eng, invert, gather, fold, unit, begin=None, close=None):
        def body(tile, s, one, two):
            for n in range(N):
                if begin is not None:
                    begin(tile, s, n)
                if n % 2 == 0 and one:
                    invert(tile - 1, 1 - s, n // 2)
                    if n == 2:
                        fold(tile - 1, 1 - s, 0)
                    elif two:
                        fold(tile - 2, s, 1)
                if n % 2 == 1 and one:
                    gather(tile - 1, 1 - s, n // 2)
                unit(tile, s, n)
                if n % 2 == 1 and one and close is not None:
                    close(tile - 1, 1 - s, n // 2)
        body(0, 0, False, False)
        body(1, 1, True, False)
        with eng.Fori(1, TILES // 2) as pair:
            for s in range(2):
                body(pair * 2 + s, s, True, True)
        invert(TILES - 1, 1, 0)
        fold(TILES - 2, 0, 1)
        gather(TILES - 1, 1, 0)
        if close is not None:
            close(TILES - 1, 1, 0)
        invert(TILES - 1, 1, 1)
        fold(TILES - 1, 1, 0)
        gather(TILES - 1, 1, 1)
        if close is not None:
            close(TILES - 1, 1, 1)
        fold(TILES - 1, 1, 1)

    def others(j):
        return [i for i in range(N) if i != j]

    def s_col(s, i, j):
        return strength_t[:, s, i * N + j:i * N + j + 1]

    def half_rows(s, ri, h):
        return ri_rows[:, s, ri, :, h * H:(h + 1) * H]

    with nc.Block() as block:

        @block.sync
        def _(sp):
            sp.dma_start(ids[:, :, :], dram["ids"]).then_inc(ids_in, 16)
            sp.dma_start(raw_w(0), dram["int_w"][0]).then_inc(w_in[0], 16)
            for i in range(1, WPIECES):
                if i >= 2:
                    sp.wait_ge(w_lo_done, i - 1)
                sp.dma_start(raw_w(i), dram["int_w"][i]).then_inc(w_in[i % 2], 16)

            def store(tile):
                sp.wait_ge(sup_ready, tile + 1)
                sp.dma_start(dram["sup_d"][bass.ds(tile, 1)].rearrange("o p r f -> (o p) r f"), sup[:, :, :]
                             ).then_inc(sup_stored, 16)

            with sp.Fori(0, TILES) as tile:
                store(tile)
            sp.wait_ge(sup_stored, 16 * TILES)

        @block.scalar
        def _(act):
            def split(n):
                for i in (2 * n, 2 * n + 1):
                    act.wait_ge(w_in[i % 2], 16 * (i // 2) + 16)
                    act.activation(w_hi[:, n, i % 2], raw_w(i), ACT.Copy).then_inc(w_hi_done, 1)

            def invert(tile, s, h):
                v = tile * 2 + h
                if h == 0:
                    act.wait_ge(r_out, tile * N + N + 2)
                    act.wait_ge(i_out, tile * N + N + 2)
                if not (isinstance(tile, int) and tile == 0):
                    act.wait_ge(fr_done, v - 1)
                    act.wait_ge(fi_done, v - 1)
                act.activation(x[h][:, :, :], half_rows(s, 0, h), ACT.Square).then_inc(squared, 1)
                if not (isinstance(tile, int) and v == 0):
                    act.wait_ge(q_steps, v * 3 - 2)
                act.activation(y[:, :, :], half_rows(s, 1, h), ACT.Square).then_inc(squared, 1)
                act.wait_ge(summed, v + 1)
                act.activation(x[h][:, :, :], x[h][:, :, :], ACT.Ln, bias=tiny[:, 0:1]).then_inc(log_done, 1)
                act.wait_ge(log_done, v + 1)
                act.activation(x[h][:, :, :], x[h][:, :, :], ACT.Exp, scale=-0.5).then_inc(inv_done, 1)

            def square(tile):
                act.wait_ge(red_done, tile * 4 + 4)
                act.activation(q[:, :, :].rearrange("p n f -> p (n f)"),
                               sup[:, :, :].rearrange("p r f -> p (r f)"), ACT.Square).then_inc(norm_steps, 1)

            def gather(tile, s, h):
                v = tile * 2 + h
                if h == 0 and not (isinstance(tile, int) and tile == 0):
                    square(tile - 1)
                act.wait_ge(strength_now, tile + 1)
                act.wait_ge(zero_done, v + 1)
                act.wait_ge(red_done, v * 2)
                for j in range(N):
                    i = others(j)[0]
                    act.activation(tt[:, j, :], zero[:, i, :], ACT.Identity, scale=s_col(s, i, j),
                                   bias=s_col(s, j, j)).then_inc(t_first, 1)
                act.wait_ge(sin_done, v + 1)
                for place, m in ((q, 0), (y, 1), (zero, 2)):
                    if m == 0 and h == 0 and not (isinstance(tile, int) and tile == 0):
                        act.wait_ge(norm_steps, tile * 3 - 1)
                    if m == 2:
                        act.wait_ge(t_steps, v * 8 + 8)
                    for j in range(N):
                        i = others(j)[m]
                        act.activation(place[:, j, :], sin[:, i, :], ACT.Copy, scale=s_col(s, i, j)
                                       ).then_inc(q_terms, 1)

            def unit(tile, s, n):
                g = tile * N + n
                if isinstance(tile, int) and tile == 0 and n < N - 1:
                    split(n + 1)
                act.wait_ge(r2_done, g + 1)
                act.wait_ge(r_out, g + 1)
                act.activation(r2[:, n % 2, :], acc_r2[n % 2][:, :], ACT.Copy).then_inc(r2_out, 1)
                act.wait_ge(i_done, g + 1)
                if n == 0:
                    if isinstance(tile, int):
                        if tile == 1:
                            act.wait_ge(w_lo_done, WPIECES)
                    else:
                        act.wait_ge(fi_done, tile * 2 - 2)
                act.activation(ri_rows[:, s, 1, n, :], acc_i[n % 2][:, :], ACT.Copy).then_inc(i_out, 1)

            act.wait_ge(const_set, 2)
            split(0)
            run(act, invert, gather, lambda tile, s, h: None, unit)
            square(TILES - 1)

        @block.tensor
        def _(pe):
            def unit(tile, n, first):
                g = tile * N + n
                s = n % 2
                if first:
                    pe.wait_ge(w_lo_done, 2 * n + 1)
                pe.wait_ge(a_in[s], tile * 32 + 16 * (n // 2) + 16)
                pe.wait_ge(r_out, g + 1)
                pe.wait_ge(i_out, g + 1)
                r2, r1, i = ((acc_r2[s], ((1, 1),), r2_done), (acc_r1[s], ((0, 0),), r1_done),
                             (acc_i[s], ((0, 1), (1, 0)), i_done))
                for bank, parts, done in (r1, r2, i) if first else (r2, r1, i):
                    if first and done is r2_done:
                        pe.wait_ge(w_lo_done, 2 * n + 2)
                    for ai_, wi in parts:
                        for k in range(DK):
                            s_hi, s_lo = [a_in_sb[:, s, c, ai_, k * P:(k + 1) * P] for c in range(2)]
                            m_hi, m_lo = w_hi[:, n, wi, k, :], w_lo[:, n, wi, k, :]
                            start = k == 0 and (ai_, wi) == parts[0]
                            stop = k == DK - 1 and (ai_, wi) == parts[-1]
                            pe.matmul(bank[:, :], s_hi, m_hi, start=start, stop=False)
                            pe.matmul(bank[:, :], s_hi, m_lo, start=False, stop=False)
                            mm = pe.matmul(bank[:, :], s_lo, m_hi, start=False, stop=stop)
                    mm.then_inc(done, 1)

            for n in range(N):
                unit(0, n, True)
            with pe.Fori(1, TILES) as tile:
                for n in range(N):
                    unit(tile, n, False)

        @block.gpsimd
        def _(pool):
            pool.memset(neg_half[:, :], -0.5).then_inc(const_set, 1)
            pool.memset(tiny[:, :], TINY).then_inc(const_set, 1)
            def load(tile, n):
                pool.dma_start(a_in_sb[:, n % 2].rearrange("p c r f -> p (c r f)"),
                               dram["a_t"][bass.ds(tile, 1), n].rearrange("o p c r f -> (o p) (c r f)")
                               ).then_inc(a_in[n % 2], 16)

            load(0, 0)
            pool.wait_ge(const_set, 2)
            pool.wait_ge(ids_in, 16)

            def look_up(t):
                for f in range(N):
                    pool.indirect_dma_start(
                        out=strength[:, t, f * N:(f + 1) * N], out_offset=None, in_=dram[f"tbl_{f}"],
                        in_offset=bass.IndirectOffsetOnAxis(ap=ids[:, t, f:f + 1], axis=0)).then_inc(strength_in, 16)

            def root(tile):
                pool.wait_ge(norm_steps, tile * 3 + 3)
                pool.tensor_tensor(norm[:, 2:3], norm[:, 1:2], neg_half[:, 0:1], ALU.pow).then_inc(rnorm_done, 1)

            def gather(tile, s, h):
                v = tile * 2 + h
                pool.wait_ge(inv_done, v + 1)
                pool.tensor_tensor(sin[:, :, :], half_rows(s, 1, h), x[h][:, :, :], ALU.mult).then_inc(sin_done, 1)
                if h == 0 and not (isinstance(tile, int) and tile == 0):
                    root(tile - 1)
                for m, term in ((1, y), (2, zero)):
                    pool.wait_ge(q_terms, v * 12 + (m * 4 + 4))
                    pool.tensor_tensor(q[:, :, :], q[:, :, :], term[:, :, :], ALU.add).then_inc(q_steps, 1)
                    pool.wait_ge(q_steps, v * 3 + m)
                pool.tensor_tensor(q[:, :, :], sin[:, :, :], q[:, :, :], ALU.mult).then_inc(q_steps, 1)

            def fold(tile, s, h):
                v = tile * 2 + h
                pool.wait_ge(f_done, v + 1)
                pool.tensor_tensor(q[:, :, :], half_rows(s, 1, h), x[h][:, :, :], ALU.mult).then_inc(fi_done, 1)

            def begin(tile, s, n):
                if not (isinstance(tile, int) and tile + n == 0):
                    wait_apart(pool, i_done, tile * N + n, passed)
                if n < N - 1:
                    load(tile, n + 1)
                elif isinstance(tile, int) or s == 0:
                    load(tile + 1, 0)
                else:
                    with pool.If(tile < TILES - 1):
                        load(tile + 1, 0)
                if isinstance(tile, int) and tile == 0:
                    for t in range(n * TILES // N, (n + 1) * TILES // N):
                        look_up(t)

            run(pool, lambda tile, s, h: None, gather, fold, lambda tile, s, n: None, begin)
            root(TILES - 1)

        @block.vector
        def _(dve):
            dve.sem_inc(r_out, 2)
            dve.sem_inc(i_out, 2)

            def split(n):
                for i in (2 * n, 2 * n + 1):
                    dve.wait_ge(w_hi_done, i + 1)
                    dve.tensor_tensor(w_lo[:, n, i % 2], raw_w(i), w_hi[:, n, i % 2], ALU.subtract
                                      ).then_inc(w_lo_done, 1)

            split(0)

            def unit(tile, s, n):
                g = tile * N + n
                if isinstance(tile, int) and tile == 0 and n < N - 1:
                    split(n + 1)
                if isinstance(tile, int) and tile == 1 and n == 0:
                    dve.wait_ge(w_lo_done, WPIECES)
                dve.wait_ge(r2_out, g + 1)
                dve.wait_ge(r1_done, g + 1)
                dve.tensor_tensor(ri_rows[:, s, 0, n, :], acc_r1[n % 2][:, :], r2[:, n % 2, :], ALU.subtract
                                  ).then_inc(r_out, 1)

            def invert(tile, s, h):
                v = tile * 2 + h
                dve.wait_ge(squared, v * 2 + 2)
                dve.tensor_tensor(x[h][:, :, :], x[h][:, :, :], y[:, :, :], ALU.add).then_inc(summed, 1)

            def squared_norm(tile):
                dve.wait_ge(norm_steps, tile * 3 + 1)
                dve.tensor_reduce(norm[:, 0:1], q[:, :, :].rearrange("p n f -> p (n f)"), AX.X, ALU.add
                                  ).then_inc(norm_steps, 1)
                dve.wait_ge(norm_steps, tile * 3 + 2)
                dve.tensor_scalar(norm[:, 1:2], norm[:, 0:1], 1e-8, None, ALU.add).then_inc(norm_steps, 1)

            def normalise(tile):
                dve.wait_ge(rnorm_done, tile + 1)
                dve.tensor_scalar(sup[:, :, :], sup[:, :, :], norm[:, 2:3], None, ALU.mult).then_inc(sup_ready, 1)

            def gather(tile, s, h):
                v = tile * 2 + h
                norm_here = h == 0 and not (isinstance(tile, int) and tile == 0)
                if h == 0:
                    if isinstance(tile, int) and tile == 0:
                        dve.wait_ge(strength_in, 16 * TILES * N)
                    dve.tensor_copy(strength_t[:, s, :], strength[:, bass.ds(tile, 1), :].rearrange("p o f -> p (o f)")
                                    ).then_inc(strength_now, 1)
                dve.wait_ge(inv_done, v + 1)
                wait_apart(dve, q_steps, v * 3, passed)
                dve.tensor_scalar(zero[:, :, :], x[h][:, :, :], ZERO_ABOVE, None, ALU.is_gt).then_inc(zero_done, 1)
                dve.tensor_tensor(cos[:, :, :], half_rows(s, 0, h), x[h][:, :, :], ALU.mult).then_inc(cos_done, 1)
                if norm_here:
                    squared_norm(tile - 1)
                dve.wait_ge(zero_done, v + 1)
                dve.wait_ge(strength_now, tile + 1)
                for m in range(1, N - 1):
                    if m == 1:
                        wait_apart(dve, t_first, v * 4 + 4, passed)
                    else:
                        wait_apart(dve, t_steps, v * 8 + 4, passed)
                    for j in range(N):
                        i = others(j)[m]
                        dve.scalar_tensor_tensor(out=tt[:, j, :], in0=zero[:, i, :], scalar=s_col(s, i, j),
                                                 in1=tt[:, j, :], op0=ALU.mult, op1=ALU.add).then_inc(t_steps, 1)
                if norm_here:
                    normalise(tile - 1)
                dve.wait_ge(cos_done, v + 1)
                wait_apart(dve, sin_done, v + 1, passed)
                for m in range(N - 1):
                    if m > 0:
                        wait_apart(dve, p_steps, v * 12 + m * 4, passed)
                    for j in range(N):
                        i = others(j)[m]
                        if m == 0:
                            dve.tensor_scalar(x[h][:, j, :], cos[:, i, :], s_col(s, i, j), None, ALU.mult
                                              ).then_inc(p_steps, 1)
                        else:
                            dve.scalar_tensor_tensor(out=x[h][:, j, :], in0=cos[:, i, :], scalar=s_col(s, i, j),
                                                     in1=x[h][:, j, :], op0=ALU.mult, op1=ALU.add).then_inc(p_steps, 1)

            def close(tile, s, h):
                v = tile * 2 + h
                dve.wait_ge(p_steps, v * 12 + 12)
                dve.tensor_tensor(x[h][:, :, :], cos[:, :, :], x[h][:, :, :], ALU.mult).then_inc(cp_done, 1)

            def fold(tile, s, h):
                v = tile * 2 + h
                dve.wait_ge(cp_done, v + 1)
                dve.wait_ge(t_steps, v * 8 + 8)
                dve.tensor_tensor(x[h][:, :, :], x[h][:, :, :], tt[:, :, :], ALU.add).then_inc(pt_done, 1)
                dve.wait_ge(pt_done, v + 1)
                dve.wait_ge(q_steps, v * 3 + 3)
                dve.tensor_tensor(x[h][:, :, :], x[h][:, :, :], q[:, :, :], ALU.add).then_inc(f_done, 1)
                dve.wait_ge(f_done, v + 1)
                dve.tensor_tensor(tt[:, :, :], half_rows(s, 0, h), x[h][:, :, :], ALU.mult).then_inc(fr_done, 1)
                if h == 0:
                    dve.wait_ge(sup_stored, tile * 16)
                dve.wait_ge(fr_done, v + 1)
                dve.tensor_reduce(sup[:, 0, h * H:(h + 1) * H], tt[:, :, :].rearrange("p n f -> p f n"),
                                  AX.X, ALU.add).then_inc(red_done, 1)
                dve.wait_ge(fi_done, v + 1)
                dve.tensor_reduce(sup[:, 1, h * H:(h + 1) * H], q[:, :, :].rearrange("p n f -> p f n"),
                                  AX.X, ALU.add).then_inc(red_done, 1)

            run(dve, invert, gather, fold, unit, close=close)
            squared_norm(TILES - 1)
            normalise(TILES - 1)


def measure_stage(nc, ctx, dram, consts):
    def sb(name, shape, dt=F32):
        return ctx.enter_context(nc.sbuf_tensor(name, shape, dt))

    def sem(name):
        return ctx.enter_context(nc.semaphore(name))

    ident = consts["ident"]
    D2 = 256
    w_raw = sb("m_raw", [P, 2, DK * D])
    meas_hi, meas_lo = sb("meas_hi", [P, 2, DK, D], F32R), sb("meas_lo", [P, 2, DK, D], F32R)
    post_hi, post_lo = sb("post_hi", [P, DK, D], F32R), sb("post_lo", [P, DK, D], F32R)
    top1_hi, top1_lo = sb("top1_hi", [P, DK, D], F32R), sb("top1_lo", [P, DK, D], F32R)
    top2_hi, top2_lo = sb("top2_hi", [P, DK, D2], F32R), sb("top2_lo", [P, DK, D2], F32R)
    post_b = sb("post_b_sb", [P, D])
    post_cols = sb("post_cols_sb", [P, 2, DK])
    top2_cols = sb("top2_cols_sb", [P, 2])
    top3_cols = sb("top3_cols_sb", [P, 2])
    sup_row = sb("sup_row", [P, TPH, 2, D])
    row = sb("row", [P, TPH, D])
    topx = sb("topx", [P, TPH, D])
    sup_hi, sup_lo = sb("sup_hi", [P, 2, DK, HALF], F32R), sb("sup_lo", [P, 2, DK, HALF], F32R)
    amp_hi, amp_lo = sb("amp_hi", [P, DK, HALF], F32R), sb("amp_lo", [P, DK, HALF], F32R)
    z_hi, z_lo = sb("z_hi", [P, DK, HALF], F32R), sb("z_lo", [P, DK, HALF], F32R)
    h_hi, h_lo = sb("h1_hi", [P, DK, HALF], F32R), sb("h1_lo", [P, DK, HALF], F32R)
    mr = sb("mr", [P, 2, HALF])
    mi = sb("mi", [P, 2, HALF])
    h2 = sb("h2", [P, 2, HALF])
    y_row = sb("y_row", [1, NHALF, HALF])
    stats = sb("post_stats", [P, TPH, 6])
    mv = sb("post_mv", [P, TPH, 2])
    var_eps, rstd = sb("post_var", [P, TPH]), sb("post_rstd", [P, TPH])
    neg_half = sb("neg_half3", [P, TPH])
    turn = [ctx.enter_context(nc.psum_tensor(f"m_turn{s}", [P, 512], F32)) for s in range(2)]
    acc_a, acc_b, acc_c = [[ctx.enter_context(nc.psum_tensor(f"m_acc_{x}{s}", [P, 512], F32)) for s in range(2)]
                           for x in "abc"]

    weights = [(dram["meas_w"][0], meas_hi[:, 0], meas_lo[:, 0]), (dram["meas_w"][1], meas_hi[:, 1], meas_lo[:, 1]),
               (dram["post_w"], post_hi[:, :, :], post_lo[:, :, :]),
               (dram["top1_w"], top1_hi[:, :, :], top1_lo[:, :, :]),
               (dram["top2_w"], top2_hi[:, :, :], top2_lo[:, :, :])]
    NW = len(weights)

    def raw(i):
        n = weights[i][1].shape[-1]
        return w_raw[:, i % 2, 0:DK * n].rearrange("p (k f) -> p k f", f=n)

    w_in = [sem("m_in0"), sem("m_in1")]
    w_hi_done, w_lo_done = sem("m_w_hi"), sem("m_w_lo")
    cols_in, sup_in, topx_in = sem("cols_in"), sem("sup_in"), sem("topx_in")
    turned = sem("m_turned")
    hi_done = sem("m_hi_done")
    lo_done = sem("m_lo_done")
    a_done, b_done, c_done = sem("ma_done"), sem("mb_done"), sem("mc_done")
    b_out, mi_done, mr_done = sem("mb_out"), sem("mi_done"), sem("mr_done")
    mr_squared, mag_summed, amp_done = sem("mr_squared"), sem("mag_summed"), sem("amp_done")
    amp_hi_done, amp_lo_done = sem("amp_hi_done"), sem("amp_lo_done")
    row_done, row_out = sem("row_done"), sem("row_out")
    stat_done, aggr_done, eps_done, rstd_done, half_set, normed = [
        sem(f"m_{x}") for x in ("stat", "aggr", "eps", "rstd", "half", "normed")]
    gelu_done = sem("m_gelu")
    h2_acc, h2_done, y_acc, y_out, y_stored = sem("h2_acc"), sem("h2_done"), sem("y_acc"), sem("y_out"), sem("y_stored")
    TURN = {("sup", 0): 0, ("sup", 1): 8, ("z", 0): 16, ("h", 0): 20, ("z", 1): 24, ("h", 1): 28}
    ROW = {("post", 0): 0, ("top", 0): 4, ("post", 1): 8, ("top", 1): 12}

    def rows(half, t):
        return row[:, t, :] if half == 0 else sup_row[:, t, 0, :]

    with nc.Block() as block:

        @block.sync
        def _(sp):
            def load_sup(half):
                for t in range(TPH):
                    sp.dma_start(sup_row[:, t], dram["sup_d"][half * TPH + t]).then_inc(sup_in, 16)

            def load_topx(half):
                sp.dma_start(topx[:, :, :], dram["top_x"][half]).then_inc(topx_in, 16)

            def load_w(i):
                if i >= 2:
                    sp.wait_ge(w_lo_done, i - 1)
                sp.dma_start(raw(i), weights[i][0]).then_inc(w_in[i % 2], 16)

            load_w(0)
            load_sup(0)
            load_w(1)
            for i in range(2, NW):
                load_w(i)
                if i == 2:
                    sp.dma_start(post_b[:, :], dram["post_row"].to_broadcast([P, D])).then_inc(cols_in, 16)
                    sp.dma_start(post_cols[:, :, :], dram["post_cols"]).then_inc(cols_in, 16)
                    sp.dma_start(top2_cols[:, :], dram["top2_cols"]).then_inc(cols_in, 16)
                    sp.dma_start(top3_cols[:, :], dram["top3_cols"]).then_inc(cols_in, 16)
            load_topx(0)
            sp.wait_ge(turned, TURN["sup", 1])
            load_sup(1)
            sp.wait_ge(row_out, ROW["top", 0] + TPH)
            load_topx(1)
            for half in range(NHALF):
                sp.wait_ge(y_out, half + 1)
                sp.dma_start(dram["y"][half * HALF:(half + 1) * HALF, :].rearrange("f o -> o f"),
                             y_row[:, half, :]).then_inc(y_stored, 16)
            sp.wait_ge(y_stored, 16 * NHALF)

        @block.scalar
        def _(act):
            def turn_high(i, g, dst, fn):
                act.wait_ge(turned, g + i + 1)
                act.activation(dst, turn[i % 2][:, :], fn).then_inc(hi_done, 1)

            def split_weights(i):
                act.wait_ge(w_in[i % 2], 16 * (i // 2) + 16)
                act.activation(weights[i][1], raw(i), ACT.Copy).then_inc(w_hi_done, 1)

            def sup_high(half):
                act.wait_ge(c_done, half * DK)
                for i in range(2 * DK):
                    turn_high(i, TURN["sup", half], sup_hi[:, i // DK, i % DK, :], ACT.Copy)

            def amplitude(half):
                for j in range(DK):
                    s = j % 2
                    u = half * DK + j
                    act.wait_ge(b_done, u + 1)
                    if u >= 2:
                        act.wait_ge(amp_lo_done, u - 1)
                    act.activation(mr[:, s, :], acc_b[s][:, :], ACT.Copy).then_inc(b_out, 1)
                    act.wait_ge(c_done, u + 1)
                    act.activation(mi[:, s, :], acc_c[s][:, :], ACT.Square).then_inc(mi_done, 1)
                    act.wait_ge(mr_done, u + 1)
                    act.activation(mr[:, s, :], mr[:, s, :], ACT.Square).then_inc(mr_squared, 1)
                    act.wait_ge(mag_summed, u + 1)
                    act.activation(mr[:, s, :], mr[:, s, :], ACT.Sqrt).then_inc(amp_done, 1)
                    act.wait_ge(amp_done, u + 1)
                    if half > 0:
                        act.wait_ge(row_done, ROW["post", 0] + TPH)
                    act.activation(amp_hi[:, j, :], mr[:, s, :], ACT.Copy).then_inc(amp_hi_done, 1)

            def gelu(half):
                if half > 0:
                    act.wait_ge(row_done, ROW["top", 0] + TPH)
                for j in range(DK):
                    act.wait_ge(turned, TURN["z", half] + j + 1)
                    act.activation(turn[j % 2][:, :], turn[j % 2][:, :], ACT.Gelu, scale=post_cols[:, 0, j:j + 1],
                                   bias=post_cols[:, 1, j:j + 1]).then_inc(gelu_done, 1)
                    act.wait_ge(gelu_done, half * DK + j + 1)
                    act.activation(z_hi[:, j, :], turn[j % 2][:, :], ACT.Copy).then_inc(hi_done, 1)

            def top_high(half):
                act.wait_ge(h2_acc, half * 2)
                for j in range(DK):
                    turn_high(j, TURN["h", half], h_hi[:, j, :], ACT.Relu)

            def last_layers(half):
                act.wait_ge(y_acc, half)
                for j in range(2):
                    act.wait_ge(h2_acc, half * 2 + (j + 1))
                    act.activation(h2[:, j, :], acc_b[j][:, :], ACT.Relu, bias=top2_cols[:, j:j + 1]
                                   ).then_inc(h2_done, 1)
                act.wait_ge(y_acc, half + 1)
                act.activation(y_row[:, half, :], acc_c[0][0:1, :], ACT.Copy).then_inc(y_out, 1)

            split_weights(0)
            sup_high(0)
            split_weights(1)
            for i in range(2, NW):
                split_weights(i)
            act.wait_ge(cols_in, 64)
            amplitude(0)
            sup_high(1)
            amplitude(1)
            for half in range(NHALF):
                gelu(half)
                top_high(half)
                last_layers(half)

        @block.gpsimd
        def _(pool):
            pool.memset(neg_half[:, :], -0.5).then_inc(half_set, 1)
            pool.wait_ge(half_set, 1)
            for half in range(NHALF):
                pool.wait_ge(eps_done, half + 1)
                pool.tensor_tensor(rstd[:, :], var_eps[:, :], neg_half[:, :], ALU.pow).then_inc(rstd_done, 1)

        @block.tensor
        def _(pe):
            def turn_tile(i, g, src):
                pe.wait_ge(lo_done, g + i + 1)
                for t in range(TPH):
                    mm = pe.transpose(turn[i % 2][:, t * P:(t + 1) * P], src(t), ident)
                mm.then_inc(turned, 1)

            def product(bank, terms, done):
                for i, (s_hi, s_lo, m_hi, m_lo) in enumerate(terms):
                    pe.matmul(bank, s_hi, m_hi, start=(i == 0), stop=False)
                    pe.matmul(bank, s_hi, m_lo, start=False, stop=False)
                    mm = pe.matmul(bank, s_lo, m_hi, start=False, stop=(i == len(terms) - 1))
                mm.then_inc(done, 1)

            def turn_sup(half):
                pe.wait_ge(sup_in, (half + 1) * 16 * TPH)
                for i in range(2 * DK):
                    turn_tile(i, TURN["sup", half], lambda t: sup_row[:, t, i // DK, i % DK * P:(i % DK + 1) * P])

            def measure(half):
                pe.wait_ge(lo_done, TURN["sup", half] + 2 * DK + 2)

                def meas(w, r, j):
                    return [(meas_hi[:, w, k, j * P:(j + 1) * P], meas_lo[:, w, k, j * P:(j + 1) * P],
                             sup_hi[:, r, k, :], sup_lo[:, r, k, :]) for k in range(DK)]

                for j in range(DK):
                    s = j % 2
                    u = half * DK + j
                    if u == 0:
                        pe.wait_ge(w_lo_done, 1)
                        product(acc_a[s][:, :], meas(0, 0, j), a_done)
                        pe.wait_ge(w_lo_done, 2)
                    if u >= 2:
                        pe.wait_ge(b_out, u - 1)
                    product(acc_b[s][:, :], meas(1, 1, j), b_done)
                    if half > 0 and j < 2:
                        pe.wait_ge(row_out, ROW["post", 0] + TPH)
                    elif u >= 2:
                        pe.wait_ge(mr_done, u - 1)
                    if u > 0:
                        product(acc_a[s][:, :], meas(0, 0, j), a_done)
                    if u >= 2:
                        pe.wait_ge(mi_done, u - 1)
                    product(acc_c[s][:, :], meas(1, 0, j) + meas(0, 1, j), c_done)

            def layer(kind, half, x_hi, x_lo, m_hi, m_lo):
                r = ROW[kind, half]
                for t in range(TPH):
                    if t < 2 and (kind, half) == ("post", 0):
                        pe.wait_ge(mr_done, DK)
                    elif t < 2 and (kind, half) == ("top", 0):
                        pe.wait_ge(mr_done, 2 * DK)
                    else:
                        pe.wait_ge(row_out, r + t - 1)
                    product(acc_a[t % 2][:, :], [(x_hi[:, k, t * P:(t + 1) * P], x_lo[:, k, t * P:(t + 1) * P],
                                                  m_hi[:, k, :], m_lo[:, k, :]) for k in range(DK)], row_done)

            def post(half):
                pe.wait_ge(w_lo_done, 3)
                pe.wait_ge(amp_lo_done, (half + 1) * DK)
                layer("post", half, amp_hi, amp_lo, post_hi, post_lo)

            def turn_post(half):
                pe.wait_ge(normed, (half + 1) * TPH)
                for k in range(DK):
                    turn_tile(k, TURN["z", half], lambda t: rows(half, t)[:, k * P:(k + 1) * P])

            def top(half):
                pe.wait_ge(w_lo_done, NW)
                pe.wait_ge(lo_done, TURN["z", half] + DK + 2)
                layer("top", half, z_hi, z_lo, top1_hi, top1_lo)

            def turn_top(half):
                pe.wait_ge(row_out, ROW["top", half] + TPH)
                for k in range(DK):
                    turn_tile(k, TURN["h", half], lambda t: rows(half, t)[:, k * P:(k + 1) * P])

            def last_layers(half):
                pe.wait_ge(lo_done, TURN["h", half] + DK + 2)
                if half == 0:
                    pe.wait_ge(b_out, 2 * DK)
                else:
                    pe.wait_ge(h2_done, half * 2)
                for j in range(2):
                    product(acc_b[j][:, :], [(top2_hi[:, k, j * P:(j + 1) * P], top2_lo[:, k, j * P:(j + 1) * P],
                                              h_hi[:, k, :], h_lo[:, k, :]) for k in range(DK)], h2_acc)
                if half == 0:
                    pe.wait_ge(mi_done, 2 * DK)
                else:
                    pe.wait_ge(y_out, half)
                pe.wait_ge(h2_done, half * 2 + 2)
                for j in range(2):
                    mm = pe.matmul(acc_c[0][0:1, :], top3_cols[:, j:j + 1], h2[:, j, :], start=(j == 0), stop=(j == 1))
                mm.then_inc(y_acc, 1)

            turn_sup(0)
            measure(0)
            turn_sup(1)
            post(0)
            measure(1)
            turn_post(0)
            top(0)
            post(1)
            pe.wait_ge(cols_in, 64)
            turn_top(0)
            last_layers(0)
            turn_post(1)
            top(1)
            turn_top(1)
            last_layers(1)

        @block.vector
        def _(dve):
            def split_weights(i):
                dve.wait_ge(w_hi_done, i + 1)
                dve.tensor_tensor(weights[i][2], raw(i), weights[i][1], ALU.subtract).then_inc(w_lo_done, 1)

            def turn_low(i, g, hi, lo):
                dve.wait_ge(hi_done, g + i + 1)
                dve.tensor_tensor(lo, turn[i % 2][:, :], hi, ALU.subtract).then_inc(lo_done, 1)

            def sup_low(half):
                for i in range(2 * DK):
                    turn_low(i, TURN["sup", half], sup_hi[:, i // DK, i % DK, :], sup_lo[:, i // DK, i % DK, :])

            def amplitude(half):
                for j in range(DK):
                    s = j % 2
                    u = half * DK + j
                    dve.wait_ge(b_out, u + 1)
                    dve.wait_ge(a_done, u + 1)
                    dve.tensor_tensor(mr[:, s, :], acc_a[s][:, :], mr[:, s, :], ALU.subtract).then_inc(mr_done, 1)
                    dve.wait_ge(mi_done, u + 1)
                    dve.wait_ge(mr_squared, u + 1)
                    dve.tensor_tensor(mr[:, s, :], mr[:, s, :], mi[:, s, :], ALU.add).then_inc(mag_summed, 1)
                    dve.wait_ge(amp_hi_done, u + 1)
                    dve.tensor_tensor(amp_lo[:, j, :], mr[:, s, :], amp_hi[:, j, :], ALU.subtract
                                      ).then_inc(amp_lo_done, 1)

            def post(half):
                dve.wait_ge(turned, TURN["sup", half] + 2 * DK)
                r = ROW["post", half]
                for t in range(TPH):
                    dve.wait_ge(row_done, r + t + 1)
                    dve.tensor_tensor(rows(half, t), acc_a[t % 2][:, :], post_b[:, :], ALU.add).then_inc(row_out, 1)
                    dve.wait_ge(row_out, r + t + 1)
                    dve.bn_stats(stats[:, t, :], rows(half, t)).then_inc(stat_done, 1)
                dve.wait_ge(stat_done, (half + 1) * TPH)
                dve.wait_ge(normed, half * TPH)
                for t in range(TPH):
                    dve.bn_aggr(mv[:, t, :], stats[:, t, :]).then_inc(aggr_done, 1)
                dve.wait_ge(aggr_done, (half + 1) * TPH)
                dve.tensor_scalar(var_eps[:, :], mv[:, :, 1], EPS, None, ALU.add).then_inc(eps_done, 1)
                dve.wait_ge(rstd_done, half + 1)
                for t in range(TPH):
                    dve.tensor_scalar(rows(half, t), rows(half, t), mv[:, t, 0:1], rstd[:, t:t + 1],
                                      ALU.subtract, ALU.mult).then_inc(normed, 1)

            def gelu_low(half):
                for j in range(DK):
                    turn_low(j, TURN["z", half], z_hi[:, j, :], z_lo[:, j, :])

            def top(half):
                dve.wait_ge(topx_in, (half + 1) * 16)
                dve.wait_ge(turned, TURN["z", half] + DK)
                r = ROW["top", half]
                for t in range(TPH):
                    dve.wait_ge(row_done, r + t + 1)
                    dve.tensor_tensor(rows(half, t), acc_a[t % 2][:, :], topx[:, t, :], ALU.add).then_inc(row_out, 1)

            def top_low(half):
                for j in range(DK):
                    dve.wait_ge(hi_done, TURN["h", half] + j + 1)
                    dve.scalar_tensor_tensor(out=h_lo[:, j, :], in0=turn[j % 2][:, :], scalar=0.0, in1=h_hi[:, j, :],
                                             op0=ALU.max, op1=ALU.subtract).then_inc(lo_done, 1)

            dve.sem_inc(lo_done, 2)
            split_weights(0)
            sup_low(0)
            split_weights(1)
            for i in range(2, NW):
                split_weights(i)
            dve.wait_ge(cols_in, 64)
            amplitude(0)
            sup_low(1)
            post(0)
            amplitude(1)
            gelu_low(0)
            top(0)
            post(1)
            top_low(0)
            gelu_low(1)
            top(1)
            top_low(1)


def quantum_tower(nc, dram):
    with ExitStack() as ctx:
        ident = ctx.enter_context(nc.sbuf_tensor("ident", [P, P], F32))
        ones_set = ctx.enter_context(nc.semaphore("ones_set"))
        ident_set = ctx.enter_context(nc.semaphore("ident_set"))
        with nc.Block() as block:

            @block.gpsimd
            def _(pool):
                pool.memset(ident[:, :], 1.0).then_inc(ones_set, 1)
                pool.wait_ge(ones_set, 1)
                pool.affine_select(out=ident[:, :], in_=ident[:, :], pattern=[[-1, P]], compare_op=ALU.is_equal,
                                   fill=0.0, base=0, channel_multiplier=1).then_inc(ident_set, 1)
                pool.wait_ge(ident_set, 1)

        consts = {"ident": ident[:, :], "passed": ctx.enter_context(nc.semaphore("passed"))}
        with ExitStack() as stage:
            encoder_stage(nc, stage, dram, consts)
        with ExitStack() as stage:
            attention_stage(nc, stage, dram, consts)
        with ExitStack() as stage:
            project_stage(nc, stage, dram, consts)
        with ExitStack() as stage:
            interact_stage(nc, stage, dram, consts)
        with ExitStack() as stage:
            measure_stage(nc, stage, dram, consts)


def layout(a):
    def k_major(w):
        return np.asarray(w).T

    def units(w):
        k, n = w.shape
        return w.reshape(k // (UNIT_K * P), UNIT_K, P, n // 512, 512).transpose(3, 0, 2, 1, 4)

    def cols(v):
        return np.asarray(v).reshape(-1, P).T

    pre = "L0_rec_"
    out = {}
    out["x_t"] = np.asarray(a["r_x"]).reshape(NHALF, HALF, KT, P).transpose(0, 3, 2, 1)
    w_top1 = np.asarray(a["W_top1"])
    out["enc_w"] = np.concatenate([
        units(w_top1[D:]), units(k_major(a[pre + "er_W1"])), units(k_major(a[pre + "ei_W1"])),
        units(k_major(a[pre + "er_W2"])), units(k_major(a[pre + "ei_W2"]))])
    out["enc_b1"] = np.concatenate([np.asarray(a[k]).reshape(-1, 512) for k in
                                    ("b_top1", pre + "er_b1", pre + "ei_b1")])
    out["ln_cols"] = np.stack([np.stack([cols(a[pre + e + "_g1"]), cols(a[pre + e + "_be1"])], 1)
                               for e in ("er", "ei")], 1)
    out["b2_cols"] = np.concatenate([cols(a[pre + "er_b2"]), cols(a[pre + "ei_b2"])], 1)
    def qkv(t):
        w = [k_major(a[pre + f"W{x}_{t}"]).reshape(DK, P, HP, P) for x in "qkv"]
        return np.stack(w, 3).reshape(DK, P, HP * 3 * P)

    out["qkv_w"] = np.stack([qkv("r"), qkv("i")])
    out["qk_bias"] = np.stack([np.stack([np.asarray(a[pre + f"b{x}_{t}"]).reshape(HP, P) for x in "qk"], 1)
                               .reshape(HP, 2 * P) for t in "ri"])
    out["v_cols"] = np.stack([cols(a[pre + "bv_r"]), cols(a[pre + "bv_i"])], 1)

    def k_tiles(w):
        return w.reshape(-1, P, w.shape[-1]).transpose(1, 0, 2)

    out["wo_w"] = np.stack([k_tiles(k_major(a[pre + f"Wo_{t}"])) for t in "ri"])
    out["bo_cols"] = np.stack([cols(a[pre + "bo_r"]), cols(a[pre + "bo_i"])], 1)
    out["int_w"] = np.stack([k_tiles(k_major(np.asarray(a[pre + f"int_W{t}"])[n])) for n in range(N) for t in "ri"])
    out["ids"] = np.asarray(a["ids"]).reshape(TILES, P, N).transpose(1, 0, 2)
    for f in range(N):
        out[f"tbl_{f}"] = np.asarray(a[f"tbl_{f}"])
    out["meas_w"] = np.stack([k_tiles(k_major(a[pre + f"meas_M{t}"])) for t in "ri"])
    out["post_w"] = k_tiles(k_major(a[pre + "post_W"]))
    out["post_row"] = np.asarray(a[pre + "post_b"]).reshape(1, D)
    out["post_cols"] = np.stack([cols(a[pre + "post_g"]), cols(a[pre + "post_be"])], 1)
    out["top1_w"] = k_tiles(w_top1[:D])
    out["top2_w"] = k_tiles(np.asarray(a["W_top2"]))
    out["top2_cols"] = cols(a["b_top2"])
    out["top3_cols"] = cols(np.asarray(a["W_top3"])[:, 0])
    return {k: np.ascontiguousarray(v) for k, v in out.items()}


def scratch_shapes():
    return {"s_t": (2, TILES, P, N * DK, P),
            "top_x": (NHALF, P, TPH, D),
            "o_t": (2, TILES * HP, P, N * P),
            "a_t": (TILES + 1, N, P, 2, 2, DK * P),
            "sup_d": (TILES, P, 2, D)}


def kernel(**inputs):
    import concourse.bacc as bacc
    from concourse.bass_utils import run_bass_kernel_spmd

    nc = bacc.Bacc("TRN2", target_bir_lowering=False, num_devices=1, dynamic_dma_scratch_size=2048)
    arrays = layout(inputs)
    dram = {}
    for name, a in arrays.items():
        dram[name] = nc.dram_tensor(name, a.shape, mybir.dt.from_np(a.dtype), kind="ExternalInput").ap()
    for name, shape in scratch_shapes().items():
        dram[name] = nc.dram_tensor(name, shape, F32, kind="Internal").ap()
    dram["y"] = nc.dram_tensor("y", (B, 1), F32, kind="ExternalOutput").ap()
    quantum_tower(nc, dram)
    return run_bass_kernel_spmd(nc, [arrays], core_ids=[0]).results[0]["y"]
```
